# Optimizing a Trainium2 kernel written in Bass

```python
import numpy as np
import jax
import jax.numpy as jnp

def _softmax(x, axis=-1):
    return jax.nn.softmax(x, axis=axis)

def _gelu(x):
    return jax.nn.gelu(x, approximate=True)

def _silu(x):
    return jax.nn.silu(x)

def _sigmoid(x):
    return jax.nn.sigmoid(x)

def _layernorm(x, axis=-1, eps=1e-05):
    m = jnp.mean(x, axis=axis, keepdims=True)
    v = jnp.var(x, axis=axis, keepdims=True)
    return (x - m) / jnp.sqrt(v + eps)

def _scatter_add(tgt, idx, src, axis=0):
    return tgt.at[idx].add(src)

def _segment_sum(src, seg, n):
    return jax.ops.segment_sum(src, seg, n)
kernel_name = 'mk_conv_attn_hybrid_d4_conv_nchw256_r4_8990c9'

def setup_inputs(seed: int=0):
    np.random.seed(seed)
    _w = jnp.asarray

    def _rec_inputs():
        import jax
        import jax.numpy as jnp
        _gk = jax.random.key(seed)
        x = -0.000125 + 0.9999 * jax.random.normal(jax.random.fold_in(_gk, 1), (32, 64, 16, 16), jnp.float32)
        return x
    x = _rec_inputs()

    def _L0_conv_setup():
        import jax, jax.numpy as jnp
        from jax import lax
        import numpy as np
        WR = 7
        NH = 4
        FF = 3.0

        def _conv_bn(x, w, s, b, groups=1):
            y = lax.conv_general_dilated(x, w, (1, 1), 'SAME', dimension_numbers=('NCHW', 'OIHW', 'NCHW'), feature_group_count=groups)
            return y * s[None, :, None, None] + b[None, :, None, None]

        def _ffn(x, w1, s1, b1, w2, s2, b2):
            return _conv_bn(jax.nn.relu(_conv_bn(x, w1, s1, b1)), w2, s2, b2)

        def _focus(t):
            n0 = jnp.linalg.norm(t, axis=-1, keepdims=True)
            tp = t ** FF
            return tp / jnp.linalg.norm(tp, axis=-1, keepdims=True) * n0

        def _attn(xw, wq, wkv, pos, scale_p, dwc_w, dwc_b, proj_w, proj_b):
            Bw, N, C = xw.shape
            hd = C // NH
            q = xw @ wq.T
            kv = xw @ wkv.T
            k, v = (kv[..., :C], kv[..., C:])
            k = k + pos
            sc = jax.nn.softplus(scale_p)
            q = (jax.nn.relu(q) + 1e-06) / sc
            k = (jax.nn.relu(k) + 1e-06) / sc
            q, k = (_focus(q), _focus(k))
            heads = lambda t: t.reshape(Bw, N, NH, hd).transpose(0, 2, 1, 3).reshape(Bw * NH, N, hd)
            q, k, v = (heads(q), heads(k), heads(v))
            z = 1.0 / (jnp.einsum('bic,bc->bi', q, k.sum(axis=1)) + 1e-06)
            if N * N * (hd + hd) > hd * hd * (N + N):
                kv2 = jnp.einsum('bjc,bjd->bcd', k, v)
                y = jnp.einsum('bic,bcd,bi->bid', q, kv2, z)
            else:
                qk = jnp.einsum('bic,bjc->bij', q, k)
                y = jnp.einsum('bij,bjd,bi->bid', qk, v, z)
            num = int(round(N ** 0.5))
            fm = v.reshape(-1, num, num, hd).transpose(0, 3, 1, 2)
            fm = lax.conv_general_dilated(fm, dwc_w, (1, 1), 'SAME', dimension_numbers=('NCHW', 'OIHW', 'NCHW'), feature_group_count=hd)
            fm = fm + dwc_b[None, :, None, None]
            y = y + fm.transpose(0, 2, 3, 1).reshape(-1, N, hd)
            y = y.reshape(Bw, NH, N, hd).transpose(0, 2, 1, 3).reshape(Bw, N, C)
            return y @ proj_w.T + proj_b

        def _windowed_attn(x, wq, wkv, pos, scale_p, dwc_w, dwc_b, proj_w, proj_b):
            B, C, H, W = x.shape
            xh = x.transpose(0, 2, 3, 1)
            pb, pr = (-H % WR, -W % WR)
            xh = jnp.pad(xh, ((0, 0), (0, pb), (0, pr), (0, 0)))
            pH, pW = (H + pb, W + pr)
            nH, nW = (pH // WR, pW // WR)
            xw = xh.reshape(B, nH, WR, nW, WR, C).transpose(0, 1, 3, 2, 4, 5)
            xw = xw.reshape(B * nH * nW, WR * WR, C)
            xw = _attn(xw, wq, wkv, pos, scale_p, dwc_w, dwc_b, proj_w, proj_b)
            xh = xw.reshape(B, nH, nW, WR, WR, C).transpose(0, 1, 3, 2, 4, 5).reshape(B, pH, pW, C)
            return xh[:, :H, :W].transpose(0, 3, 1, 2)

        def _forward(x, dw0_w, dw0_s, dw0_b, f0_w1, f0_s1, f0_b1, f0_w2, f0_s2, f0_b2, wq, wkv, pos, scale_p, dwc_w, dwc_b, proj_w, proj_b, dw1_w, dw1_s, dw1_b, f1_w1, f1_s1, f1_b1, f1_w2, f1_s2, f1_b2):
            C = x.shape[1]
            x = x + _conv_bn(x, dw0_w, dw0_s, dw0_b, groups=C)
            x = x + _ffn(x, f0_w1, f0_s1, f0_b1, f0_w2, f0_s2, f0_b2)
            x = x + _windowed_attn(x, wq, wkv, pos, scale_p, dwc_w, dwc_b, proj_w, proj_b)
            x = x + _conv_bn(x, dw1_w, dw1_s, dw1_b, groups=C)
            x = x + _ffn(x, f1_w1, f1_s1, f1_b1, f1_w2, f1_s2, f1_b2)
            return x
        key = jax.random.key(seed)
        ks = iter(jax.random.split(key, 32))
        rn = lambda shape, s=0.02: jax.random.normal(next(ks), shape, jnp.float32) * s
        C, H, B = (64, 16, 32)
        hid, hd = (2 * C, C // NH)
        d = {'x': jax.random.normal(next(ks), (B, C, H, H), jnp.float32)}
        d.update(dw0_w=rn((C, 1, 3, 3)), dw0_s=jnp.ones(C), dw0_b=jnp.zeros(C))
        d.update(f0_w1=rn((hid, C, 1, 1)), f0_s1=jnp.ones(hid), f0_b1=jnp.zeros(hid), f0_w2=rn((C, hid, 1, 1)), f0_s2=jnp.ones(C), f0_b2=jnp.zeros(C))
        d.update(wq=rn((C, C)), wkv=rn((2 * C, C)), pos=rn((1, WR * WR, C)), scale_p=rn((1, 1, C)), dwc_w=rn((hd, 1, 5, 5)), dwc_b=jnp.zeros(hd), proj_w=rn((C, C)), proj_b=jnp.zeros(C))
        d.update(dw1_w=rn((C, 1, 3, 3)), dw1_s=jnp.ones(C), dw1_b=jnp.zeros(C))
        d.update(f1_w1=rn((hid, C, 1, 1)), f1_s1=jnp.ones(hid), f1_b1=jnp.zeros(hid), f1_w2=rn((C, hid, 1, 1)), f1_s2=jnp.ones(C), f1_b2=jnp.zeros(C))
        return d
    _L0_conv_all = _L0_conv_setup()
    _L0_conv_in = {k: v for k, v in _L0_conv_all.items() if k in ('dw0_w', 'dw0_s', 'dw0_b', 'f0_w1', 'f0_s1', 'f0_b1', 'f0_w2', 'f0_s2', 'f0_b2', 'wq', 'wkv', 'pos', 'scale_p', 'dwc_w', 'dwc_b', 'proj_w', 'proj_b', 'dw1_w', 'dw1_s', 'dw1_b', 'f1_w1', 'f1_s1', 'f1_b1', 'f1_w2', 'f1_s2', 'f1_b2')}
    del _L0_conv_all

    def _L1_conv_setup():
        import jax, jax.numpy as jnp
        import numpy as np
        EPS = 1e-05
        T = 3
        G = 4
        D = 16
        LN_EPS = 1e-05
        key = jax.random.key(seed)
        k0, k1, k2 = jax.random.split(key, 3)
        X = jax.random.normal(k0, (32, 64, 16, 16), dtype=jnp.float32)
        fc1_w = jax.random.normal(k1, (16, 64), dtype=jnp.float32) * 0.05
        ln_g = jnp.ones((16,), dtype=jnp.float32)
        ln_b = jnp.zeros((16,), dtype=jnp.float32)
        fc2_w = jax.random.normal(k2, (64, 16), dtype=jnp.float32) * 0.05
        x_weight = jnp.zeros((1,), dtype=jnp.float32)
        return {'X': X, 'fc1_w': fc1_w, 'ln_g': ln_g, 'ln_b': ln_b, 'fc2_w': fc2_w, 'x_weight': x_weight}
    _L1_conv_all = _L1_conv_setup()
    _L1_conv_in = {k: v for k, v in _L1_conv_all.items() if k in ('fc1_w', 'ln_g', 'ln_b', 'fc2_w', 'x_weight')}
    del _L1_conv_all

    def _L2_attn_setup():
        import jax, jax.numpy as jnp
        import numpy as np
        HEADS, DIM_HEAD = (8, 16)
        BASE_TEMP, EPSILON = (0.5, 1e-06)
        key = jax.random.key(seed)
        ks = jax.random.split(key, 6)
        s = lambda k, sh, fan: jax.random.normal(k, sh, jnp.float32) * fan ** (-0.5)
        return {'x': jax.random.normal(ks[0], (2, 25000, 64), jnp.float32), 'W_x': s(ks[1], (128, 64), 64), 'b_x': jnp.zeros((128,), jnp.float32), 'W_slice': s(ks[2], (16, 16), 16), 'b_slice': jnp.zeros((16,), jnp.float32), 'W_temp': s(ks[3], (1, 16), 16), 'b_temp': jnp.zeros((1,), jnp.float32), 'W_out': s(ks[4], (64, 128), 128), 'b_out': jnp.zeros((64,), jnp.float32)}
    _L2_attn_all = _L2_attn_setup()
    _L2_attn_in = {k: v for k, v in _L2_attn_all.items() if k in ('W_x', 'b_x', 'W_slice', 'b_slice', 'W_temp', 'b_temp', 'W_out', 'b_out')}
    del _L2_attn_all

    def _L2_ffn_setup():
        import jax, jax.numpy as jnp
        import numpy as np
        from jax import lax
        key = jax.random.key(seed)
        B, T, I, H = (16, 512, 64, 64)
        ks = jax.random.split(key, 13)
        s = 1.0 / np.sqrt(H)

        def w(k, shape):
            return jax.random.uniform(k, shape, jnp.float32, -s, s)
        return {'x': jax.random.normal(ks[0], (B, T, I), jnp.float32), 'U_i': w(ks[1], (I, H)), 'V_i': w(ks[2], (H, H)), 'b_i': w(ks[3], (H,)), 'U_f': w(ks[4], (I, H)), 'V_f': w(ks[5], (H, H)), 'b_f': w(ks[6], (H,)), 'U_c': w(ks[7], (I, H)), 'V_c': w(ks[8], (H, H)), 'b_c': w(ks[9], (H,)), 'U_o': w(ks[10], (I, H)), 'V_o': w(ks[11], (H, H)), 'b_o': w(ks[12], (H,))}
    _L2_ffn_all = _L2_ffn_setup()
    _L2_ffn_in = {k: v for k, v in _L2_ffn_all.items() if k in ('U_i', 'V_i', 'b_i', 'U_f', 'V_f', 'b_f', 'U_c', 'V_c', 'b_c', 'U_o', 'V_o', 'b_o')}
    del _L2_ffn_all

    def _L3_attn_setup():
        import jax, jax.numpy as jnp
        import numpy as np
        key = jax.random.key(seed)
        k1, k2 = jax.random.split(key)
        B, N, D = (4, 1024, 64)
        inp = jax.random.normal(k1, (B, N, D), dtype=jnp.float32)
        q_weight = jax.random.normal(k2, (D, D), dtype=jnp.float32)
        return {'input': inp, 'q_weight': q_weight}
    _L3_attn_all = _L3_attn_setup()
    _L3_attn_in = {k: v for k, v in _L3_attn_all.items() if k in ('q_weight',)}
    del _L3_attn_all

    def _L3_ffn_setup():
        import jax, jax.numpy as jnp
        import numpy as np
        D_MODEL = 64
        N_EXPERTS = 16
        HIDDEN = 128
        SCALE = 0.02
        key = jax.random.key(seed)
        ks = jax.random.split(key, 5)
        x = jax.random.normal(ks[0], (4, 2048, D_MODEL), dtype=jnp.float32)
        gate_w = jax.random.normal(ks[1], (D_MODEL, N_EXPERTS), dtype=jnp.float32) * SCALE
        gate_b = jnp.zeros((N_EXPERTS,), dtype=jnp.float32)
        w1 = jax.random.normal(ks[2], (N_EXPERTS, D_MODEL, HIDDEN), dtype=jnp.float32) * SCALE
        w2 = jax.random.normal(ks[3], (N_EXPERTS, D_MODEL, HIDDEN), dtype=jnp.float32) * SCALE
        w3 = jax.random.normal(ks[4], (N_EXPERTS, HIDDEN, D_MODEL), dtype=jnp.float32) * SCALE
        return {'x': x, 'gate_w': gate_w, 'gate_b': gate_b, 'w1': w1, 'w2': w2, 'w3': w3}
    _L3_ffn_all = _L3_ffn_setup()
    _L3_ffn_in = {k: v for k, v in _L3_ffn_all.items() if k in ('gate_w', 'gate_b', 'w1', 'w2', 'w3')}
    del _L3_ffn_all
    return {'x': x, 'L0_conv_dw0_w': _L0_conv_in['dw0_w'], 'L0_conv_dw0_s': _L0_conv_in['dw0_s'], 'L0_conv_dw0_b': _L0_conv_in['dw0_b'], 'L0_conv_f0_w1': _L0_conv_in['f0_w1'], 'L0_conv_f0_s1': _L0_conv_in['f0_s1'], 'L0_conv_f0_b1': _L0_conv_in['f0_b1'], 'L0_conv_f0_w2': _L0_conv_in['f0_w2'], 'L0_conv_f0_s2': _L0_conv_in['f0_s2'], 'L0_conv_f0_b2': _L0_conv_in['f0_b2'], 'L0_conv_wq': _L0_conv_in['wq'], 'L0_conv_wkv': _L0_conv_in['wkv'], 'L0_conv_pos': _L0_conv_in['pos'], 'L0_conv_scale_p': _L0_conv_in['scale_p'], 'L0_conv_dwc_w': _L0_conv_in['dwc_w'], 'L0_conv_dwc_b': _L0_conv_in['dwc_b'], 'L0_conv_proj_w': _L0_conv_in['proj_w'], 'L0_conv_proj_b': _L0_conv_in['proj_b'], 'L0_conv_dw1_w': _L0_conv_in['dw1_w'], 'L0_conv_dw1_s': _L0_conv_in['dw1_s'], 'L0_conv_dw1_b': _L0_conv_in['dw1_b'], 'L0_conv_f1_w1': _L0_conv_in['f1_w1'], 'L0_conv_f1_s1': _L0_conv_in['f1_s1'], 'L0_conv_f1_b1': _L0_conv_in['f1_b1'], 'L0_conv_f1_w2': _L0_conv_in['f1_w2'], 'L0_conv_f1_s2': _L0_conv_in['f1_s2'], 'L0_conv_f1_b2': _L0_conv_in['f1_b2'], 'L1_conv_fc1_w': _L1_conv_in['fc1_w'], 'L1_conv_ln_g': _L1_conv_in['ln_g'], 'L1_conv_ln_b': _L1_conv_in['ln_b'], 'L1_conv_fc2_w': _L1_conv_in['fc2_w'], 'L1_conv_x_weight': _L1_conv_in['x_weight'], 'L2_attn_W_x': _L2_attn_in['W_x'], 'L2_attn_b_x': _L2_attn_in['b_x'], 'L2_attn_W_slice': _L2_attn_in['W_slice'], 'L2_attn_b_slice': _L2_attn_in['b_slice'], 'L2_attn_W_temp': _L2_attn_in['W_temp'], 'L2_attn_b_temp': _L2_attn_in['b_temp'], 'L2_attn_W_out': _L2_attn_in['W_out'], 'L2_attn_b_out': _L2_attn_in['b_out'], 'L2_ffn_U_i': _L2_ffn_in['U_i'], 'L2_ffn_V_i': _L2_ffn_in['V_i'], 'L2_ffn_b_i': _L2_ffn_in['b_i'], 'L2_ffn_U_f': _L2_ffn_in['U_f'], 'L2_ffn_V_f': _L2_ffn_in['V_f'], 'L2_ffn_b_f': _L2_ffn_in['b_f'], 'L2_ffn_U_c': _L2_ffn_in['U_c'], 'L2_ffn_V_c': _L2_ffn_in['V_c'], 'L2_ffn_b_c': _L2_ffn_in['b_c'], 'L2_ffn_U_o': _L2_ffn_in['U_o'], 'L2_ffn_V_o': _L2_ffn_in['V_o'], 'L2_ffn_b_o': _L2_ffn_in['b_o'], 'L3_attn_q_weight': _L3_attn_in['q_weight'], 'L3_ffn_gate_w': _L3_ffn_in['gate_w'], 'L3_ffn_gate_b': _L3_ffn_in['gate_b'], 'L3_ffn_w1': _L3_ffn_in['w1'], 'L3_ffn_w2': _L3_ffn_in['w2'], 'L3_ffn_w3': _L3_ffn_in['w3']}

def reference(x, L0_conv_dw0_w, L0_conv_dw0_s, L0_conv_dw0_b, L0_conv_f0_w1, L0_conv_f0_s1, L0_conv_f0_b1, L0_conv_f0_w2, L0_conv_f0_s2, L0_conv_f0_b2, L0_conv_wq, L0_conv_wkv, L0_conv_pos, L0_conv_scale_p, L0_conv_dwc_w, L0_conv_dwc_b, L0_conv_proj_w, L0_conv_proj_b, L0_conv_dw1_w, L0_conv_dw1_s, L0_conv_dw1_b, L0_conv_f1_w1, L0_conv_f1_s1, L0_conv_f1_b1, L0_conv_f1_w2, L0_conv_f1_s2, L0_conv_f1_b2, L1_conv_fc1_w, L1_conv_ln_g, L1_conv_ln_b, L1_conv_fc2_w, L1_conv_x_weight, L2_attn_W_x, L2_attn_b_x, L2_attn_W_slice, L2_attn_b_slice, L2_attn_W_temp, L2_attn_b_temp, L2_attn_W_out, L2_attn_b_out, L2_ffn_U_i, L2_ffn_V_i, L2_ffn_b_i, L2_ffn_U_f, L2_ffn_V_f, L2_ffn_b_f, L2_ffn_U_c, L2_ffn_V_c, L2_ffn_b_c, L2_ffn_U_o, L2_ffn_V_o, L2_ffn_b_o, L3_attn_q_weight, L3_ffn_gate_w, L3_ffn_gate_b, L3_ffn_w1, L3_ffn_w2, L3_ffn_w3):
    import jax
    import jax.numpy as jnp

    def _L0_conv_ref(x, dw0_w, dw0_s, dw0_b, f0_w1, f0_s1, f0_b1, f0_w2, f0_s2, f0_b2, wq, wkv, pos, scale_p, dwc_w, dwc_b, proj_w, proj_b, dw1_w, dw1_s, dw1_b, f1_w1, f1_s1, f1_b1, f1_w2, f1_s2, f1_b2):
        import jax, jax.numpy as jnp
        from jax import lax
        import numpy as np
        WR = 7
        NH = 4
        FF = 3.0

        def _conv_bn(x, w, s, b, groups=1):
            y = lax.conv_general_dilated(x, w, (1, 1), 'SAME', dimension_numbers=('NCHW', 'OIHW', 'NCHW'), feature_group_count=groups)
            return y * s[None, :, None, None] + b[None, :, None, None]

        def _ffn(x, w1, s1, b1, w2, s2, b2):
            return _conv_bn(jax.nn.relu(_conv_bn(x, w1, s1, b1)), w2, s2, b2)

        def _focus(t):
            n0 = jnp.linalg.norm(t, axis=-1, keepdims=True)
            tp = t ** FF
            return tp / jnp.linalg.norm(tp, axis=-1, keepdims=True) * n0

        def _attn(xw, wq, wkv, pos, scale_p, dwc_w, dwc_b, proj_w, proj_b):
            Bw, N, C = xw.shape
            hd = C // NH
            q = xw @ wq.T
            kv = xw @ wkv.T
            k, v = (kv[..., :C], kv[..., C:])
            k = k + pos
            sc = jax.nn.softplus(scale_p)
            q = (jax.nn.relu(q) + 1e-06) / sc
            k = (jax.nn.relu(k) + 1e-06) / sc
            q, k = (_focus(q), _focus(k))
            heads = lambda t: t.reshape(Bw, N, NH, hd).transpose(0, 2, 1, 3).reshape(Bw * NH, N, hd)
            q, k, v = (heads(q), heads(k), heads(v))
            z = 1.0 / (jnp.einsum('bic,bc->bi', q, k.sum(axis=1)) + 1e-06)
            if N * N * (hd + hd) > hd * hd * (N + N):
                kv2 = jnp.einsum('bjc,bjd->bcd', k, v)
                y = jnp.einsum('bic,bcd,bi->bid', q, kv2, z)
            else:
                qk = jnp.einsum('bic,bjc->bij', q, k)
                y = jnp.einsum('bij,bjd,bi->bid', qk, v, z)
            num = int(round(N ** 0.5))
            fm = v.reshape(-1, num, num, hd).transpose(0, 3, 1, 2)
            fm = lax.conv_general_dilated(fm, dwc_w, (1, 1), 'SAME', dimension_numbers=('NCHW', 'OIHW', 'NCHW'), feature_group_count=hd)
            fm = fm + dwc_b[None, :, None, None]
            y = y + fm.transpose(0, 2, 3, 1).reshape(-1, N, hd)
            y = y.reshape(Bw, NH, N, hd).transpose(0, 2, 1, 3).reshape(Bw, N, C)
            return y @ proj_w.T + proj_b

        def _windowed_attn(x, wq, wkv, pos, scale_p, dwc_w, dwc_b, proj_w, proj_b):
            B, C, H, W = x.shape
            xh = x.transpose(0, 2, 3, 1)
            pb, pr = (-H % WR, -W % WR)
            xh = jnp.pad(xh, ((0, 0), (0, pb), (0, pr), (0, 0)))
            pH, pW = (H + pb, W + pr)
            nH, nW = (pH // WR, pW // WR)
            xw = xh.reshape(B, nH, WR, nW, WR, C).transpose(0, 1, 3, 2, 4, 5)
            xw = xw.reshape(B * nH * nW, WR * WR, C)
            xw = _attn(xw, wq, wkv, pos, scale_p, dwc_w, dwc_b, proj_w, proj_b)
            xh = xw.reshape(B, nH, nW, WR, WR, C).transpose(0, 1, 3, 2, 4, 5).reshape(B, pH, pW, C)
            return xh[:, :H, :W].transpose(0, 3, 1, 2)

        def _forward(x, dw0_w, dw0_s, dw0_b, f0_w1, f0_s1, f0_b1, f0_w2, f0_s2, f0_b2, wq, wkv, pos, scale_p, dwc_w, dwc_b, proj_w, proj_b, dw1_w, dw1_s, dw1_b, f1_w1, f1_s1, f1_b1, f1_w2, f1_s2, f1_b2):
            C = x.shape[1]
            x = x + _conv_bn(x, dw0_w, dw0_s, dw0_b, groups=C)
            x = x + _ffn(x, f0_w1, f0_s1, f0_b1, f0_w2, f0_s2, f0_b2)
            x = x + _windowed_attn(x, wq, wkv, pos, scale_p, dwc_w, dwc_b, proj_w, proj_b)
            x = x + _conv_bn(x, dw1_w, dw1_s, dw1_b, groups=C)
            x = x + _ffn(x, f1_w1, f1_s1, f1_b1, f1_w2, f1_s2, f1_b2)
            return x
        return _forward(x, dw0_w, dw0_s, dw0_b, f0_w1, f0_s1, f0_b1, f0_w2, f0_s2, f0_b2, wq, wkv, pos, scale_p, dwc_w, dwc_b, proj_w, proj_b, dw1_w, dw1_s, dw1_b, f1_w1, f1_s1, f1_b1, f1_w2, f1_s2, f1_b2)

    def _L1_conv_ref(X, fc1_w, ln_g, ln_b, fc2_w, x_weight):
        import jax, jax.numpy as jnp
        import numpy as np
        EPS = 1e-05
        T = 3
        G = 4
        D = 16
        LN_EPS = 1e-05
        N, C, H, W = X.shape
        x_var = jnp.var(X.reshape(N, C, -1), axis=-1, ddof=1)
        h = x_var @ fc1_w.T
        mu = h.mean(-1, keepdims=True)
        var = h.var(-1, keepdims=True)
        h = (h - mu) / jnp.sqrt(var + LN_EPS) * ln_g + ln_b
        h = jax.nn.relu(h)
        y = jax.nn.sigmoid(h @ fc2_w.T)
        scale = jnp.sqrt(x_var.mean())
        xin = (y / scale)[:, :, None, None] * X
        x = jnp.transpose(X, (1, 0, 2, 3)).reshape(G, D, -1)
        m = x.shape[-1]
        mean = x.mean(-1, keepdims=True)
        xc = x - mean
        I = jnp.eye(D, dtype=X.dtype)
        Sigma = 1.0 / m * I + EPS * jnp.einsum('gdm,gem->gde', xc, xc)
        rTr = 1.0 / jnp.trace(Sigma, axis1=1, axis2=2)[:, None, None]
        Sigma_N = Sigma * rTr
        P = jnp.broadcast_to(I, (G, D, D))
        for _ in range(T):
            P3 = P @ P @ P
            P = -0.5 * P + 1.5 * (P3 @ Sigma_N)
        xn = P @ x
        Xn = jnp.transpose(xn.reshape(C, N, H, W), (1, 0, 2, 3))
        w = jax.nn.sigmoid(x_weight)[0]
        return w * Xn + (1.0 - w) * xin

    def _L2_attn_ref(x, W_x, b_x, W_slice, b_slice, W_temp, b_temp, W_out, b_out):
        import jax, jax.numpy as jnp
        import numpy as np
        HEADS, DIM_HEAD = (8, 16)
        BASE_TEMP, EPSILON = (0.5, 1e-06)
        B, N, C = x.shape
        H, D = (HEADS, DIM_HEAD)
        x_proj = (x @ W_x.T + b_x).reshape(B, N, H, D).transpose(0, 2, 1, 3)
        adaptive_temp = BASE_TEMP + jnp.clip(x_proj @ W_temp.T + b_temp, -0.4, 0.4)
        log_neg_log_eps = jnp.log(-jnp.log(jnp.float32(EPSILON)))
        slice_logits = x_proj @ W_slice.T + b_slice - log_neg_log_eps
        slice_weights = jax.nn.softmax(slice_logits / adaptive_temp, axis=2)
        slice_norm = slice_weights.sum(axis=2)
        eidetic = jnp.einsum('bhnc,bhng->bhgc', x_proj, slice_weights)
        eidetic = eidetic / (slice_norm + 1e-05)[..., None]
        processed = eidetic
        out_x = jnp.einsum('bhgc,bhng->bhnc', processed, slice_weights)
        out_x = out_x.transpose(0, 2, 1, 3).reshape(B, N, H * D)
        return out_x @ W_out.T + b_out

    def _L2_ffn_ref(x, U_i, V_i, b_i, U_f, V_f, b_f, U_c, V_c, b_c, U_o, V_o, b_o):
        import jax, jax.numpy as jnp
        import numpy as np
        from jax import lax
        B, T, _ = x.shape
        H = U_i.shape[1]
        xt = jnp.swapaxes(x, 0, 1)
        xi = xt @ U_i + b_i
        xf = xt @ U_f + b_f
        xg = xt @ U_c + b_c
        xo = xt @ U_o + b_o
        h0 = jnp.zeros((B, H), x.dtype)
        c0 = jnp.zeros((B, H), x.dtype)

        def step(carry, xs):
            h, c = carry
            xi_t, xf_t, xg_t, xo_t = xs
            i_t = jax.nn.sigmoid(xi_t + h @ V_i)
            f_t = jax.nn.sigmoid(xf_t + h @ V_f)
            g_t = jnp.tanh(xg_t + h @ V_c)
            o_t = jax.nn.sigmoid(xo_t + h @ V_o)
            c_new = h * c + i_t * g_t
            h_new = o_t * jnp.tanh(c_new)
            return ((h_new, c_new), h_new)
        (_, _), hs = lax.scan(step, (h0, c0), (xi, xf, xg, xo))
        return jnp.swapaxes(hs, 0, 1)

    def _L3_attn_ref(input, q_weight):
        import jax, jax.numpy as jnp
        import numpy as np
        query = jnp.einsum('bnd,de->bne', input, q_weight)
        att = jax.nn.sigmoid(jnp.einsum('bnd,bmd->bnm', query, input))
        value = jnp.einsum('bnm,bmd->bnd', att, input)
        return value

    def _L3_ffn_ref(x, gate_w, gate_b, w1, w2, w3):
        import jax, jax.numpy as jnp
        import numpy as np
        D_MODEL = 64
        N_EXPERTS = 16
        HIDDEN = 128
        SCALE = 0.02
        n_experts = w1.shape[0]
        logits = jnp.einsum('bsd,de->bse', x, gate_w) + gate_b
        probs = jax.nn.softmax(logits, axis=-1)
        top_probs, top_idx = jax.lax.top_k(probs, 2)
        top_probs = top_probs / jnp.sum(top_probs, axis=-1, keepdims=True)
        dispatch = jnp.sum(jax.nn.one_hot(top_idx, n_experts, dtype=x.dtype) * top_probs[..., None], axis=-2)
        h1 = jnp.einsum('bsd,edh->bseh', x, w1)
        h2 = jnp.einsum('bsd,edh->bseh', x, w2)
        hidden = jax.nn.silu(h1) * h2
        expert_out = jnp.einsum('bseh,eho->bseo', hidden, w3)
        return jnp.einsum('bseo,bse->bso', expert_out, dispatch)

    def _gn(v, G=32, eps=1e-05):
        B_, C_, H_, W_ = v.shape
        g = v.reshape(B_, G, C_ // G, H_, W_)
        m = jnp.mean(g, axis=(2, 3, 4), keepdims=True)
        s = jnp.var(g, axis=(2, 3, 4), keepdims=True)
        return ((g - m) / jnp.sqrt(s + eps)).reshape(v.shape)

    def _ln_c(v, eps=1e-06):
        m = jnp.mean(v, axis=1, keepdims=True)
        s = jnp.var(v, axis=1, keepdims=True)
        return (v - m) / jnp.sqrt(s + eps)

    def _ln_t(v, eps=1e-05):
        m = jnp.mean(v, axis=-1, keepdims=True)
        s = jnp.var(v, axis=-1, keepdims=True)
        return (v - m) / jnp.sqrt(s + eps)

    def _to_tokens(v):
        B_, C_, H_, W_ = v.shape
        return v.reshape(B_, C_, H_ * W_).transpose(0, 2, 1)

    def _from_tokens(t, like):
        B_, C_, H_, W_ = like.shape
        return t.transpose(0, 2, 1).reshape(B_, C_, H_, W_)
    x = _L0_conv_ref(x, L0_conv_dw0_w, L0_conv_dw0_s, L0_conv_dw0_b, L0_conv_f0_w1, L0_conv_f0_s1, L0_conv_f0_b1, L0_conv_f0_w2, L0_conv_f0_s2, L0_conv_f0_b2, L0_conv_wq, L0_conv_wkv, L0_conv_pos, L0_conv_scale_p, L0_conv_dwc_w, L0_conv_dwc_b, L0_conv_proj_w, L0_conv_proj_b, L0_conv_dw1_w, L0_conv_dw1_s, L0_conv_dw1_b, L0_conv_f1_w1, L0_conv_f1_s1, L0_conv_f1_b1, L0_conv_f1_w2, L0_conv_f1_s2, L0_conv_f1_b2)
    x = x + _L1_conv_ref(_gn(x), L1_conv_fc1_w, L1_conv_ln_g, L1_conv_ln_b, L1_conv_fc2_w, L1_conv_x_weight)
    t = _to_tokens(x)
    t = t + _L2_attn_ref(_ln_t(t), L2_attn_W_x, L2_attn_b_x, L2_attn_W_slice, L2_attn_b_slice, L2_attn_W_temp, L2_attn_b_temp, L2_attn_W_out, L2_attn_b_out)
    t = t + _L2_ffn_ref(_ln_t(t), L2_ffn_U_i, L2_ffn_V_i, L2_ffn_b_i, L2_ffn_U_f, L2_ffn_V_f, L2_ffn_b_f, L2_ffn_U_c, L2_ffn_V_c, L2_ffn_b_c, L2_ffn_U_o, L2_ffn_V_o, L2_ffn_b_o)
    t = t + _L3_attn_ref(_ln_t(t), L3_attn_q_weight)
    t = t + _L3_ffn_ref(_ln_t(t), L3_ffn_gate_w, L3_ffn_gate_b, L3_ffn_w1, L3_ffn_w2, L3_ffn_w3)
    x = _from_tokens(t, x)
    return x

_drawn_inputs = setup_inputs


def setup_inputs(seed=0):
    import zlib

    import numpy as np

    out = dict(_drawn_inputs(seed))
    spreads = {'L0_conv_dw0_s': (1.0, 0.6),
     'L0_conv_dw0_b': (0.0, 0.1),
     'L0_conv_f0_s1': (1.0, 0.6),
     'L0_conv_f0_b1': (0.0, 0.1),
     'L0_conv_f0_s2': (1.0, 0.6),
     'L0_conv_f0_b2': (0.0, 0.1),
     'L0_conv_dwc_b': (0.0, 0.1),
     'L0_conv_proj_b': (0.0, 0.1),
     'L0_conv_dw1_s': (1.0, 0.6),
     'L0_conv_dw1_b': (0.0, 0.1),
     'L0_conv_f1_s1': (1.0, 0.6),
     'L0_conv_f1_b1': (0.0, 0.1),
     'L0_conv_f1_s2': (1.0, 0.6),
     'L0_conv_f1_b2': (0.0, 0.1),
     'L1_conv_ln_g': (1.0, 0.6),
     'L1_conv_ln_b': (0.0, 2.0),
     'L2_attn_b_x': (0.0, 0.1),
     'L2_attn_b_slice': (0.0, 0.501),
     'L2_attn_b_out': (0.0, 0.1),
     'L3_ffn_gate_b': (0.0, 0.8)}
    factors = {'L0_conv_wq': 4.923,
     'L0_conv_wkv': 2.741,
     'L0_conv_pos': 31.293,
     'L0_conv_scale_p': 36.403,
     'L0_conv_dwc_w': 8.0,
     'L1_conv_fc1_w': 2.74,
     'L2_ffn_V_i': 8.0,
     'L2_ffn_b_i': 7.77,
     'L2_ffn_V_c': 2.751,
     'L2_ffn_V_o': 8.0,
     'L2_ffn_b_o': 8.0,
     'L3_ffn_gate_w': 8.0,
     'L3_ffn_w1': 8.0,
     'L3_ffn_w2': 8.0,
     'L3_ffn_w3': 8.0}
    for name, (base, spread) in spreads.items():
        noise = np.random.default_rng([zlib.crc32(name.encode()), seed]).standard_normal(out[name].shape)
        drawn = base * np.exp(spread * noise) if base else spread * noise
        out[name] = jnp.asarray(drawn.astype(out[name].dtype))
    for name, factor in factors.items():
        out[name] = (out[name] * factor).astype(out[name].dtype)
    return out
```

```python
from contextlib import ExitStack

import numpy as np

import concourse.bass as bass
from concourse import mybir

ALU = mybir.AluOpType
ACT = mybir.ActivationFunctionType
AXX = mybir.AxisListType.X
F32 = mybir.dt.float32
F16 = mybir.dt.float16
BF16 = mybir.dt.bfloat16

P = 128
C = 64
B = 32
HB = B // 2
SIDE = 16
HW = SIDE * SIDE
COLS = HB * HW
TW = 512
TILES = COLS // TW
PADW = SIDE + 1
PADI = PADW * PADW
WR = 7
NWIN = 9
SLOT = 64
NH = 4
HD = 16
E = 16
HID = 128
SEG = [(0, 7), (7, 7), (14, 2)]
XSCALE = 2.0 ** 10

LAYOUT = {
    "conv0": dict(ident=128, dw0_w=9, dw0_s=1, dw0_b=1, f0_w1=256, f0_s1=1, f0_b1=1, f0_w2=256, f0_s2=1,
                  f0_b2=1),
    "attn": dict(wq=128, wk=128, wv=128, scale=128, pos=128, toep=16 * 128, dwc_b=1, proj=128, proj_b=1,
                 headmask=128, headind=8, slots=2),
    "rest": dict(dw1_w=9, dw1_s=1, dw1_b=1, f1_w1=256, f1_s1=1, f1_b1=1, f1_w2=256, f1_s2=1, f1_b2=1,
                 center=128, mean=128, pair=128, fold=128, group16=128, fc1=32, ln_g=32, ln_b=32, fc2=128,
                 x_weight=1, eps5=1, lstm_half=1, w_x=256, b_x=1, b_x_row=256, w_slice=128, b_slice=1, w_temp=128, b_temp=1,
                 w_out=256, b_out=1, u_i=128, u_g=128, u_o=128, v_i=128, v_g=128, v_o=128,
                 lstm_b=128, gate_sel=384, q_w=128, gate_w=32, gate_b=32, idx_w=32),
}


def widths(chunk):
    return sum(LAYOUT[chunk].values())


class StageSemaphores:

    def __init__(self, nc, prefix):
        self.nc, self.prefix, self.made = nc, prefix, []

    def __call__(self, name):
        self.made.append(self.nc.alloc_semaphore(f"{self.prefix}_{name}"))
        return self.made[-1]

    def __enter__(self):
        return self

    def __exit__(self, *_):
        self.nc.clear_and_free_semaphores(self.made)
        self.nc.all_engine_barrier()


class Mem:
    pass


def tile_of(ap, t):
    return ap[:, bass.ds(t * TW, TW)]


def padded(ap, t, dy, dx):
    off = (1 + dy) * PADW + 1 + dx
    v = ap[:, bass.ds(t * (2 * PADI) + off, 2 * PADI)]
    return v.rearrange("p (a r c) -> p a r c", a=2, r=PADW)[:, :, 0:SIDE, 0:SIDE]


def conv_ffn_stage(nc, m, layer, out, stats=None):
    p = m.par
    dw_w, dw_s, dw_b = (p[f"dw{layer}_{n}"] for n in "wsb")
    w1, s1, b1 = (p[f"f{layer}_{n}"] for n in ("w1", "s1", "b1"))
    w2, s2, b2 = (p[f"f{layer}_{n}"] for n in ("w2", "s2", "b2"))
    with ExitStack() as c:
        def sb(name, shape, dt=F32):
            return c.enter_context(nc.sbuf_tensor(f"L{layer}_{name}", shape, dt))

        sem = c.enter_context(StageSemaphores(nc, f"L{layer}"))

        taps = sb("taps", [P, 9])
        diag = sb("diag", [P, 9, P])
        y = sb("y", [P, 2, TW])
        hid = sb("hid", [P, 2, 2, TW])
        branch = sb("branch", [P, 2, TW])
        if layer == 0:
            xin = sb("xin", [P, COLS])
        taps_ready, diag_ready = sem("taps_ready"), sem("diag_ready")
        x_landed = [sem(f"x_landed{g}") for g in range(4)]
        pad_zeroed, pad_ready = sem("pad_zeroed"), sem("pad_ready")
        conv_done, y_ready, up_done, hid_ready = sem("conv_done"), sem("y_ready"), sem("up_done"), sem("hid_ready")
        down_done, branch_ready, out_ready, stat_ready = (sem("down_done"), sem("branch_ready"),
                                                          sem("out_ready"), sem("stat_ready"))
        block = c.enter_context(nc.Block())

        if layer == 0:
            @block.sync
            def _(sp):
                xd = m.x.rearrange("(h g b) c n -> g h c b n", h=2, b=4)
                for g in range(4):
                    if g == 0:
                        sp.dma_start(m.chunk["conv0"][:], m.dram["conv0"]).then_inc(m.conv0_landed, 16)
                    for h in range(2):
                        sp.dma_start(xin[C * h:C * h + C, g * 1024:(g + 1) * 1024].rearrange(
                            "p (b n) -> p b n", b=4), xd[g, h]).then_inc(x_landed[g], 16)
                for name, s in (("attn", m.attn_landed), ("rest", m.rest_landed)):
                    sp.dma_start(m.chunk[name][:], m.dram[name]).then_inc(s, 16)
                sp.dma_start(m.w12[:], m.dram["w12"]).then_inc(m.moe_landed, 16)
                sp.dma_start(m.w3[:], m.dram["w3"]).then_inc(m.moe_landed, 16)

        @block.gpsimd
        def _(pool):
            if layer == 0:
                pool.memset(m.xpad[:], 0.0).then_inc(pad_zeroed, 1)
                pool.wait_ge(pad_zeroed, 1)
                for g in range(4):
                    pool.wait_ge(x_landed[g], 32)
                    for a in range(2):
                        pool.tensor_copy(padded(m.xpad, 2 * g + a, 0, 0),
                                         xin[:, (2 * g + a) * TW:(2 * g + a + 1) * TW].rearrange(
                                             "p (a r c) -> p a r c", a=2, r=SIDE)).then_inc(pad_ready, 1)

        @block.tensor
        def _(pe):
            pe.wait_ge(diag_ready, 9)
            with pe.Fori(0, TILES // 2) as i:
                for k in range(2):
                    t = 2 * i + k
                    if layer == 0:
                        pe.wait_ge(pad_ready, t + 1)
                    pe.wait_ge(y_ready, t + 1)
                    for q in range(9):
                        mm = pe.matmul(m.bank[k][:], diag[:, q, :], padded(m.xpad, t, q // 3 - 1, q % 3 - 1),
                                       start=(q == 0), stop=(q == 8))
                    mm.then_inc(conv_done, 1)
                for k in range(2):
                    t = 2 * i + k
                    pe.wait_ge(y_ready, t + 3)
                    for h in range(2):
                        pe.wait_ge(hid_ready, 2 * t + h + 1)
                        pe.matmul(m.bank[2 + 2 * k + h][:], w1[:, h * HID:(h + 1) * HID], y[:, k, :],
                                  start=True, stop=True).then_inc(up_done, 1)
                for k in range(2):
                    t = 2 * i + k
                    pe.wait_ge(branch_ready, t + 1)
                    for h in range(2):
                        pe.wait_ge(hid_ready, 2 * t + h + 5)
                        mm = pe.matmul(m.bank[6 + k][:], w2[:, h * P:(h + 1) * P], hid[:, k, h, :],
                                       start=(h == 0), stop=(h == 1))
                    mm.then_inc(down_done, 1)

        @block.scalar
        def _(act):
            act.sem_inc(y_ready, 2)
            act.sem_inc(hid_ready, 4)
            act.sem_inc(branch_ready, 2)
            if layer == 0:
                act.wait_ge(m.conv0_landed, 16)
            else:
                act.wait_ge(m.rest_landed, 16)
            with act.Fori(0, TILES // 2) as i:
                for k in range(2):
                    t = 2 * i + k
                    act.wait_ge(out_ready, t + 1)
                    act.wait_ge(conv_done, t + 1)
                    act.activation(y[:, k, :], m.bank[k][:], ACT.Identity, bias=dw_b[:, 0:1]).then_inc(y_ready, 1)
                for k in range(2):
                    t = 2 * i + k
                    for h in range(2):
                        act.wait_ge(up_done, 2 * t + h + 1)
                        act.activation(hid[:, k, h, :], m.bank[2 + 2 * k + h][:], ACT.Relu, bias=b1[:, 0:1],
                                       scale=s1[:, 0:1]).then_inc(hid_ready, 1)
                for k in range(2):
                    t = 2 * i + k
                    act.wait_ge(down_done, t + 1)
                    act.activation(branch[:, k, :], m.bank[6 + k][:], ACT.Identity, bias=b2[:, 0:1],
                                   scale=s2[:, 0:1]).then_inc(branch_ready, 1)

        @block.vector
        def _(dve):
            dve.sem_inc(out_ready, 2)
            if layer == 0:
                dve.wait_ge(m.conv0_landed, 16)
            else:
                dve.wait_ge(m.rest_landed, 16)
            dve.tensor_scalar(taps[:], dw_w, dw_s[:, 0:1], None, ALU.mult).then_inc(taps_ready, 1)
            dve.wait_ge(taps_ready, 1)
            dve.tensor_scalar(taps[:, 4:5], taps[:, 4:5], 1.0, None, ALU.add).then_inc(taps_ready, 1)
            dve.wait_ge(taps_ready, 2)
            for q in range(9):
                dve.tensor_scalar(diag[:, q, :], p["ident"], taps[:, q:q + 1], None, ALU.mult)\
                   .then_inc(diag_ready, 1)
            with dve.Fori(0, TILES // 2) as i:
                for k in range(2):
                    t = 2 * i + k
                    dve.wait_ge(y_ready, t + 3)
                    dve.wait_ge(branch_ready, t + 3)
                    dve.tensor_tensor(tile_of(out, t), branch[:, k, :], y[:, k, :], ALU.add).then_inc(out_ready, 1)
                    if stats is not None:
                        dve.wait_ge(out_ready, t + 3)
                        for a in range(2):
                            dve.bn_stats(stats[:, bass.ds(t * 2 + a, 1), :],
                                         out[:, bass.ds(t * TW + a * HW, HW)]).then_inc(stat_ready, 1)


def region(ap3, wi, wj, windowed):
    (r0, nr), (c0, ncol) = SEG[wi], SEG[wj]
    if windowed:
        v = ap3.rearrange("p (a s) -> p a s", a=2)[:, :, 0:WR * WR].rearrange("p a (r c) -> p a r c", r=WR)
        return v[:, :, 0:nr, 0:ncol]
    return ap3.rearrange("p (a r c) -> p a r c", a=2, r=SIDE)[:, :, r0:r0 + nr, c0:c0 + ncol]


def attention_stage(nc, m, x2):
    p = m.par
    U = 2 * NWIN
    UW = U * P
    KVW = 2 * P + 2
    YW = P + 2 * NH
    with ExitStack() as c:
        def sb(name, shape, dt=F32):
            return c.enter_context(nc.sbuf_tensor(f"att_{name}", shape, dt))

        sem = c.enter_context(StageSemaphores(nc, "att"))

        sc = sb("sc", [P, 4, P])
        inv_sc = sb("inv_sc", [P, P])
        wq, wk, pos, floor = sb("wq", [P, P]), sb("wk", [P, P]), sb("pos", [P, P]), sb("floor", [P, P])
        bias = sb("bias", [P, 1])
        xw = sb("xw", [P, U, P])
        base = sb("base", [P, 2, 3 * P])
        sqa, cube, sqb = sb("sqa", [P, 2, 3 * P]), sb("cube", [P, 2, 3 * P]), sb("sqb", [P, 2, 3 * P])
        norms, roots, factor = sb("norms", [P, 2, 12]), sb("roots", [P, 2, 12]), sb("factor", [P, 2, 12])
        kq = sb("kq", [P, 2, 2, 3 * P])
        val = sb("val", [P, U, P])
        valz = sb("valz", [P, U, KVW + 2])
        kvm = sb("kvm", [P, 2, 2, YW])
        qt = sb("qt", [P, 2, P])
        den = sb("den", [P, 2, 3, 2 * NH])
        ysum = sb("ysum", [P, U, P])
        yt = sb("yt", [P, UW])
        proj = sb("proj", [P, UW])
        names = ("ready0 act_ready0 zeroed ind xw_ready qkv_done base_ready sqa_ready cube_ready s2_ready "
                 "sqb_ready s6_ready root_ready inv_ready factor_ready kq_ready v_ready kv_done kvm_ready "
                 "qt_done qt_ready y_done den_ready ysum_ready conv_done conv_added yt_done yt_ready proj_done "
                 "proj_ready out_ready").split()
        s = {n: sem(n) for n in names}
        block = c.enter_context(nc.Block())
        bank = m.bank
        conv_bank = [0, 1, 2, 5]
        chunks = [(0, 4), (4, 4), (8, 4), (12, 4), (16, 2)]
        yt_bank, proj_bank = [0, 1, 2, 5, 3], [4, 6, 7, 4, 6]

        @block.gpsimd
        def _(pool):
            pool.sem_inc(s["out_ready"], 1)
            pool.memset(xw[:], 0.0).then_inc(s["zeroed"], 1)
            pool.memset(valz[:], 0.0).then_inc(s["zeroed"], 1)
            pool.wait_ge(s["zeroed"], 2)
            pool.wait_ge(m.attn_landed, 16)
            for u in range(U):
                pool.tensor_copy(valz[:, u, 2 * P:KVW], p["slots"]).then_inc(s["ind"], 1)
            with pool.Fori(0, TILES // 2) as i:
                pool.wait_ge(s["qkv_done"], 6 * i + 1)
                for u in range(U):
                    k, w = u // NWIN, u % NWIN
                    pool.tensor_copy(region(xw[:, u, :], w // 3, w % 3, True),
                                     region(tile_of(x2, 2 * i + k), w // 3, w % 3, False))\
                        .then_inc(s["xw_ready"], 1)
                pool.wait_ge(s["proj_ready"], 5 * i + 6)
                for u in range(U):
                    k, w = u // NWIN, u % NWIN
                    (r0, nr), (c0, ncol) = SEG[w // 3], SEG[w % 3]
                    pool.tensor_tensor(padded(m.xpad, 2 * i + k, 0, 0)[:, :, r0:r0 + nr, c0:c0 + ncol],
                                       region(proj[:, u * P:(u + 1) * P], w // 3, w % 3, True),
                                       region(tile_of(x2, 2 * i + k), w // 3, w % 3, False), ALU.add)\
                        .then_inc(s["out_ready"], 1)

        @block.tensor
        def _(pe):
            pe.sem_inc(s["yt_done"], 1)
            pe.sem_inc(s["qt_done"], 1)
            pe.sem_inc(s["y_done"], 1)
            pe.sem_inc(s["kv_done"], 1)
            pe.sem_inc(s["conv_done"], 1)
            pe.sem_inc(s["qkv_done"], 1)
            def qkv(i, g):
                pe.wait_ge(s["xw_ready"], U * i + 3 * g + 3)
                pe.wait_ge(s["base_ready"], 6 * i + g + 1)
                pe.wait_ge(s["v_ready"], 6 * i + g + 1)
                for u in range(3):
                    x = xw[:, 3 * g + u, :]
                    o = slice(u * P, (u + 1) * P)
                    pe.matmul(bank[0][:, o], x, wk[:], start=True, stop=True)
                    pe.matmul(bank[1][:, o], x, wq[:], start=True, stop=True)
                    mm = pe.matmul(bank[2][:, o], x, p["wv"], start=True, stop=True)
                mm.then_inc(s["qkv_done"], 1)

            def kv_and_turn(i, n):
                g, u = n // 3, n % 3
                pe.wait_ge(s["kq_ready"], 6 * i + g + 1)
                pe.wait_ge(s["kvm_ready"], U * i + n + 1)
                pe.matmul(bank[3 + n % 2][:, 0:KVW], kq[:, g % 2, 0, u * P:(u + 1) * P], valz[:, n, 0:KVW],
                          start=True, stop=True).then_inc(s["kv_done"], 1)
                pe.wait_ge(s["qt_ready"], U * i + n + 1)
                pe.transpose(bank[5][:, 0:P], kq[:, g % 2, 1, u * P:(u + 1) * P], p["ident"])\
                  .then_inc(s["qt_done"], 1)

            def attend(i, n):
                pe.wait_ge(s["kvm_ready"], U * i + n + 3)
                pe.wait_ge(s["qt_ready"], U * i + n + 2)
                if n % 3 == 0:
                    pe.wait_ge(s["ysum_ready"], 6 * i + n // 3 + 1)
                for a in range(2):
                    o = bank[6][SLOT * a:SLOT * (a + 1), (n % 3) * YW:(n % 3 + 1) * YW]
                    mm = pe.matmul(o, qt[:, n % 2, SLOT * a:SLOT * (a + 1)], kvm[:, n % 2, a, :],
                                   start=True, stop=True)
                mm.then_inc(s["y_done"], 1)

            pe.wait_ge(s["inv_ready"], 4)
            pe.wait_ge(m.attn_landed, 16)
            pe.matmul(bank[7][:, 0:1], p["proj"], p["dwc_b"], start=True, stop=True).then_inc(s["ready0"], 1)
            pe.wait_ge(s["ind"], U)
            pe.wait_ge(s["act_ready0"], 5)
            with pe.Fori(0, TILES // 2) as i:
                pe.wait_ge(s["proj_ready"], 5 * i + 1)
                qkv(i, 0)
                for g in range(6):
                    if g < 5:
                        qkv(i, g + 1)
                    else:
                        pe.wait_ge(s["v_ready"], 6 * i + 7)
                    for u in range(3):
                        kv_and_turn(i, 3 * g + u)
                        if u:
                            attend(i, 3 * g + u - 1)
                    attend(i, 3 * g + 2)
                pe.wait_ge(s["base_ready"], 6 * i + 7)
                pe.wait_ge(s["qt_ready"], U * i + U + 1)
                for dg in range(HD // 2):
                    pe.wait_ge(s["conv_added"], 8 * i + dg + 1)
                    for e in range(2):
                        d = 2 * dg + e
                        rhs = val[:].rearrange("p u (n d) -> p (u n) d", d=HD)[:, :, d]
                        mm = pe.matmul(bank[conv_bank[dg % 4]][:, e * 144:(e + 1) * 144],
                                       p["toep"][:, d * P:(d + 1) * P], rhs, start=True, stop=True)
                    mm.then_inc(s["conv_done"], 1)
                pe.wait_ge(s["conv_added"], 8 * i + 8 + 4)
                pe.wait_ge(s["kvm_ready"], U * i + U + 2)
                for j, (u0, nu) in enumerate(chunks):
                    for u in range(nu):
                        mm = pe.transpose(bank[yt_bank[j]][:, u * P:(u + 1) * P], ysum[:, u0 + u, :], p["ident"])
                    mm.then_inc(s["yt_done"], 1)
                pe.wait_ge(s["ysum_ready"], 6 * i + 7)
                for j, (u0, nu) in enumerate(chunks):
                    pe.wait_ge(s["yt_ready"], 5 * i + j + 1)
                    if j >= 3:
                        pe.wait_ge(s["proj_ready"], 5 * i + j - 1)
                    pe.matmul(bank[proj_bank[j]][:, 0:nu * P], p["proj"], yt[:, u0 * P:(u0 + nu) * P],
                              start=True, stop=True).then_inc(s["proj_done"], 1)

        @block.scalar
        def _(act):
            act.sem_inc(s["proj_ready"], 1)
            act.sem_inc(s["v_ready"], 1)
            act.sem_inc(s["qt_ready"], 1)
            act.wait_ge(m.attn_landed, 16)
            act.activation(sc[:, 0, :], p["scale"], ACT.Abs).then_inc(s["act_ready0"], 1)
            act.wait_ge(s["act_ready0"], 1)
            act.activation(sc[:, 1, :], sc[:, 0, :], ACT.Exp, scale=-1.0).then_inc(s["act_ready0"], 1)
            act.wait_ge(s["act_ready0"], 2)
            act.activation(sc[:, 2, :], sc[:, 1, :], ACT.Ln, bias=1.0).then_inc(s["act_ready0"], 1)
            act.activation(sc[:, 3, :], p["scale"], ACT.Relu).then_inc(s["act_ready0"], 1)
            act.wait_ge(s["ready0"], 1)
            act.activation(bias[:], bank[7][:, 0:1], ACT.Identity, bias=p["proj_b"][:, 0:1])\
               .then_inc(s["act_ready0"], 1)
            act.activation(sc[:, 0, 0:1], sc[:, 3, 0:1], ACT.Sqrt).then_inc(s["act_ready0"], 1)
            act.wait_ge(s["act_ready0"], 6)

            def values(i, g):
                act.wait_ge(s["qkv_done"], 6 * i + g + 2)
                if g == 0:
                    act.wait_ge(s["conv_done"], 8 * i + 1)
                    act.wait_ge(s["kv_done"], U * i + 1)
                v3 = bank[2][:, 0:3 * P].rearrange("p (u n) -> p u n", u=3)
                act.activation(val[:, 3 * g:3 * g + 3, :], v3, ACT.Copy)
                act.activation(valz[0:SLOT, 3 * g:3 * g + 3, 0:P], v3[0:SLOT], ACT.Copy)
                act.activation(valz[SLOT:P, 3 * g:3 * g + 3, P:2 * P], v3[SLOT:P], ACT.Copy)\
                   .then_inc(s["v_ready"], 1)

            def turned(i, n):
                act.wait_ge(s["qt_done"], U * i + n + 2)
                act.wait_ge(s["y_done"], U * i + n + 1)
                act.activation(qt[:, n % 2, :], bank[5][:, 0:P], ACT.Copy).then_inc(s["qt_ready"], 1)

            def square_base(i, g):
                act.wait_ge(s["base_ready"], 6 * i + g + 2)
                act.activation(sqa[:], base[:], ACT.Square).then_inc(s["sqa_ready"], 1)

            def square_cube(i, g):
                act.wait_ge(s["cube_ready"], 6 * i + g + 1)
                act.activation(sqb[:], cube[:], ACT.Square).then_inc(s["sqb_ready"], 1)

            def root(i, g):
                act.wait_ge(s["s2_ready"], 6 * i + g + 1)
                act.wait_ge(s["s6_ready"], 6 * i + g + 1)
                act.activation(roots[:], norms[:], ACT.Sqrt).then_inc(s["root_ready"], 1)

            act.wait_ge(s["ind"], U)
            with act.Fori(0, TILES // 2) as i:
                values(i, 0)
                square_base(i, 0)
                square_cube(i, 0)
                root(i, 0)
                for g in range(6):
                    if g < 5:
                        values(i, g + 1)
                        square_base(i, g + 1)
                    turned(i, 3 * g)
                    if g < 5:
                        square_cube(i, g + 1)
                    turned(i, 3 * g + 1)
                    if g < 5:
                        root(i, g + 1)
                    turned(i, 3 * g + 2)
                for j, (u0, nu) in enumerate(chunks):
                    act.wait_ge(s["yt_done"], 5 * i + j + 2)
                    act.activation(yt[:, u0 * P:(u0 + nu) * P], bank[yt_bank[j]][:, 0:nu * P], ACT.Copy)\
                       .then_inc(s["yt_ready"], 1)
                act.wait_ge(s["out_ready"], U * i + 1)
                for j, (u0, nu) in enumerate(chunks):
                    act.wait_ge(s["proj_done"], 5 * i + j + 1)
                    act.activation(proj[:, u0 * P:(u0 + nu) * P], bank[proj_bank[j]][:, 0:nu * P], ACT.Identity,
                                   bias=bias[:, 0:1]).then_inc(s["proj_ready"], 1)

        @block.vector
        def _(dve):
            dve.sem_inc(s["base_ready"], 1)
            dve.sem_inc(s["kvm_ready"], 2)
            dve.sem_inc(s["ysum_ready"], 1)
            dve.sem_inc(s["conv_added"], 4)
            dve.wait_ge(s["act_ready0"], 4)
            dve.tensor_tensor(inv_sc[:], sc[:, 2, :], sc[:, 3, :], ALU.add).then_inc(s["inv_ready"], 1)
            dve.wait_ge(s["inv_ready"], 1)
            dve.reciprocal(inv_sc[:], inv_sc[:]).then_inc(s["inv_ready"], 1)
            dve.wait_ge(s["inv_ready"], 2)
            dve.tensor_tensor(wq[:], p["wq"], inv_sc[:], ALU.mult)
            dve.tensor_tensor(wk[:], p["wk"], inv_sc[:], ALU.mult)
            dve.tensor_tensor(pos[:], p["pos"], inv_sc[:], ALU.mult).then_inc(s["inv_ready"], 1)
            dve.tensor_scalar(floor[:], inv_sc[:], 1e-6, None, ALU.mult).then_inc(s["inv_ready"], 1)
            dve.wait_ge(s["inv_ready"], 4)

            def over3(ap):
                return ap.unsqueeze(1).broadcast_to([P, 3, P])

            def grouped(ap):
                return ap.rearrange("p z (n c) -> p (z n) c", c=C)

            def base_of(i, g):
                dve.wait_ge(s["qkv_done"], 6 * i + g + 2)
                kps = bank[0][:, 0:3 * P].rearrange("p (u n) -> p u n", u=3)
                qps = bank[1][:, 0:3 * P].rearrange("p (u n) -> p u n", u=3)
                b = base[:].rearrange("p z (u n) -> p z u n", u=3)
                dve.tensor_tensor(b[:, 0], kps, over3(pos[:]), ALU.add).then_inc(s["inv_ready"], 1)
                dve.scalar_tensor_tensor(b[:, 1], qps, 0.0, over3(floor[:]), ALU.max, ALU.add)
                dve.wait_ge(s["inv_ready"], 6 * i + g + 5)
                dve.scalar_tensor_tensor(b[:, 0], b[:, 0], 0.0, over3(floor[:]), ALU.max, ALU.add)\
                   .then_inc(s["base_ready"], 1)

            def cube_of(i, g):
                dve.wait_ge(s["sqa_ready"], 6 * i + g + 1)
                dve.wait_ge(s["base_ready"], 6 * i + g + 2)
                dve.tensor_tensor(cube[:], sqa[:], base[:], ALU.mult).then_inc(s["cube_ready"], 1)
                dve.tensor_reduce(norms[:, 0, :], grouped(sqa[:]), AXX, ALU.add).then_inc(s["s2_ready"], 1)

            def sum6(i, g):
                dve.wait_ge(s["sqb_ready"], 6 * i + g + 1)
                dve.tensor_reduce(norms[:, 1, :], grouped(sqb[:]), AXX, ALU.add).then_inc(s["s6_ready"], 1)

            def normalise(i, g):
                dve.wait_ge(s["root_ready"], 6 * i + g + 1)
                dve.reciprocal(factor[:, 0, :], roots[:, 1, :]).then_inc(s["factor_ready"], 1)
                dve.wait_ge(s["factor_ready"], 12 * i + 2 * g + 1)
                dve.tensor_tensor(factor[:, 1, :], roots[:, 0, :], factor[:, 0, :], ALU.mult)\
                   .then_inc(s["factor_ready"], 1)
                dve.wait_ge(s["factor_ready"], 12 * i + 2 * g + 2)
                if g >= 2:
                    dve.wait_ge(s["qt_done"], U * i + 3 * (g - 1) + 1)
                else:
                    dve.wait_ge(s["qt_done"], U * i + 1)
                dve.tensor_tensor(grouped(kq[:, g % 2]), grouped(cube[:]),
                                  factor[:, 1, :].unsqueeze(2).broadcast_to([P, 12, C]), ALU.mult)\
                   .then_inc(s["kq_ready"], 1)

            def mask_kv(i, n):
                dve.wait_ge(s["kv_done"], U * i + n + 2)
                dve.wait_ge(s["y_done"], U * i + max(n - 1, 0) + 1)
                b = bank[3 + n % 2]
                dve.tensor_tensor(kvm[:, n % 2, :, 0:P], b[:, 0:2 * P].rearrange("p (a n) -> p a n", a=2),
                                  p["headmask"].unsqueeze(1).broadcast_to([P, 2, P]), ALU.mult)
                dve.tensor_tensor(kvm[:, n % 2, :, P:YW],
                                  b[:, 2 * P:KVW].unsqueeze(2).broadcast_to([P, 2, 2 * NH]),
                                  p["headind"].unsqueeze(1).broadcast_to([P, 2, 2 * NH]), ALU.mult)\
                   .then_inc(s["kvm_ready"], 1)

            def divide(i, g):
                dve.wait_ge(s["y_done"], U * i + 3 * g + 4)
                ps = bank[6][:, 0:3 * YW].rearrange("p (u n) -> p u n", u=3)
                dve.tensor_scalar(den[:, 0], ps[:, :, P:YW], 1e-6, None, ALU.add).then_inc(s["den_ready"], 1)
                dve.wait_ge(s["den_ready"], 12 * i + 2 * g + 1)
                dve.reciprocal(den[:, 1], den[:, 0]).then_inc(s["den_ready"], 1)
                dve.wait_ge(s["den_ready"], 12 * i + 2 * g + 2)
                if g == 0:
                    dve.wait_ge(s["yt_done"], 5 * i + 1)
                dve.tensor_tensor(ysum[:, 3 * g:3 * g + 3, :].rearrange("p u (n d) -> p u n d", d=HD),
                                  ps[:, :, 0:P].rearrange("p u (n d) -> p u n d", d=HD),
                                  den[:, 1].unsqueeze(3).broadcast_to([P, 3, 2 * NH, HD]), ALU.mult)\
                   .then_inc(s["ysum_ready"], 1)

            with dve.Fori(0, TILES // 2) as i:
                base_of(i, 0)
                cube_of(i, 0)
                sum6(i, 0)
                normalise(i, 0)
                for g in range(6):
                    if g < 5:
                        base_of(i, g + 1)
                    mask_kv(i, 3 * g)
                    if g < 5:
                        cube_of(i, g + 1)
                    mask_kv(i, 3 * g + 1)
                    if g < 5:
                        sum6(i, g + 1)
                    mask_kv(i, 3 * g + 2)
                    if g < 5:
                        normalise(i, g + 1)
                    divide(i, g)
                dve.wait_ge(s["ysum_ready"], 6 * i + 7)
                for dg in range(HD // 2):
                    dve.wait_ge(s["conv_done"], 8 * i + dg + 2)
                    y = ysum[:].rearrange("p u (n d) -> p d (u n)", d=HD)[:, 2 * dg:2 * dg + 2, :]
                    dve.tensor_tensor(y, y, bank[conv_bank[dg % 4]][:, 0:288].rearrange("p (e n) -> p e n", e=2),
                                      ALU.add).then_inc(s["conv_added"], 1)

def whiten_stage(nc, m):
    p = m.par
    with ExitStack() as c:
        def sb(name, shape, dt=F32):
            return c.enter_context(nc.sbuf_tensor(f"wh_{name}", shape, dt))

        sem = c.enter_context(StageSemaphores(nc, "wh"))

        mv = sb("mv", [P, HB, 2])
        st = sb("st", [P, 2, HB])
        gst = sb("gst", [P, 2, HB])
        gvar, a, b, bc, xv, tmp = (sb(n, [P, HB]) for n in ("gvar", "a", "b", "bc", "xv", "tmp"))
        sums = sb("sums", [P, 4])
        scal = sb("scal", [P, 8])
        h = sb("h", [HB, 8, 2 * HD])
        hs = sb("hs", [HB, 4, 2])
        hT = sb("hT", [2 * HD, HB])
        gate = sb("gate", [P, HB])
        xc = sb("xc", [P, 2, TW])
        xt = sb("xt", [P, 2, TW])
        zero = sb("zero", [P, P])
        gram = sb("gram", [P, P])
        half = sb("half", [P, C])
        sigma = sb("sigma", [P, P])
        pw = sb("pw", [P, 4, P])
        wP = sb("wP", [P, P])
        ga, bias = sb("ga", [P, HB]), sb("bias", [P, HB])
        mat = sb("mat", [P, 4, P])
        names = ("dve_step act_step st_ready pair_done var_ready std_ready sums_ready fold_done mu_ready xm_done "
                 "xv_ready fc1_done hvar_ready hstd_ready hrelu_ready turn_done ht_ready fc2_done sig_ready "
                 "centre_ready xc_ready xt_done xt_ready gram_done tile_gram mask_ready folded trace_in trace_done "
                 "sig_mat prod_done pw_ready wp_ready wb_done b_ready scaled mat_ready app_done out_ready "
                 "scale_in scale_ready").split()
        s = {n: sem(n) for n in names}
        block = c.enter_context(nc.Block())
        bank = m.bank

        @block.tensor
        def _(pe):
            pe.sem_inc(s["app_done"], 1)
            pe.sem_inc(s["tile_gram"], 1)
            pe.sem_inc(s["xt_done"], 1)
            pe.wait_ge(s["st_ready"], 1)
            pe.matmul(bank[0][:, 0:2 * HB], p["pair"], st[:], start=True, stop=True).then_inc(s["pair_done"], 1)
            pe.wait_ge(s["sums_ready"], 1)
            pe.matmul(bank[1][:, 0:2], p["fold"], sums[:, 0:2], start=True, stop=True).then_inc(s["fold_done"], 1)
            pe.matmul(bank[2][0:HB, 0:2 * HD], xv[:], p["fc1"], start=True, stop=True).then_inc(s["fc1_done"], 1)
            pe.wait_ge(s["mu_ready"], 1)
            pe.matmul(bank[3][:, 0:1], p["mean"], sums[:, 3:4], start=True, stop=True).then_inc(s["xm_done"], 1)
            pe.wait_ge(s["hrelu_ready"], 1)
            pe.transpose(bank[2][0:2 * HD, 0:HB], h[:, 7, :], p["ident"][0:HB, 0:HB]).then_inc(s["turn_done"], 1)
            pe.wait_ge(s["ht_ready"], 1)
            pe.matmul(bank[4][:, 0:HB], p["fc2"][0:2 * HD, :], hT[:], start=True, stop=True)\
              .then_inc(s["fc2_done"], 1)
            pe.matmul(bank[7][:, 0:P], zero[:], zero[:], start=True, stop=False, skip_group_check=True)
            with pe.Fori(0, TILES // 2) as i:
                for k in range(2):
                    t = 2 * i + k
                    pe.wait_ge(s["xc_ready"], 2 * t + 2 + 4)
                    pe.wait_ge(s["xt_ready"], t + 1)
                    for q in range(4):
                        mm = pe.transpose(bank[5 + k][:, q * P:(q + 1) * P], xc[:, k, q * P:(q + 1) * P], p["ident"])
                    mm.then_inc(s["xt_done"], 1)
                for k in range(2):
                    t = 2 * i + k
                    pe.wait_ge(s["xt_ready"], t + 3)
                    for q in range(4):
                        o = xt[:, k, q * P:(q + 1) * P]
                        mm = pe.matmul(bank[7][:, 0:P], o, o, start=False, stop=False, skip_group_check=True)
                    mm.then_inc(s["tile_gram"], 1)
            pe.matmul(bank[7][:, 0:P], zero[:], zero[:], start=False, stop=True, skip_group_check=True)\
              .then_inc(s["gram_done"], 1)
            pe.wait_ge(s["mask_ready"], 1)
            pe.matmul(bank[0][:, 0:P], p["fold"], gram[:], start=True, stop=True).then_inc(s["folded"], 1)
            pe.wait_ge(s["trace_in"], 1)
            pe.matmul(bank[1][:, 0:1], p["group16"], sums[:, 2:3], start=True, stop=True).then_inc(s["trace_done"], 1)
            for n in range(2):
                pe.wait_ge(s["pw_ready"], 4 * n + 1)
                pe.matmul(bank[2][:, 0:P], pw[:, 0, :], pw[:, 0, :], start=True, stop=True).then_inc(s["prod_done"], 1)
                pe.wait_ge(s["pw_ready"], 4 * n + 2)
                pe.matmul(bank[3][:, 0:P], pw[:, 1, :], pw[:, 0, :], start=True, stop=True).then_inc(s["prod_done"], 1)
                pe.wait_ge(s["pw_ready"], 4 * n + 3)
                pe.matmul(bank[4][:, 0:P], pw[:, 2, :], sigma[:], start=True, stop=True).then_inc(s["prod_done"], 1)
            pe.wait_ge(s["wp_ready"], 1)
            pe.matmul(bank[0][:, 0:HB], wP[:], b[:], start=True, stop=True).then_inc(s["wb_done"], 1)
            pe.wait_ge(s["b_ready"], 1)
            with pe.Fori(0, HB // 4) as i:
                for k in range(4):
                    n = 4 * i + k
                    pe.wait_ge(s["mat_ready"], n + 1 + 4)
                    pe.wait_ge(s["out_ready"], n + 1)
                    pe.matmul(bank[k + 1][:, 0:HW], mat[:, k, :], m.xa[:, bass.ds(n * HW, HW)],
                              start=True, stop=True).then_inc(s["app_done"], 1)

        @block.scalar
        def _(act):
            act.sem_inc(s["xc_ready"], 4)
            act.wait_ge(s["var_ready"], 1)
            act.activation(a[:], gvar[:], ACT.Sqrt).then_inc(s["std_ready"], 1)
            act.wait_ge(s["xm_done"], 1)
            act.activation(scal[:, 0:1], bank[3][:, 0:1], ACT.Sqrt).then_inc(s["scale_ready"], 1)
            act.wait_ge(s["hvar_ready"], 1)
            act.activation(hs[:, 2, :], hs[:, 1, :], ACT.Sqrt).then_inc(s["hstd_ready"], 1)
            act.activation(scal[:, 1:2], p["x_weight"], ACT.Sigmoid).then_inc(s["sig_ready"], 1)
            act.wait_ge(s["fc2_done"], 1)
            act.activation(gate[:], bank[4][:, 0:HB], ACT.Sigmoid).then_inc(s["sig_ready"], 1)
            act.wait_ge(s["centre_ready"], 1)
            with act.Fori(0, TILES // 2) as i:
                for k in range(2):
                    t = 2 * i + k
                    act.wait_ge(s["xt_done"], 2 * i + 1)
                    for q in range(2):
                        n = 2 * t + q
                        act.activation(xc[:, k, q * HW:(q + 1) * HW], m.xa[:, bass.ds(n * HW, HW)], ACT.Identity,
                                       scale=a[:, bass.ds(n, 1)], bias=bc[:, bass.ds(n, 1)])\
                           .then_inc(s["xc_ready"], 1)

        @block.vector
        def _(dve):
            count = [0]

            def link(ins):
                count[0] += 1
                ins.then_inc(s["dve_step"], 1)
                dve.wait_ge(s["dve_step"], count[0])

            dve.sem_inc(s["xt_ready"], 2)
            dve.sem_inc(s["mat_ready"], 4)
            dve.sem_inc(s["out_ready"], 4)
            for n in range(HB):
                ins = dve.bn_aggr(mv[:, n, :], m.stats[:, n, :])
            link(ins)
            mean_c, var_c = mv[:, :, 0], mv[:, :, 1]
            dve.memset(zero[:], 0.0)
            link(dve.tensor_copy(st[:, 0, :], mean_c))
            link(dve.tensor_tensor(tmp[:], mean_c, mean_c, ALU.mult))
            dve.tensor_tensor(st[:, 1, :], tmp[:], var_c, ALU.add).then_inc(s["st_ready"], 1)
            dve.wait_ge(s["pair_done"], 1)
            link(dve.tensor_copy(gst[:].rearrange("p a b -> p (a b)"), bank[0][:, 0:2 * HB]))
            link(dve.tensor_tensor(tmp[:], gst[:, 0, :], gst[:, 0, :], ALU.mult))
            link(dve.tensor_tensor(gvar[:], gst[:, 1, :], tmp[:], ALU.subtract))
            link(dve.tensor_scalar(gvar[:], gvar[:], 0.0, None, ALU.max))
            dve.tensor_scalar(gvar[:], gvar[:], 1e-5, None, ALU.add).then_inc(s["var_ready"], 1)
            dve.wait_ge(s["std_ready"], 1)
            link(dve.reciprocal(a[:], a[:]))
            link(dve.scalar_tensor_tensor(b[:], gst[:, 0, :], -1.0, a[:], ALU.mult, ALU.mult))
            link(dve.tensor_tensor(tmp[:], a[:], a[:], ALU.mult))
            link(dve.scalar_tensor_tensor(xv[:], tmp[:], float(HW) / (HW - 1), var_c, ALU.mult, ALU.mult))
            link(dve.tensor_tensor(tmp[:], a[:], mean_c, ALU.mult))
            link(dve.tensor_tensor(tmp[:], tmp[:], b[:], ALU.add))
            link(dve.tensor_reduce(sums[:, 0:1], tmp[:], AXX, ALU.add))
            dve.tensor_reduce(sums[:, 1:2], xv[:], AXX, ALU.add).then_inc(s["sums_ready"], 1)
            dve.wait_ge(s["fold_done"], 1)
            link(dve.tensor_scalar(scal[:, 2:3], bank[1][:, 0:1], 1.0 / B, None, ALU.mult))
            dve.tensor_scalar(sums[:, 3:4], bank[1][:, 1:2], 1.0 / B, None, ALU.mult).then_inc(s["mu_ready"], 1)
            dve.tensor_scalar(bc[:], b[:], scal[:, 2:3], None, ALU.subtract).then_inc(s["centre_ready"], 1)
            def two(v):
                return v.rearrange("p (h j) -> p h j", h=2)

            def over16(v):
                return v.unsqueeze(2).broadcast_to([HB, 2, HD])

            dve.wait_ge(s["fc1_done"], 1)
            link(dve.tensor_copy(h[:, 0, :], bank[2][0:HB, 0:2 * HD]))
            link(dve.tensor_reduce(hs[:, 0, :], two(h[:, 0, :]), AXX, ALU.add))
            link(dve.tensor_scalar(hs[:, 0, :], hs[:, 0, :], 1.0 / HD, None, ALU.mult))
            link(dve.tensor_tensor(two(h[:, 1, :]), two(h[:, 0, :]), over16(hs[:, 0, :]), ALU.subtract))
            link(dve.tensor_tensor(h[:, 2, :], h[:, 1, :], h[:, 1, :], ALU.mult))
            link(dve.tensor_reduce(hs[:, 1, :], two(h[:, 2, :]), AXX, ALU.add))
            dve.tensor_scalar(hs[:, 1, :], hs[:, 1, :], 1.0 / HD, 1e-5, ALU.mult, ALU.add).then_inc(s["hvar_ready"], 1)
            dve.wait_ge(s["hstd_ready"], 1)
            link(dve.reciprocal(hs[:, 3, :], hs[:, 2, :]))
            link(dve.tensor_tensor(two(h[:, 3, :]), two(h[:, 1, :]), over16(hs[:, 3, :]), ALU.mult))
            link(dve.tensor_tensor(h[:, 4, :], h[:, 3, :], p["ln_g"][0:HB, :], ALU.mult))
            link(dve.tensor_tensor(h[:, 5, :], h[:, 4, :], p["ln_b"][0:HB, :], ALU.add))
            dve.tensor_scalar(h[:, 7, :], h[:, 5, :], 0.0, None, ALU.max).then_inc(s["hrelu_ready"], 1)
            dve.wait_ge(s["turn_done"], 1)
            dve.tensor_copy(hT[:], bank[2][0:2 * HD, 0:HB]).then_inc(s["ht_ready"], 1)
            with dve.Fori(0, TILES // 2) as i:
                for k in range(2):
                    t = 2 * i + k
                    dve.wait_ge(s["xt_done"], t + 2)
                    dve.wait_ge(s["tile_gram"], 2 * i + 1)
                    dve.tensor_copy(xt[:, k, :], bank[5 + k][:]).then_inc(s["xt_ready"], 1)
            dve.wait_ge(s["scale_ready"], 1)
            link(dve.reciprocal(scal[:, 3:4], scal[:, 0:1]))
            dve.wait_ge(s["sig_ready"], 2)
            link(dve.tensor_scalar(scal[:, 4:5], scal[:, 1:2], -1.0, 1.0, ALU.mult, ALU.add))
            link(dve.tensor_tensor(scal[:, 5:6], scal[:, 4:5], scal[:, 3:4], ALU.mult))
            link(dve.tensor_scalar(gate[:], gate[:], scal[:, 5:6], None, ALU.mult))
            link(dve.tensor_tensor(ga[:], gate[:], a[:], ALU.mult))
            dve.wait_ge(s["gram_done"], 1)
            dve.tensor_tensor(gram[:], bank[7][:, 0:P], p["group16"], ALU.mult).then_inc(s["mask_ready"], 1)
            dve.wait_ge(s["folded"], 1)
            link(dve.tensor_copy(pw[:, 3, :], bank[0][:, 0:P]))
            link(dve.tensor_tensor(half[:], pw[:, 3, 0:C], pw[:, 3, C:P], ALU.add))
            link(dve.tensor_tensor(sigma[:].rearrange("p (h n) -> p h n", h=2),
                                   half[:].unsqueeze(1).broadcast_to([P, 2, C]),
                                   p["group16"].rearrange("p (h n) -> p h n", h=2), ALU.mult))
            link(dve.tensor_scalar(sigma[:], sigma[:], 1e-5, None, ALU.mult))
            link(dve.scalar_tensor_tensor(sigma[:], p["ident"], 1.0 / (B * HW), sigma[:], ALU.mult, ALU.add))
            link(dve.tensor_tensor(pw[:, 3, :], sigma[:], p["ident"], ALU.mult))
            dve.tensor_reduce(sums[:, 2:3], pw[:, 3, :], AXX, ALU.add).then_inc(s["trace_in"], 1)
            dve.wait_ge(s["trace_done"], 1)
            link(dve.reciprocal(scal[:, 6:7], bank[1][:, 0:1]))
            link(dve.tensor_scalar(sigma[:], sigma[:], scal[:, 6:7], None, ALU.mult))
            link(dve.tensor_scalar(pw[:, 3, :], sigma[:], 1.5, None, ALU.mult))
            dve.scalar_tensor_tensor(pw[:, 0, :], p["ident"], -0.5, pw[:, 3, :], ALU.mult, ALU.add)\
               .then_inc(s["pw_ready"], 1)
            for n in range(2):
                dve.wait_ge(s["prod_done"], 3 * n + 1)
                dve.tensor_copy(pw[:, 1, :], bank[2][:, 0:P]).then_inc(s["pw_ready"], 1)
                dve.wait_ge(s["prod_done"], 3 * n + 2)
                dve.tensor_copy(pw[:, 2, :], bank[3][:, 0:P]).then_inc(s["pw_ready"], 1)
                dve.wait_ge(s["prod_done"], 3 * n + 3)
                link(dve.tensor_scalar(pw[:, 3, :], bank[4][:, 0:P], 1.5, None, ALU.mult))
                link(dve.scalar_tensor_tensor(pw[:, 0, :], pw[:, 0, :], -0.5, pw[:, 3, :], ALU.mult, ALU.add))
                dve.sem_inc(s["pw_ready"], 2)
            dve.tensor_scalar(wP[:], pw[:, 0, :], scal[:, 1:2], None, ALU.mult).then_inc(s["wp_ready"], 1)
            link(dve.tensor_tensor(bias[:], gate[:], b[:], ALU.mult))
            dve.wait_ge(s["wb_done"], 1)
            link(dve.tensor_tensor(bias[:], bias[:], bank[0][:, 0:HB], ALU.add))
            dve.sem_inc(s["b_ready"], 1)

            def matrix(n, k):
                dve.tensor_scalar(mat[:, k, :], wP[:], a[:, bass.ds(n, 1)], None, ALU.mult).then_inc(s["scaled"], 1)
                dve.wait_ge(s["scaled"], n + 1)
                dve.scalar_tensor_tensor(mat[:, k, :], p["ident"], ga[:, bass.ds(n, 1)], mat[:, k, :],
                                         ALU.mult, ALU.add).then_inc(s["mat_ready"], 1)

            dve.wait_ge(s["wp_ready"], 1)
            with dve.Fori(0, HB // 4) as i:
                for k in range(4):
                    dve.wait_ge(s["app_done"], 4 * i + 1)
                    matrix(4 * i + k, k)
                for k in range(4):
                    n = 4 * i + k
                    dve.wait_ge(s["app_done"], n + 2)
                    x = m.xa[:, bass.ds(n * HW, HW)]
                    dve.scalar_tensor_tensor(x, bank[k + 1][:, 0:HW], bias[:, bass.ds(n, 1)], x, ALU.add, ALU.add)\
                       .then_inc(s["out_ready"], 1)

def slice_attention_stage(nc, m):
    p = m.par
    LOG_NEG_LOG_EPS = float(np.log(-np.log(np.float32(1e-6)), dtype=np.float32))
    with ExitStack() as c:
        def sb(name, shape, dt=F32):
            return c.enter_context(nc.sbuf_tensor(f"sl_{name}", shape, dt))

        b_slice = sb("b_slice", [P, 1])
        sq, std, xn = sb("sq", [P, 2, TW]), sb("std", [P, 2, TW]), sb("xn", [P, 2, TW])
        xps = sb("xps", [P, 2, TW])
        clip, logit = sb("clip", [P, 2, TW]), sb("logit", [P, 2, TW])
        negmax = sb("negmax", [P, 2, 2])
        ex = sb("ex", [P, 2, 2, TW])
        tot, f = sb("tot", [P, 2, 4]), sb("f", [P, 4, 4])
        xpt = sb("xpt", [P, 2, 4, 2 * P])
        et = sb("et", [P, 2, TW])
        gtm, bm = sb("gtm", [P, 4, P]), sb("bm", [P, 4, P])
        names = ("bs_ready centred sq_ready var_done std_ready inv_ready xn_ready xp_done xps_ready lt_done "
                 "clip1 clip2 clip3 logit_ready max_ready negmax_ready ex_ready xpt_done xpt_ready et_done "
                 "et_ready gt_done gtm_ready b_done f_step bm_ready o_done out_ready warm").split()
        sem = c.enter_context(StageSemaphores(nc, "sl"))
        s = {n: sem(n) for n in names}
        block = c.enter_context(nc.Block())
        bank = m.bank
        XP, LG, TM = (4, 7), (2, 0), (3, 1)

        @block.tensor
        def _(pe):
            pe.sem_inc(s["xpt_done"], 1)
            pe.sem_inc(s["gt_done"], 1)
            pe.sem_inc(s["o_done"], 1)
            pe.sem_inc(s["lt_done"], 1)
            with pe.Fori(0, TILES // 2) as i:
                pe.wait_ge(s["out_ready"], 2 * i + 1)
                pe.wait_ge(s["logit_ready"], 4 * i + 1)
                for k in range(2):
                    pe.matmul(bank[k][:], p["center"], tile_of(m.xa, 2 * i + k), start=True, stop=True)\
                      .then_inc(s["centred"], 1)
                for k in range(2):
                    pe.wait_ge(s["sq_ready"], 2 * i + k + 1)
                    pe.matmul(bank[2 + k][:], p["mean"], sq[:, k, :], start=True, stop=True)\
                      .then_inc(s["var_done"], 1)
                for k in range(2):
                    t = 2 * i + k
                    pe.wait_ge(s["xn_ready"], 2 * i + 2)
                    for h in range(2):
                        pe.wait_ge(s["xps_ready"], 2 * t + 1)
                        pe.wait_ge(s["gtm_ready"], 2 * i + 1)
                        pe.wait_ge(s["bm_ready"], 2 * i + 1)
                        pe.matmul(bank[XP[h]][:], p["w_x"][:, h * P:(h + 1) * P], xn[:, k, :],
                                  start=True, stop=True).then_inc(s["xp_done"], 1)
                    pe.wait_ge(s["xpt_ready"], 2 * t + 1)
                    pe.wait_ge(s["et_ready"], 4 * i + 1)
                    for q in range(4):
                        mm = pe.matmul(bank[5 + q // 2][:, (q % 2) * 2 * P:(q % 2 + 1) * 2 * P],
                                       xn[:, k, q * P:(q + 1) * P], p["w_x"], start=True, stop=True)
                        if q % 2:
                            mm.then_inc(s["xpt_done"], 1)
                    for h in range(2):
                        pe.wait_ge(s["xps_ready"], 2 * t + h + 2)
                        pe.wait_ge(s["logit_ready"], 2 * t + 1)
                        pe.matmul(bank[TM[h]][:], p["w_temp"], xps[:, h, :], start=True, stop=True)
                        pe.matmul(bank[LG[h]][:], p["w_slice"], xps[:, h, :], start=True, stop=True)\
                          .then_inc(s["lt_done"], 1)
                for k in range(2):
                    t = 2 * i + k
                    pe.wait_ge(s["xpt_ready"], 4 * i + 5)
                    pe.wait_ge(s["et_ready"], 2 * t + 1)
                    for h in range(2):
                        pe.wait_ge(s["ex_ready"], 4 * t + 2 * h + 3)
                        for q in range(4):
                            mm = pe.transpose(bank[5 + h][:, q * P:(q + 1) * P], ex[:, k, h, q * P:(q + 1) * P],
                                              p["ident"])
                        mm.then_inc(s["et_done"], 1)
                    pe.wait_ge(s["gtm_ready"], t + 1)
                    for h in range(2):
                        pe.wait_ge(s["et_ready"], 2 * t + h + 2)
                        for b in range(2):
                            for q in (2 * b, 2 * b + 1):
                                mm = pe.matmul(bank[4][:, (2 * h + b) * P:(2 * h + b + 1) * P],
                                               xpt[:, k, q, h * P:(h + 1) * P], et[:, h, q * P:(q + 1) * P],
                                               start=(q == 2 * b), stop=(q == 2 * b + 1))
                    mm.then_inc(s["gt_done"], 1)
                    pe.wait_ge(s["gtm_ready"], t + 2)
                    pe.wait_ge(s["bm_ready"], t + 1)
                    for n in range(4):
                        mm = pe.matmul(bank[7][:, n * P:(n + 1) * P], gtm[:, n, :],
                                       p["w_out"][:, (n // 2) * P:(n // 2 + 1) * P], start=True, stop=True)
                    mm.then_inc(s["b_done"], 1)
                    pe.wait_ge(s["bm_ready"], t + 2)
                    pe.wait_ge(s["out_ready"], t + 1)
                    pe.wait_ge(s["logit_ready"], 4 * i + 5)
                    for b in range(2):
                        for h in range(2):
                            mm = pe.matmul(bank[2][:, b * HW:(b + 1) * HW], bm[:, 2 * h + b, :],
                                           ex[:, k, h, b * HW:(b + 1) * HW], start=(h == 0), stop=(h == 1))
                    mm.then_inc(s["o_done"], 1)

        @block.scalar
        def _(act):
            act.sem_inc(s["ex_ready"], 1)
            act.sem_inc(s["et_ready"], 1)
            act.sem_inc(s["xps_ready"], 1)
            act.activation(std[:, 0, 0:1], p["ident"][:, 0:1], ACT.Sqrt).then_inc(s["warm"], 1)
            act.wait_ge(s["warm"], 1)
            with act.Fori(0, TILES // 2) as i:
                for k in range(2):
                    act.wait_ge(s["centred"], 2 * i + k + 1)
                    act.activation(sq[:, k, :], bank[k][:], ACT.Square).then_inc(s["sq_ready"], 1)
                for k in range(2):
                    act.wait_ge(s["var_done"], 2 * i + k + 1)
                    act.activation(std[:, k, :], bank[2 + k][:], ACT.Sqrt, bias=m.eps5[:, 0:1])\
                       .then_inc(s["std_ready"], 1)
                for k in range(2):
                    t = 2 * i + k
                    for h in range(2):
                        act.wait_ge(s["xp_done"], 2 * t + h + 1)
                        act.wait_ge(s["lt_done"], 2 * t + 1)
                        act.activation(xps[:, h, :], bank[XP[h]][:], ACT.Identity, bias=p["b_x"][:, 0:1])\
                           .then_inc(s["xps_ready"], 1)
                    for h in range(2):
                        act.wait_ge(s["negmax_ready"], 2 * t + h + 1)
                        act.wait_ge(s["o_done"], 2 * i + 1)
                        for b in range(2):
                            act.activation(ex[:, k, h, b * HW:(b + 1) * HW], logit[:, h, b * HW:(b + 1) * HW],
                                           ACT.Exp, bias=negmax[:, h, b:b + 1],
                                           accum_out=tot[:, k, 2 * h + b:2 * h + b + 1]).then_inc(s["ex_ready"], 1)
                for k in range(2):
                    t = 2 * i + k
                    for h in range(2):
                        act.wait_ge(s["et_done"], 2 * t + h + 1)
                        act.wait_ge(s["gt_done"], t + 1)
                        act.activation(et[:, h, :], bank[5 + h][:], ACT.Copy).then_inc(s["et_ready"], 1)

        @block.vector
        def _(dve):
            dve.sem_inc(s["xpt_ready"], 1)
            dve.sem_inc(s["bm_ready"], 1)
            dve.sem_inc(s["gtm_ready"], 1)
            dve.sem_inc(s["logit_ready"], 1)
            dve.sem_inc(s["out_ready"], 1)
            dve.tensor_scalar(b_slice[:], p["b_slice"], LOG_NEG_LOG_EPS, None, ALU.subtract).then_inc(s["bs_ready"], 1)
            dve.wait_ge(s["bs_ready"], 1)
            with dve.Fori(0, TILES // 2) as i:
                for k in range(2):
                    t = 2 * i + k
                    dve.wait_ge(s["std_ready"], t + 1)
                    dve.reciprocal(std[:, k, :], std[:, k, :]).then_inc(s["inv_ready"], 1)
                    dve.wait_ge(s["inv_ready"], t + 1)
                    dve.wait_ge(s["xpt_done"], 4 * i + 1)
                    dve.tensor_tensor(xn[:, k, :], bank[k][:], std[:, k, :], ALU.mult).then_inc(s["xn_ready"], 1)
                for k in range(2):
                    t = 2 * i + k
                    for j in range(2):
                        dve.wait_ge(s["xpt_done"], 2 * t + j + 2)
                        if k == 0:
                            dve.wait_ge(s["gt_done"], 2 * i + 1)
                        dve.tensor_tensor(xpt[:, k, 2 * j:2 * j + 2, :],
                                          bank[5 + j][:].rearrange("p (q n) -> p q n", q=2),
                                          p["b_x_row"].unsqueeze(1).broadcast_to([P, 2, 2 * P]), ALU.add)\
                           .then_inc(s["xpt_ready"], 1)
                    for h in range(2):
                        n = 2 * t + h
                        dve.wait_ge(s["lt_done"], n + 2)
                        dve.tensor_scalar(clip[:, h, :], bank[TM[h]][:], p["b_temp"][:, 0:1], 0.4, ALU.add, ALU.min)\
                           .then_inc(s["clip1"], 1)
                        dve.wait_ge(s["clip1"], n + 1)
                        dve.tensor_scalar(clip[:, h, :], clip[:, h, :], -0.4, 0.5, ALU.max, ALU.add)\
                           .then_inc(s["clip2"], 1)
                        dve.wait_ge(s["clip2"], n + 1)
                        dve.reciprocal(clip[:, h, :], clip[:, h, :]).then_inc(s["clip3"], 1)
                        dve.wait_ge(s["clip3"], n + 1)
                        dve.wait_ge(s["ex_ready"], 4 * t + 1)
                        dve.scalar_tensor_tensor(logit[:, h, :], bank[LG[h]][:], b_slice[:, 0:1], clip[:, h, :],
                                                 ALU.add, ALU.mult).then_inc(s["logit_ready"], 1)
                        dve.wait_ge(s["logit_ready"], n + 2)
                        dve.tensor_reduce(negmax[:, h, :], logit[:, h, :].rearrange("p (b n) -> p b n", b=2),
                                          AXX, ALU.max).then_inc(s["max_ready"], 1)
                        dve.wait_ge(s["max_ready"], n + 1)
                        dve.tensor_scalar(negmax[:, h, :], negmax[:, h, :], -1.0, None, ALU.mult)\
                           .then_inc(s["negmax_ready"], 1)
                for k in range(2):
                    t = 2 * i + k
                    dve.wait_ge(s["ex_ready"], 4 * t + 5)
                    dve.reciprocal(f[:, 0, :], tot[:, k, :]).then_inc(s["f_step"], 1)
                    dve.wait_ge(s["f_step"], 5 * t + 1)
                    dve.tensor_tensor(f[:, 1, :], tot[:, k, :], f[:, 0, :], ALU.mult).then_inc(s["f_step"], 1)
                    dve.wait_ge(s["f_step"], 5 * t + 2)
                    dve.tensor_scalar(f[:, 1, :], f[:, 1, :], 1e-5, None, ALU.add).then_inc(s["f_step"], 1)
                    dve.wait_ge(s["f_step"], 5 * t + 3)
                    dve.reciprocal(f[:, 2, :], f[:, 1, :]).then_inc(s["f_step"], 1)
                    dve.wait_ge(s["f_step"], 5 * t + 4)
                    dve.tensor_tensor(f[:, 2, :], f[:, 2, :], f[:, 0, :], ALU.mult).then_inc(s["f_step"], 1)
                    dve.wait_ge(s["f_step"], 5 * t + 5)
                    dve.tensor_tensor(f[:, 3, :], f[:, 2, :], f[:, 0, :], ALU.mult)
                    dve.wait_ge(s["gt_done"], t + 2)
                    dve.tensor_tensor(gtm[:], bank[4][:].rearrange("p (n g) -> p n g", n=4),
                                      p["headmask"].unsqueeze(1).broadcast_to([P, 4, P]), ALU.mult)\
                       .then_inc(s["gtm_ready"], 1)
                    dve.wait_ge(s["b_done"], t + 1)
                    dve.wait_ge(s["gtm_ready"], t + 2)
                    dve.tensor_tensor(bm[:], bank[7][:].rearrange("p (n g) -> p n g", n=4),
                                      f[:, 3, :].unsqueeze(2).broadcast_to([P, 4, P]), ALU.mult)\
                       .then_inc(s["bm_ready"], 1)
                    dve.wait_ge(s["o_done"], t + 2)
                    x = tile_of(m.xa, t)
                    dve.scalar_tensor_tensor(x, bank[2][:], p["b_out"][:, 0:1], x, ALU.add, ALU.add)\
                       .then_inc(s["out_ready"], 1)


def lstm_stage(nc, m):
    p = m.par
    STEPS = 8
    CH = STEPS * HB
    SC = 2.0 ** 12
    with ExitStack() as c:
        def sb(name, shape, dt=F32):
            return c.enter_context(nc.sbuf_tensor(f"ls_{name}", shape, dt))

        xn = sb("xn", [P, COLS + CH])
        hs = sb("hs", [P, COLS])
        sq, std = sb("sq", [P, 4, TW]), sb("std", [P, 4, TW])
        u = sb("u", [P, 3, P])
        bias = sb("bias", [P, P])
        vs, rest = sb("vs", [P, 3, P]), sb("rest", [P, 3, P])
        vp = [sb(f"v{k}", [P, 3, P], BF16) for k in range(3)]
        gates, ig, cell, hc, tc = (sb("gates", [P, 3, HB]), sb("ig", [P, HB]), sb("cell", [P, HB]),
                                   sb("hc", [P, HB]), sb("tc", [P, HB]))
        og = sb("og", [P, HB])
        h1, h2 = sb("h1", [P, HB], F16), sb("h2", [P, HB], F16)
        names = ("w_step u_ready centred sq_ready var_done std_ready inv_ready xn_ready zeros warm z_done "
                 "gates_ready ig_ready cell_ready tc_ready og_ready h1_ready h32_ready h2_ready hc_ready "
                 "out_ready").split()
        sem = c.enter_context(StageSemaphores(nc, "ls"))
        s = {n: sem(n) for n in names}
        block = c.enter_context(nc.Block())
        bank = m.bank
        xn_bt = xn[:, 0:COLS].rearrange("p (t b) -> p b t", b=HB)
        hs_bt = hs[:].rearrange("p (t b) -> p b t", b=HB)
        xa_bt = m.xa[:].rearrange("p (b t) -> p b t", b=HB)

        @block.tensor
        def _(pe):
            pe.sem_inc(s["var_done"], 1)
            with pe.Fori(0, TILES // 4) as i:
                for k in range(4):
                    pe.wait_ge(s["xn_ready"], 4 * i + 1)
                    pe.matmul(bank[k][:], p["center"], tile_of(m.xa, 4 * i + k), start=True, stop=True)\
                      .then_inc(s["centred"], 1)
                for k in range(4):
                    pe.wait_ge(s["sq_ready"], 4 * i + k + 1)
                    pe.matmul(bank[4 + k][:], p["mean"], sq[:, k, :], start=True, stop=True)\
                      .then_inc(s["var_done"], 1)

            def prepare(chunk, b, part):
                if part == 0:
                    pe.matmul(bank[b][:, 0:3 * CH], bias[0:3, :], p["gate_sel"][0:3, :], start=True, stop=False,
                              skip_group_check=True)
                else:
                    o = bank[b][:, 0:3 * CH].rearrange("p (s g b) -> p s g b", s=STEPS, g=3)[:, :, part - 1, :]
                    pe.matmul(o, u[:, part - 1, :], xn[:, bass.ds(chunk * CH, CH)], start=False, stop=False,
                              skip_group_check=True)

            pe.wait_ge(s["xn_ready"], TILES + 1)
            pe.wait_ge(s["u_ready"], 1)
            pe.wait_ge(s["zeros"], 1)
            for part in range(4):
                prepare(0, 0, part)
            with pe.Fori(0, HW // (2 * STEPS)) as i:
                for b in range(2):
                    for q in range(STEPS):
                        t = 2 * STEPS * i + STEPS * b + q
                        pe.wait_ge(s["h1_ready"], t + 1)
                        for part in range(3):
                            for g in range(3):
                                o = bank[b][:, (3 * q + g) * HB:(3 * q + g + 1) * HB]
                                pe.matmul(o, vp[part][:, g, :], h1[:], start=False, stop=False,
                                          skip_group_check=True)
                        pe.wait_ge(s["h2_ready"], t + 1)
                        for part in range(2):
                            for g in range(3):
                                o = bank[b][:, (3 * q + g) * HB:(3 * q + g + 1) * HB]
                                mm = pe.matmul(o, vp[part][:, g, :], h2[:], start=False, stop=(part == 1),
                                               skip_group_check=True)
                        mm.then_inc(s["z_done"], 1)
                        if q < 4:
                            prepare(2 * i + b + 1, 1 - b, q)

        @block.scalar
        def _(act):
            act.activation(std[:, 0, 0:1], p["ident"][:, 0:1], ACT.Sqrt).then_inc(s["warm"], 1)
            act.wait_ge(s["warm"], 1)
            with act.Fori(0, TILES // 4) as i:
                for k in range(4):
                    act.wait_ge(s["centred"], 4 * i + k + 1)
                    act.wait_ge(s["var_done"], 4 * i + 1)
                    act.activation(sq[:, k, :], bank[k][:], ACT.Square).then_inc(s["sq_ready"], 1)
                for k in range(4):
                    act.wait_ge(s["var_done"], 4 * i + k + 2)
                    act.wait_ge(s["xn_ready"], 4 * i + 1)
                    act.activation(std[:, k, :], bank[4 + k][:], ACT.Sqrt, bias=m.eps5[:, 0:1])\
                       .then_inc(s["std_ready"], 1)
            act.wait_ge(s["xn_ready"], TILES + 1)
            act.activation(std[:, 0, 0:1], p["ident"][:, 0:1], ACT.Tanh).then_inc(s["warm"], 1)
            with act.Fori(0, HW // (2 * STEPS)) as i:
                for b in range(2):
                    for q in range(STEPS):
                        t = 2 * STEPS * i + STEPS * b + q
                        act.wait_ge(s["z_done"], t + 1)
                        act.activation(gates[:], bank[b][:, 3 * q * HB:3 * (q + 1) * HB].rearrange(
                            "p (g b) -> p g b", g=3), ACT.Tanh).then_inc(s["gates_ready"], 1)
                        act.wait_ge(s["cell_ready"], t + 1)
                        act.activation(tc[:], cell[:], ACT.Tanh).then_inc(s["tc_ready"], 1)

        @block.vector
        def _(dve):
            dve.sem_inc(s["xn_ready"], 1)
            count = [0]

            def link(ins):
                count[0] += 1
                ins.then_inc(s["w_step"], 1)
                dve.wait_ge(s["w_step"], count[0])

            for g, n in enumerate("igo"):
                half = 1.0 if n == "g" else 0.5
                dve.tensor_scalar(u[:, g, :], p[f"u_{n}"], half, None, ALU.mult)
                dve.tensor_scalar(vs[:, g, :], p[f"v_{n}"], half / SC, None, ALU.mult)
            link(dve.tensor_scalar(bias[0:3, :], p["lstm_b"][0:3, :], p["lstm_half"][0:3, :], None, ALU.mult))
            link(dve.tensor_copy(vp[0][:], vs[:]))
            link(dve.tensor_tensor(rest[:], vs[:], vp[0][:], ALU.subtract))
            link(dve.tensor_copy(vp[1][:], rest[:]))
            link(dve.tensor_tensor(vs[:], rest[:], vp[1][:], ALU.subtract))
            dve.tensor_copy(vp[2][:], vs[:])
            dve.memset(xn[:, COLS:COLS + CH], 0.0)
            dve.memset(hc[:], 0.0)
            dve.memset(h1[:], 0.0)
            link(dve.memset(h2[:], 0.0))
            dve.sem_inc(s["u_ready"], 1)
            dve.sem_inc(s["zeros"], 1)
            dve.sem_inc(s["h1_ready"], 1)
            dve.sem_inc(s["h2_ready"], 1)
            dve.sem_inc(s["hc_ready"], 1)
            with dve.Fori(0, TILES // 4) as i:
                for k in range(4):
                    t = 4 * i + k
                    dve.wait_ge(s["std_ready"], t + 1)
                    dve.reciprocal(std[:, k, :], std[:, k, :]).then_inc(s["inv_ready"], 1)
                    dve.wait_ge(s["inv_ready"], t + 1)
                    dve.tensor_tensor(xn_bt[:, bass.ds(2 * t, 2), :], bank[k][:].rearrange("p (b t) -> p b t", b=2),
                                      std[:, k, :].rearrange("p (b t) -> p b t", b=2), ALU.mult)\
                       .then_inc(s["xn_ready"], 1)
            with dve.Fori(0, HW // (2 * STEPS)) as i:
                for b in range(2):
                    for q in range(STEPS):
                        t = 2 * STEPS * i + STEPS * b + q
                        dve.wait_ge(s["gates_ready"], t + 1)
                        dve.scalar_tensor_tensor(ig[:], gates[:, 0, :], 1.0, gates[:, 1, :], ALU.add, ALU.mult)\
                           .then_inc(s["ig_ready"], 1)
                        dve.wait_ge(s["ig_ready"], t + 1)
                        dve.wait_ge(s["hc_ready"], t + 1)
                        dve.scalar_tensor_tensor(cell[:], ig[:], 0.5, hc[:], ALU.mult, ALU.add)\
                           .then_inc(s["cell_ready"], 1)
                        dve.tensor_scalar(og[:], gates[:, 2, :], SC / 2, SC / 2, ALU.mult, ALU.add)\
                           .then_inc(s["og_ready"], 1)
                        dve.wait_ge(s["og_ready"], t + 1)
                        dve.wait_ge(s["tc_ready"], t + 1)
                        h32 = hs[:, bass.ds(t * HB, HB)]
                        dve.tensor_tensor(h1[:], og[:], tc[:], ALU.mult).then_inc(s["h1_ready"], 1)
                        dve.tensor_tensor(h32, og[:], tc[:], ALU.mult).then_inc(s["h32_ready"], 1)
                        dve.wait_ge(s["h32_ready"], t + 1)
                        dve.tensor_tensor(h2[:], h32, h1[:], ALU.subtract).then_inc(s["h2_ready"], 1)
                        dve.scalar_tensor_tensor(hc[:], h32, 1.0 / SC, cell[:], ALU.mult, ALU.mult)\
                           .then_inc(s["hc_ready"], 1)
                    t0 = 2 * STEPS * i + STEPS * b
                    x = xa_bt[:, :, bass.ds(t0, STEPS)]
                    dve.scalar_tensor_tensor(x, hs_bt[:, :, bass.ds(t0, STEPS)], 1.0 / SC, x, ALU.mult, ALU.add)\
                       .then_inc(s["out_ready"], 1)

def sigmoid_attention_stage(nc, m):
    p = m.par
    with ExitStack() as c:
        def sb(name, shape, dt=F32):
            return c.enter_context(nc.sbuf_tensor(f"sg_{name}", shape, dt))

        sem = c.enter_context(StageSemaphores(nc, "sg"))
        sq, std, xn = sb("sq", [P, 2, TW]), sb("std", [P, 2, TW]), sb("xn", [P, 2, TW])
        qz = sb("qz", [P, 2, TW])
        xt = sb("xt", [P, TW])
        att = sb("att", [P, 3, TW])
        names = ("zeroed warm centred sq_ready var_done std_ready inv_ready xn_ready q_done q_ready xt_done "
                 "xt_ready s_done att_ready v_done out_ready").split()
        s = {n: sem(n) for n in names}
        block = c.enter_context(nc.Block())
        bank = m.bank
        SB = (6, 7, 3)

        @block.tensor
        def _(pe):
            pe.sem_inc(s["v_done"], 1)
            pe.sem_inc(s["s_done"], 1)
            with pe.Fori(0, TILES // 2) as i:
                pe.wait_ge(s["out_ready"], 2 * i + 1)
                pe.wait_ge(s["att_ready"], 8 * i + 1)
                for k in range(2):
                    pe.matmul(bank[k][:], p["center"], tile_of(m.xa, 2 * i + k), start=True, stop=True)\
                      .then_inc(s["centred"], 1)
                for k in range(2):
                    pe.wait_ge(s["sq_ready"], 2 * i + k + 1)
                    pe.matmul(bank[2 + k][:], p["mean"], sq[:, k, :], start=True, stop=True)\
                      .then_inc(s["var_done"], 1)
                for k in range(2):
                    t = 2 * i + k
                    pe.wait_ge(s["xn_ready"], 2 * i + 2)
                    pe.wait_ge(s["q_ready"], 2 * t + 1)
                    pe.matmul(bank[4][:], p["q_w"], xn[:, k, :], start=True, stop=True).then_inc(s["q_done"], 1)
                    pe.wait_ge(s["xt_ready"], t + 1)
                    for q in range(4):
                        mm = pe.transpose(bank[5][:, q * P:(q + 1) * P], xn[:, k, q * P:(q + 1) * P], p["ident"])
                    mm.then_inc(s["xt_done"], 1)
                    pe.wait_ge(s["q_ready"], 2 * t + 3)
                    pe.wait_ge(s["xt_ready"], t + 2)

                    def scores(n):
                        h, b = n // 2, n % 2
                        r = 4 * t + n
                        pe.wait_ge(s["att_ready"], r + 1 if n < 3 else r - 1)
                        for q in range(2):
                            mm = pe.matmul(bank[SB[n % 3]][:, q * HW:(q + 1) * HW],
                                           xn[:, k, (2 * b + q) * P:(2 * b + q + 1) * P],
                                           qz[:, h, b * HW:(b + 1) * HW], start=True, stop=True)
                        mm.then_inc(s["s_done"], 1)

                    def values(n):
                        h, b = n // 2, n % 2
                        pe.wait_ge(s["att_ready"], 4 * t + n + 2)
                        for q in range(2):
                            mm = pe.matmul(bank[k][C * h:C * (h + 1), b * HW:(b + 1) * HW],
                                           xt[:, (2 * b + q) * P + C * h:(2 * b + q) * P + C * (h + 1)],
                                           att[:, n % 3, q * HW:(q + 1) * HW], start=(q == 0), stop=(q == 1))
                        mm.then_inc(s["v_done"], 1)

                    scores(0)
                    scores(1)
                    for n in range(4):
                        values(n)
                        if n < 2:
                            scores(n + 2)

        @block.scalar
        def _(act):
            act.sem_inc(s["q_ready"], 1)
            act.sem_inc(s["att_ready"], 1)
            act.activation(std[:, 0, 0:1], p["ident"][:, 0:1], ACT.Sqrt).then_inc(s["warm"], 1)
            act.wait_ge(s["warm"], 1)
            act.wait_ge(s["zeroed"], 1)
            with act.Fori(0, TILES // 2) as i:
                for k in range(2):
                    act.wait_ge(s["centred"], 2 * i + k + 1)
                    act.activation(sq[:, k, :], bank[k][:], ACT.Square).then_inc(s["sq_ready"], 1)
                for k in range(2):
                    act.wait_ge(s["var_done"], 2 * i + k + 1)
                    act.activation(std[:, k, :], bank[2 + k][:], ACT.Sqrt, bias=m.eps5[:, 0:1])\
                       .then_inc(s["std_ready"], 1)
                for k in range(2):
                    t = 2 * i + k
                    act.wait_ge(s["q_done"], t + 1)
                    act.wait_ge(s["s_done"], 4 * t + 1)
                    for h in range(2):
                        r = slice(C * h, C * (h + 1))
                        act.activation(qz[r, h, :], bank[4][r, :], ACT.Copy).then_inc(s["q_ready"], 1)
                    for n in range(4):
                        act.wait_ge(s["s_done"], 4 * t + n + 2)
                        act.wait_ge(s["v_done"], 4 * t + (0 if n < 3 else n - 2) + 1)
                        act.activation(att[:, n % 3, :], bank[SB[n % 3]][:], ACT.Sigmoid).then_inc(s["att_ready"], 1)

        @block.vector
        def _(dve):
            dve.sem_inc(s["xt_ready"], 1)
            dve.sem_inc(s["out_ready"], 1)
            dve.memset(qz[:], 0.0).then_inc(s["zeroed"], 1)
            with dve.Fori(0, TILES // 2) as i:
                for k in range(2):
                    t = 2 * i + k
                    dve.wait_ge(s["std_ready"], t + 1)
                    dve.reciprocal(std[:, k, :], std[:, k, :]).then_inc(s["inv_ready"], 1)
                    dve.wait_ge(s["inv_ready"], t + 1)
                    dve.tensor_tensor(xn[:, k, :], bank[k][:], std[:, k, :], ALU.mult).then_inc(s["xn_ready"], 1)
                for k in range(2):
                    t = 2 * i + k
                    dve.wait_ge(s["xt_done"], t + 1)
                    dve.wait_ge(s["v_done"], 4 * t + 1)
                    dve.tensor_copy(xt[:], bank[5][:]).then_inc(s["xt_ready"], 1)
                    dve.wait_ge(s["v_done"], 4 * t + 5)
                    x = tile_of(m.xa, t)
                    dve.tensor_tensor(x, bank[k][:], x, ALU.add).then_inc(s["out_ready"], 1)


def route_stage(nc, m):
    p = m.par
    G = TILES * 4 * 2
    with ExitStack() as c:
        def sb(name, shape, dt=F32):
            return c.enter_context(nc.sbuf_tensor(f"ro_{name}", shape, dt))

        sem = c.enter_context(StageSemaphores(nc, "ro"))
        sq, std, xn = sb("sq", [P, 2, TW]), sb("std", [P, 2, TW]), sb("xn", [P, 2, TW])
        x1 = sb("x1", [P, 2, TW], F16)
        lg = sb("lg", [P, G, E])
        e, e2, pick = sb("e", [P, G, E]), sb("e2", [P, G, E]), sb("pick", [P, G, E])
        masks = sb("masks", [P, 2, G, E])
        top = sb("top", [P, 4, G])
        wb = sb("wb", [P, 2, 2 * E * HID])
        dt = sb("dt", [2 * E, 2, TW])
        names = ("warm centred sq_ready var_done std_ready inv_ready xn_ready x1_ready parts_ready gate_done "
                 "lg_ready exp_in e_ready step w_step d_ready dt_done dt_ready stored").split()
        s = {n: sem(n) for n in names}
        block = c.enter_context(nc.Block())
        bank = m.bank

        @block.tensor
        def _(pe):
            pe.sem_inc(s["gate_done"], 1)
            with pe.Fori(0, TILES // 2) as i:
                for k in range(2):
                    pe.wait_ge(s["xn_ready"], 2 * i + 1)
                    pe.matmul(bank[k][:], p["center"], tile_of(m.xa, 2 * i + k), start=True, stop=True)\
                      .then_inc(s["centred"], 1)
                for k in range(2):
                    pe.wait_ge(s["sq_ready"], 2 * i + k + 1)
                    pe.matmul(bank[2 + k][:], p["mean"], sq[:, k, :], start=True, stop=True)\
                      .then_inc(s["var_done"], 1)
                for k in range(2):
                    pe.wait_ge(s["xn_ready"], 2 * i + k + 2)
                    pe.wait_ge(s["lg_ready"], 2 * i + 1)
                    for q in range(4):
                        mm = pe.matmul(bank[4 + k][:, q * 2 * E:(q + 1) * 2 * E], xn[:, k, q * P:(q + 1) * P],
                                       p["gate_w"], start=True, stop=True)
                    mm.then_inc(s["gate_done"], 1)
            pe.wait_ge(s["d_ready"], 1)
            for t in range(TILES):
                if t >= 2:
                    pe.wait_ge(s["dt_ready"], t - 1)
                for q in range(4):
                    g = 2 * (4 * t + q)
                    mm = pe.transpose(bank[6 + t % 2][0:2 * E, q * P:(q + 1) * P],
                                      e2[:, g:g + 2, :].rearrange("p g e -> p (g e)"), p["ident"])
                mm.then_inc(s["dt_done"], 1)

        @block.scalar
        def _(act):
            act.activation(std[:, 0, 0:1], p["ident"][:, 0:1], ACT.Sqrt).then_inc(s["warm"], 1)
            act.wait_ge(s["warm"], 1)
            with act.Fori(0, TILES // 2) as i:
                for k in range(2):
                    act.wait_ge(s["centred"], 2 * i + k + 1)
                    act.activation(sq[:, k, :], bank[k][:], ACT.Square).then_inc(s["sq_ready"], 1)
                for k in range(2):
                    act.wait_ge(s["var_done"], 2 * i + k + 1)
                    act.activation(std[:, k, :], bank[2 + k][:], ACT.Sqrt, bias=m.eps5[:, 0:1])\
                       .then_inc(s["std_ready"], 1)
            act.wait_ge(s["exp_in"], 1)
            act.activation(e[:], lg[:], ACT.Exp).then_inc(s["e_ready"], 1)
            for t in range(TILES):
                act.wait_ge(s["dt_done"], t + 1)
                if t >= 2:
                    act.wait_ge(s["stored"], 16 * (t - 1))
                act.activation(dt[:, t % 2, :], bank[6 + t % 2][0:2 * E, :], ACT.Copy).then_inc(s["dt_ready"], 1)

        @block.sync
        def _(sp):
            for t in range(TILES):
                sp.wait_ge(s["dt_ready"], t + 1)
                if t:
                    sp.wait_ge(s["stored"], 16 * t)
                sp.dma_start(m.route[:, :, t, :].rearrange("h e n -> (h e) n"), dt[:, t % 2, :])\
                  .then_inc(s["stored"], 16)
            sp.wait_ge(s["stored"], 16 * TILES)

        @block.gpsimd
        def _(pool):
            pool.wait_ge(m.moe_landed, 32)
            n = 0

            def link(ins):
                nonlocal n
                n += 1
                ins.then_inc(s["w_step"], 1)
                pool.wait_ge(s["w_step"], n)

            link(pool.tensor_scalar(wb[:, 0, :], m.w12[:], 1.0 / XSCALE, None, ALU.mult))
            link(pool.tensor_copy(m.wp[0][:], wb[:, 0, :]))
            link(pool.tensor_tensor(wb[:, 1, :], wb[:, 0, :], m.wp[0][:], ALU.subtract))
            link(pool.tensor_copy(m.wp[1][:], wb[:, 1, :]))
            link(pool.tensor_tensor(wb[:, 0, :], wb[:, 1, :], m.wp[1][:], ALU.subtract))
            pool.tensor_copy(m.wp[2][:], wb[:, 0, :]).then_inc(s["w_step"], 1)

        @block.vector
        def _(dve):
            dve.sem_inc(s["lg_ready"], 1)
            dve.sem_inc(s["xn_ready"], 1)
            with dve.Fori(0, TILES // 2) as i:
                for k in range(2):
                    t = 2 * i + k
                    dve.wait_ge(s["std_ready"], t + 1)
                    dve.reciprocal(std[:, k, :], std[:, k, :]).then_inc(s["inv_ready"], 1)
                    dve.wait_ge(s["inv_ready"], t + 1)
                    dve.wait_ge(s["gate_done"], 2 * i + 1)
                    dve.tensor_tensor(xn[:, k, :], bank[k][:], std[:, k, :], ALU.mult).then_inc(s["xn_ready"], 1)
                for k in range(2):
                    t = 2 * i + k
                    dve.wait_ge(s["xn_ready"], t + 2)
                    dve.tensor_scalar(x1[:, k, :], xn[:, k, :], XSCALE, None, ALU.mult).then_inc(s["x1_ready"], 1)
                    dve.wait_ge(s["x1_ready"], t + 1)
                    for h in range(2):
                        r = slice(C * h, C * (h + 1))
                        o = m.xs[h][:, bass.ds(t * TW, TW)]
                        dve.tensor_copy(o[0:C, :], x1[r, k, :])
                        dve.scalar_tensor_tensor(o[C:P, :], xn[r, k, :], XSCALE, x1[r, k, :],
                                                 ALU.mult, ALU.subtract).then_inc(s["parts_ready"], 1)
                for k in range(2):
                    t = 2 * i + k
                    dve.wait_ge(s["gate_done"], t + 2)
                    dve.tensor_tensor(lg[:, bass.ds(t * 8, 8), :].rearrange("p (q h) e -> p q (h e)", h=2),
                                      bank[4 + k][:, 0:8 * E].rearrange("p (q n) -> p q n", q=4),
                                      p["gate_b"].unsqueeze(1).broadcast_to([P, 4, 2 * E]), ALU.add)\
                       .then_inc(s["lg_ready"], 1)
            count = [0]

            def link(ins):
                count[0] += 1
                ins.then_inc(s["step"], 1)
                dve.wait_ge(s["step"], count[0])

            def over(v):
                return v.unsqueeze(2).broadcast_to([P, G, E])

            idx = p["idx_w"][:, 0:E].unsqueeze(1).broadcast_to([P, G, E])
            dve.wait_ge(s["lg_ready"], TILES + 1)
            link(dve.tensor_reduce(top[:, 0, :], lg[:], AXX, ALU.max))
            dve.tensor_tensor(lg[:], lg[:], over(top[:, 0, :]), ALU.subtract).then_inc(s["exp_in"], 1)
            dve.wait_ge(s["e_ready"], 1)

            def choose(src, mask):
                link(dve.tensor_reduce(top[:, 1, :], src, AXX, ALU.max))
                link(dve.tensor_tensor(pick[:], src, over(top[:, 1, :]), ALU.is_equal))
                link(dve.tensor_tensor(pick[:], pick[:], idx, ALU.mult))
                link(dve.tensor_reduce(top[:, 2, :], pick[:], AXX, ALU.max))
                link(dve.tensor_tensor(mask, pick[:], over(top[:, 2, :]), ALU.is_equal))

            choose(e[:], masks[:, 0])
            link(dve.scalar_tensor_tensor(e2[:], masks[:, 0], -2.0, e[:], ALU.mult, ALU.add))
            choose(e2[:], masks[:, 1])
            link(dve.tensor_tensor(pick[:], masks[:, 0], masks[:, 1], ALU.add))
            link(dve.tensor_tensor(e2[:], pick[:], e[:], ALU.mult))
            link(dve.tensor_reduce(top[:, 3, :], e2[:], AXX, ALU.add))
            link(dve.reciprocal(top[:, 0, :], top[:, 3, :]))
            dve.tensor_tensor(e2[:], e2[:], over(top[:, 0, :]), ALU.mult).then_inc(s["d_ready"], 1)


def expert_stage(nc, m):
    p = m.par
    with ExitStack() as c:
        def sb(name, shape, dt=F32):
            return c.enter_context(nc.sbuf_tensor(f"ex_{name}", shape, dt))

        sem = c.enter_context(StageSemaphores(nc, "ex"))
        d = sb("d", [P, 2, E, TW])
        gated, hid = sb("gated", [P, 2, TW]), sb("hid", [P, 2, TW])
        part, acc = sb("part", [P, 2, TW]), sb("acc", [P, 2, TW])
        s = {n: sem(n) for n in ("warm", "up1_done", "up2_done", "gated_ready", "hid_ready", "down_done",
                                 "part_ready", "acc_ready")}
        d_landed = [sem(f"d_landed{k}") for k in range(2)]
        stored = [sem(f"stored{k}") for k in range(2)]
        block = c.enter_context(nc.Block())
        bank = m.bank
        N = 2 * E

        @block.sync
        def _(sp):
            od = m.out.rearrange("(h g b) c n -> g h c b n", h=2, b=2)
            sp.sem_inc(stored[0], 1)
            sp.sem_inc(stored[1], 1)
            with sp.Fori(0, TILES // 2) as i:
                for k in range(2):
                    t = 2 * i + k
                    sp.wait_ge(s["part_ready"], E * 2 * i + 2)
                    for h in range(2):
                        src = m.route[h:h + 1, :, bass.ds(t, 1), :].rearrange("h e t n -> (h t) e n")
                        sp.dma_start(d[C * h:C * (h + 1), k], src.broadcast_to([C, E, TW])).then_inc(d_landed[k], 16)
                for k in range(2):
                    t = 2 * i + k
                    sp.wait_ge(s["acc_ready"], E * (t + 1))
                    for h in range(2):
                        sp.dma_start(od[bass.ds(t, 1), h].rearrange("g c b n -> (g c) b n"),
                                     acc[C * h:C * (h + 1), k, :].rearrange("p (b n) -> p b n", b=2))\
                          .then_inc(stored[k], 16)
            for k in range(2):
                sp.wait_ge(stored[k], 32 * (TILES // 2) + 1)

        @block.tensor
        def _(pe):
            pe.sem_inc(s["down_done"], 1)
            def up(t, k, n):
                e, h = n // 2, n % 2
                x = m.xs[h][:, bass.ds(t * TW, TW)]
                for w in range(2):
                    pe.wait_ge(s["gated_ready"] if w == 0 else s["hid_ready"], N * t + n + 1)
                    for q in range(3):
                        mm = pe.matmul(bank[2 * w + n % 2][:], m.wp[q][:, (2 * e + w) * HID:(2 * e + w + 1) * HID],
                                       x, start=(q == 0), stop=(q == 2))
                    mm.then_inc(s["up1_done"] if w == 0 else s["up2_done"], 1)

            def down(t, k, n):
                e, h = n // 2, n % 2
                pe.wait_ge(s["hid_ready"], N * t + n + 3)
                if h == 0:
                    pe.wait_ge(s["part_ready"], E * t + e + 1)
                mm = pe.matmul(bank[4 + e % 2][C * h:C * (h + 1), :], m.w3[:, e * C:(e + 1) * C],
                               hid[:, n % 2, :], start=True, stop=True)
                mm.then_inc(s["down_done"], 1)

            with pe.Fori(0, TILES // 2) as i:
                for k in range(2):
                    t = 2 * i + k
                    up(t, k, 0)
                    for n in range(N):
                        if n + 1 < N:
                            up(t, k, n + 1)
                        down(t, k, n)

        @block.scalar
        def _(act):
            act.sem_inc(s["gated_ready"], 2)
            act.activation(gated[:, 0, 0:1], p["ident"][:, 0:1], ACT.Silu).then_inc(s["warm"], 1)
            act.wait_ge(s["warm"], 1)
            with act.Fori(0, TILES // 2) as i:
                for k in range(2):
                    for n in range(N):
                        r = N * (2 * i + k) + n
                        act.wait_ge(s["up1_done"], r + 1)
                        act.wait_ge(s["hid_ready"], r + 1)
                        act.activation(gated[:, n % 2, :], bank[n % 2][:], ACT.Silu).then_inc(s["gated_ready"], 1)

        @block.vector
        def _(dve):
            dve.sem_inc(s["hid_ready"], 2)
            dve.sem_inc(s["part_ready"], 2)
            with dve.Fori(0, TILES // 2) as i:
                for k in range(2):
                    t = 2 * i + k

                    def hidden(n):
                        r = N * t + n
                        dve.wait_ge(s["up2_done"], r + 1)
                        dve.wait_ge(s["gated_ready"], r + 3)
                        dve.wait_ge(s["down_done"], N * t + max(n - 1, 0) + 1)
                        dve.tensor_tensor(hid[:, n % 2, :], bank[2 + n % 2][:], gated[:, n % 2, :], ALU.mult)\
                           .then_inc(s["hid_ready"], 1)

                    def gather(e):
                        dve.wait_ge(s["down_done"], N * t + 2 * e + 3)
                        if e == 0:
                            dve.wait_ge(d_landed[k], 32 * (i + 1))
                            dve.wait_ge(stored[k], 32 * i + 1)
                        else:
                            dve.wait_ge(s["acc_ready"], E * t + e)
                        dve.tensor_tensor(part[:, e % 2, :], bank[4 + e % 2][:], d[:, k, e, :], ALU.mult)\
                           .then_inc(s["part_ready"], 1)
                        dve.wait_ge(s["part_ready"], E * t + e + 3)
                        dve.tensor_tensor(acc[:, k, :], part[:, e % 2, :],
                                          tile_of(m.xa, t) if e == 0 else acc[:, k, :], ALU.add)\
                           .then_inc(s["acc_ready"], 1)

                    for e in range(E):
                        hidden(2 * e)
                        hidden(2 * e + 1)
                        if e:
                            gather(e - 1)
                    gather(E - 1)



def param_views(m):
    views = {}
    for chunk, cols in LAYOUT.items():
        at = 0
        for name, n in cols.items():
            views[name] = m.chunk[chunk][:, at:at + n]
            at += n
    return views


def build(nc, x, dram, out):
    m = Mem()
    m.x, m.dram, m.out = x, dram, out
    with ExitStack() as c:
        m.chunk = {n: c.enter_context(nc.sbuf_tensor(f"par_{n}", [P, widths(n)], F32)) for n in LAYOUT}
        m.w12 = c.enter_context(nc.sbuf_tensor("w12", [P, 2 * E * HID], F32))
        m.w3 = c.enter_context(nc.sbuf_tensor("w3", [P, E * C], F32))
        m.xpad = c.enter_context(nc.sbuf_tensor("xpad", [P, (HB + 1) * PADI + 2 * PADW + 2], F32))
        m.xa = c.enter_context(nc.sbuf_tensor("xa", [P, COLS], F32))
        m.bank = [c.enter_context(nc.psum_tensor(f"bank{k}", [P, TW], F32)) for k in range(8)]
        m.conv0_landed = c.enter_context(nc.semaphore("conv0_landed"))
        m.attn_landed = c.enter_context(nc.semaphore("attn_landed"))
        m.rest_landed = c.enter_context(nc.semaphore("rest_landed"))
        m.moe_landed = c.enter_context(nc.semaphore("moe_landed"))
        m.par = param_views(m)
        m.eps5 = m.par["eps5"]
        conv_ffn_stage(nc, m, 0, m.xa)
        attention_stage(nc, m, m.xa)
        m.stats = c.enter_context(nc.sbuf_tensor("stats", [P, HB, 6], F32))
        conv_ffn_stage(nc, m, 1, m.xa, m.stats)
        whiten_stage(nc, m)
        slice_attention_stage(nc, m)
        lstm_stage(nc, m)
        sigmoid_attention_stage(nc, m)
        m.route = nc.dram_tensor("route", (2, E, TILES, TW), F32, kind="Internal").ap()
        m.xs = [c.enter_context(nc.sbuf_tensor(f"xs{h}", [P, COLS], F16)) for h in range(2)]
        m.wp = [c.enter_context(nc.sbuf_tensor(f"wp{q}", [P, 2 * E * HID], BF16)) for q in range(3)]
        route_stage(nc, m)
        expert_stage(nc, m)


def both(w, cols=None):
    o = np.zeros((2 * w.shape[0], 2 * w.shape[1]), w.dtype)
    o[:w.shape[0], :w.shape[1]] = w
    o[w.shape[0]:, w.shape[1]:] = w
    return o


def twice(v):
    return np.concatenate([v, v], 0)


def rows(v):
    return np.ascontiguousarray(np.broadcast_to(v[None, :], (P, v.size)))


def by_half(w):
    o = np.zeros((P, 2 * w.shape[1]), w.dtype)
    o[:C, :w.shape[1]] = w
    o[C:, w.shape[1]:] = w
    return o


def out_by_half(w):
    o = np.zeros((w.shape[0], 2 * P), w.dtype)
    o[:, :C] = w
    o[:, P + C:] = w
    return o


def padded_rows(a, n=P):
    o = np.zeros((n, a.shape[1]), a.dtype)
    o[:a.shape[0]] = a
    return o


def lay_out(v):
    f = np.float32
    q = {}
    for n in (0, 1):
        q[f"dw{n}_w"] = twice(v[f"L0_conv_dw{n}_w"].reshape(C, 9))
        q[f"dw{n}_s"] = twice(v[f"L0_conv_dw{n}_s"][:, None])
        q[f"dw{n}_b"] = twice(v[f"L0_conv_dw{n}_b"][:, None])
        q[f"f{n}_w1"] = by_half(v[f"L0_conv_f{n}_w1"][:, :, 0, 0].T)
        q[f"f{n}_s1"] = v[f"L0_conv_f{n}_s1"][:, None]
        q[f"f{n}_b1"] = v[f"L0_conv_f{n}_b1"][:, None]
        q[f"f{n}_w2"] = out_by_half(v[f"L0_conv_f{n}_w2"][:, :, 0, 0].T)
        q[f"f{n}_s2"] = twice(v[f"L0_conv_f{n}_s2"][:, None])
        q[f"f{n}_b2"] = twice(v[f"L0_conv_f{n}_b2"][:, None])
    q["wq"] = both(v["L0_conv_wq"].T)
    q["wk"] = both(v["L0_conv_wkv"][:C].T)
    q["wv"] = both(v["L0_conv_wkv"][C:].T)
    q["scale"] = rows(np.tile(v["L0_conv_scale_p"].reshape(C), 2))
    pos = np.zeros((P, P), f)
    for a in range(2):
        for h in range(2):
            pos[SLOT * a:SLOT * a + WR * WR, C * h:C * h + C] = v["L0_conv_pos"][0]
    q["pos"] = pos
    toep = np.zeros((P, HD, P), f)
    w = v["L0_conv_dwc_w"][:, 0]
    for ro in range(WR):
        for co in range(WR):
            for ky in range(5):
                for kx in range(5):
                    ri, ci = ro + ky - 2, co + kx - 2
                    if 0 <= ri < WR and 0 <= ci < WR:
                        for a in range(2):
                            toep[SLOT * a + ri * WR + ci, :, SLOT * a + ro * WR + co] = w[:, ky, kx]
    q["toep"] = toep.reshape(P, HD * P)
    q["dwc_b"] = np.tile(v["L0_conv_dwc_b"], 2 * NH)[:, None]
    q["proj"] = both(v["L0_conv_proj_w"].T)
    q["proj_b"] = twice(v["L0_conv_proj_b"][:, None])
    i = np.arange(P)
    q["ident"] = np.eye(P, dtype=f)
    q["headmask"] = (i[:, None] // HD == i[None, :] // HD).astype(f)
    q["headind"] = (i[:, None] // HD == np.arange(2 * NH)[None, :]).astype(f)
    valid = (i % SLOT < WR * WR).astype(f)
    q["slots"] = np.stack([valid * (i < SLOT), valid * (i >= SLOT)], 1).astype(f)
    same = (i[:, None] // C == i[None, :] // C).astype(f)
    q["mean"] = same / f(C)
    q["center"] = np.eye(P, dtype=f) - same / f(C)
    q["pair"] = (i[:, None] // 2 == i[None, :] // 2).astype(f) / f(2)
    q["fold"] = (i[:, None] % C == i[None, :] % C).astype(f)
    q["group16"] = q["headmask"]
    q["fc1"] = both(v["L1_conv_fc1_w"].T)
    q["ln_g"] = rows(np.tile(v["L1_conv_ln_g"], 2))
    q["ln_b"] = rows(np.tile(v["L1_conv_ln_b"], 2))
    q["fc2"] = padded_rows(both(v["L1_conv_fc2_w"].T))
    q["x_weight"] = np.repeat(v["L1_conv_x_weight"], P)[:, None]
    q["w_x"] = by_half(v["L2_attn_W_x"].T)
    q["b_x"] = v["L2_attn_b_x"][:, None]
    q["b_x_row"] = rows(np.tile(v["L2_attn_b_x"], 2))
    q["w_slice"] = heads8(v["L2_attn_W_slice"].T)
    q["b_slice"] = np.tile(v["L2_attn_b_slice"], 8)[:, None]
    q["w_temp"] = heads8(np.repeat(v["L2_attn_W_temp"].T, 16, 1))
    q["b_temp"] = np.repeat(v["L2_attn_b_temp"], P)[:, None]
    q["w_out"] = out_by_half(v["L2_attn_W_out"].T)
    q["b_out"] = twice(v["L2_attn_b_out"][:, None])
    lstm_b = np.zeros((3, P), f)
    for n, g in enumerate(("i", "c", "o")):
        q["u_" + "igo"[n]] = both(v[f"L2_ffn_U_{g}"])
        q["v_" + "igo"[n]] = both(v[f"L2_ffn_V_{g}"])
        lstm_b[n] = np.tile(v[f"L2_ffn_b_{g}"], 2)
    q["lstm_b"] = padded_rows(lstm_b)
    q["lstm_half"] = padded_rows(np.array([[0.5], [1.0], [0.5]], f))
    q["eps5"] = np.full((P, 1), 1e-5, f)
    q["gate_sel"] = padded_rows(np.tile(np.repeat(np.eye(3, dtype=f), HB, 1), (1, 8)))
    q["q_w"] = both(v["L3_attn_q_weight"])
    q["gate_w"] = both(v["L3_ffn_gate_w"])
    q["gate_b"] = rows(np.tile(v["L3_ffn_gate_b"], 2))
    q["idx_w"] = rows(np.tile(np.arange(E, 0, -1), 2).astype(f))
    arrays = {}
    for chunk, cols in LAYOUT.items():
        for name, n in cols.items():
            assert q[name].shape == (P, n), (name, q[name].shape)
        arrays[chunk] = np.concatenate([q[name] for name in cols], 1)
    w12 = np.stack([v["L3_ffn_w1"], v["L3_ffn_w2"]], 1).transpose(2, 0, 1, 3).reshape(C, 2 * E * HID)
    arrays["w12"] = twice(w12)
    arrays["w3"] = v["L3_ffn_w3"].transpose(1, 0, 2).reshape(HID, E * C)
    return {n: np.ascontiguousarray(a) for n, a in arrays.items()}


def heads8(w):
    o = np.zeros((P, P), w.dtype)
    for h in range(8):
        o[16 * h:16 * h + 16, 16 * h:16 * h + 16] = w
    return o


def kernel(**inputs):
    import concourse.bacc as bacc
    from concourse.bass_utils import run_bass_kernel_spmd

    v = {n: np.ascontiguousarray(a) for n, a in inputs.items()}
    nc = bacc.Bacc("TRN2", target_bir_lowering=False, num_devices=1)
    arrays = {"in_x": v["x"].reshape(B, C, HW)}
    arrays.update({f"in_{n}": a for n, a in lay_out(v).items()})
    aps = {n: nc.dram_tensor(n, a.shape, mybir.dt.from_np(a.dtype), kind="ExternalInput").ap()
           for n, a in arrays.items()}
    out = nc.dram_tensor("out", (B, C, HW), F32, kind="ExternalOutput").ap()
    build(nc, aps["in_x"], {n[3:]: a for n, a in aps.items() if n != "in_x"}, out)
    r = run_bass_kernel_spmd(nc, [arrays], core_ids=[0])
    return r.results[0]["out"].reshape(B, C, SIDE, SIDE)
```

```python
from contextlib import ExitStack

import numpy as np

import concourse.bass as bass
from concourse import mybir

ALU = mybir.AluOpType
ACT = mybir.ActivationFunctionType
AXX = mybir.AxisListType.X
F32 = mybir.dt.float32
F16 = mybir.dt.float16
BF16 = mybir.dt.bfloat16

P = 128
C = 64
B = 32
HB = B // 2
SIDE = 16
HW = SIDE * SIDE
COLS = HB * HW
TW = 512
TILES = COLS // TW
PADW = SIDE + 1
PADI = PADW * PADW
WR = 7
NWIN = 9
SLOT = 64
NH = 4
HD = 16
E = 16
HID = 128
SEG = [(0, 7), (7, 7), (14, 2)]
XSCALE = 2.0 ** 10

LAYOUT = {
    "conv0": dict(ident=128, dw0_w=9, dw0_s=1, dw0_b=1, f0_w1=256, f0_s1=1, f0_b1=1, f0_w2=256, f0_s2=1,
                  f0_b2=1),
    "attn": dict(wq=128, wk=128, wv=128, scale=128, pos=128, toep=16 * 128, dwc_b=1, proj=128, proj_b=1,
                 headmask=128, headind=8, slots=2),
    "rest": dict(dw1_w=9, dw1_s=1, dw1_b=1, f1_w1=256, f1_s1=1, f1_b1=1, f1_w2=256, f1_s2=1, f1_b2=1,
                 center=128, mean=128, var_rows=4 * 8, spread=4 * 128, pair=128, fold=128, group16=128, fc1=32, ln_g=32, ln_b=32, fc2=128,
                 x_weight=1, eps5=1, lstm_half=1, w_x=256, b_x=1, b_x_row=256, w_slice=128, b_slice=1, w_temp=128, b_temp=1,
                 w_out=256, b_out=1, u_i=128, u_g=128, u_o=128, v_i=128, v_g=128, v_o=128,
                 lstm_b=128, gate_sel=384, q_w=128, gate_w=32, gate_b=32, idx_w=32),
}


def widths(chunk):
    return sum(LAYOUT[chunk].values())


class StageSemaphores:

    def __init__(self, nc, prefix):
        self.nc, self.prefix, self.made = nc, prefix, []

    def __call__(self, name):
        self.made.append(self.nc.alloc_semaphore(f"{self.prefix}_{name}"))
        return self.made[-1]

    def __enter__(self):
        return self

    def __exit__(self, *_):
        self.nc.clear_and_free_semaphores(self.made)
        self.nc.all_engine_barrier()


class Mem:
    pass


def tile_of(ap, t):
    return ap[:, bass.ds(t * TW, TW)]


def padded(ap, t, dy, dx):
    off = (1 + dy) * PADW + 1 + dx
    v = ap[:, bass.ds(t * (2 * PADI) + off, 2 * PADI)]
    return v.rearrange("p (a r c) -> p a r c", a=2, r=PADW)[:, :, 0:SIDE, 0:SIDE]


def conv_ffn_stage(nc, m, layer, out, stats=None):
    p = m.par
    dw_w, dw_s, dw_b = (p[f"dw{layer}_{n}"] for n in "wsb")
    w1, s1, b1 = (p[f"f{layer}_{n}"] for n in ("w1", "s1", "b1"))
    w2, s2, b2 = (p[f"f{layer}_{n}"] for n in ("w2", "s2", "b2"))
    with ExitStack() as c:
        def sb(name, shape, dt=F32):
            return c.enter_context(nc.sbuf_tensor(f"L{layer}_{name}", shape, dt))

        sem = c.enter_context(StageSemaphores(nc, f"L{layer}"))

        taps = sb("taps", [P, 9])
        diag = sb("diag", [P, 9, P])
        y = sb("y", [P, 2, TW])
        hid = sb("hid", [P, 2, 2, TW])
        branch = sb("branch", [P, 2, TW])
        if layer == 0:
            xin = sb("xin", [P, COLS])
        taps_ready, diag_ready = sem("taps_ready"), sem("diag_ready")
        x_landed = [sem(f"x_landed{g}") for g in range(4)]
        pad_zeroed, pad_ready = sem("pad_zeroed"), sem("pad_ready")
        conv_done, y_ready, up_done, hid_ready = sem("conv_done"), sem("y_ready"), sem("up_done"), sem("hid_ready")
        down_done, branch_ready, out_ready, stat_ready = (sem("down_done"), sem("branch_ready"),
                                                          sem("out_ready"), sem("stat_ready"))
        block = c.enter_context(nc.Block())

        if layer == 0:
            @block.sync
            def _(sp):
                xd = m.x.rearrange("(h g b) c n -> g h c b n", h=2, b=4)
                for g in range(4):
                    if g == 0:
                        sp.dma_start(m.chunk["conv0"][:], m.dram["conv0"]).then_inc(m.conv0_landed, 16)
                    for h in range(2):
                        sp.dma_start(xin[C * h:C * h + C, g * 1024:(g + 1) * 1024].rearrange(
                            "p (b n) -> p b n", b=4), xd[g, h]).then_inc(x_landed[g], 16)
                for name, s in (("attn", m.attn_landed), ("rest", m.rest_landed)):
                    sp.dma_start(m.chunk[name][:], m.dram[name]).then_inc(s, 16)
                sp.dma_start(m.w12[:], m.dram["w12"]).then_inc(m.moe_landed, 16)
                sp.dma_start(m.w3[:], m.dram["w3"]).then_inc(m.moe_landed, 16)

        @block.gpsimd
        def _(pool):
            if layer == 0:
                pool.memset(m.xpad[:], 0.0).then_inc(pad_zeroed, 1)
                pool.wait_ge(pad_zeroed, 1)
                for g in range(4):
                    pool.wait_ge(x_landed[g], 32)
                    for a in range(2):
                        pool.tensor_copy(padded(m.xpad, 2 * g + a, 0, 0),
                                         xin[:, (2 * g + a) * TW:(2 * g + a + 1) * TW].rearrange(
                                             "p (a r c) -> p a r c", a=2, r=SIDE)).then_inc(pad_ready, 1)

        @block.tensor
        def _(pe):
            pe.wait_ge(diag_ready, 9)
            with pe.Fori(0, TILES // 2) as i:
                for k in range(2):
                    t = 2 * i + k
                    if layer == 0:
                        pe.wait_ge(pad_ready, t + 1)
                    pe.wait_ge(y_ready, t + 1)
                    for q in range(9):
                        mm = pe.matmul(m.bank[k][:], diag[:, q, :], padded(m.xpad, t, q // 3 - 1, q % 3 - 1),
                                       start=(q == 0), stop=(q == 8))
                    mm.then_inc(conv_done, 1)
                for k in range(2):
                    t = 2 * i + k
                    pe.wait_ge(y_ready, t + 3)
                    for h in range(2):
                        pe.wait_ge(hid_ready, 2 * t + h + 1)
                        pe.matmul(m.bank[2 + 2 * k + h][:], w1[:, h * HID:(h + 1) * HID], y[:, k, :],
                                  start=True, stop=True).then_inc(up_done, 1)
                for k in range(2):
                    t = 2 * i + k
                    pe.wait_ge(branch_ready, t + 1)
                    for h in range(2):
                        pe.wait_ge(hid_ready, 2 * t + h + 5)
                        mm = pe.matmul(m.bank[6 + k][:], w2[:, h * P:(h + 1) * P], hid[:, k, h, :],
                                       start=(h == 0), stop=(h == 1))
                    mm.then_inc(down_done, 1)

        @block.scalar
        def _(act):
            act.sem_inc(y_ready, 2)
            act.sem_inc(hid_ready, 4)
            act.sem_inc(branch_ready, 2)
            if layer == 0:
                act.wait_ge(m.conv0_landed, 16)
            else:
                act.wait_ge(m.rest_landed, 16)
            with act.Fori(0, TILES // 2) as i:
                for k in range(2):
                    t = 2 * i + k
                    act.wait_ge(out_ready, t + 1)
                    act.wait_ge(conv_done, t + 1)
                    act.activation(y[:, k, :], m.bank[k][:], ACT.Identity, bias=dw_b[:, 0:1]).then_inc(y_ready, 1)
                for k in range(2):
                    t = 2 * i + k
                    for h in range(2):
                        act.wait_ge(up_done, 2 * t + h + 1)
                        act.activation(hid[:, k, h, :], m.bank[2 + 2 * k + h][:], ACT.Relu, bias=b1[:, 0:1],
                                       scale=s1[:, 0:1]).then_inc(hid_ready, 1)
                for k in range(2):
                    t = 2 * i + k
                    act.wait_ge(down_done, t + 1)
                    act.activation(branch[:, k, :], m.bank[6 + k][:], ACT.Identity, bias=b2[:, 0:1],
                                   scale=s2[:, 0:1]).then_inc(branch_ready, 1)

        @block.vector
        def _(dve):
            dve.sem_inc(out_ready, 2)
            if layer == 0:
                dve.wait_ge(m.conv0_landed, 16)
            else:
                dve.wait_ge(m.rest_landed, 16)
            dve.tensor_scalar(taps[:], dw_w, dw_s[:, 0:1], None, ALU.mult).then_inc(taps_ready, 1)
            dve.wait_ge(taps_ready, 1)
            dve.tensor_scalar(taps[:, 4:5], taps[:, 4:5], 1.0, None, ALU.add).then_inc(taps_ready, 1)
            dve.wait_ge(taps_ready, 2)
            for q in range(9):
                dve.tensor_scalar(diag[:, q, :], p["ident"], taps[:, q:q + 1], None, ALU.mult)\
                   .then_inc(diag_ready, 1)
            if layer == 1:
                dve.wait_ge(m.moe_landed, 32)
                dve.tensor_reduce(m.wrange[:, 0:1], m.w12[:], AXX, ALU.max)
                dve.tensor_reduce(m.wrange[:, 1:2], m.w12[:], AXX, ALU.min)
            with dve.Fori(0, TILES // 2) as i:
                for k in range(2):
                    t = 2 * i + k
                    dve.wait_ge(y_ready, t + 3)
                    dve.wait_ge(branch_ready, t + 3)
                    dve.tensor_tensor(tile_of(out, t), branch[:, k, :], y[:, k, :], ALU.add).then_inc(out_ready, 1)
                    if stats is not None:
                        dve.wait_ge(out_ready, t + 3)
                        for a in range(2):
                            dve.bn_stats(stats[:, bass.ds(t * 2 + a, 1), :],
                                         out[:, bass.ds(t * TW + a * HW, HW)]).then_inc(stat_ready, 1)


def region(ap3, wi, wj, windowed):
    (r0, nr), (c0, ncol) = SEG[wi], SEG[wj]
    if windowed:
        v = ap3.rearrange("p (a s) -> p a s", a=2)[:, :, 0:WR * WR].rearrange("p a (r c) -> p a r c", r=WR)
        return v[:, :, 0:nr, 0:ncol]
    return ap3.rearrange("p (a r c) -> p a r c", a=2, r=SIDE)[:, :, r0:r0 + nr, c0:c0 + ncol]


def attention_stage(nc, m, x2):
    p = m.par
    U = 2 * NWIN
    UW = U * P
    KVW = 2 * P + 2
    YW = P + 2 * NH
    with ExitStack() as c:
        def sb(name, shape, dt=F32):
            return c.enter_context(nc.sbuf_tensor(f"att_{name}", shape, dt))

        sem = c.enter_context(StageSemaphores(nc, "att"))

        sc = sb("sc", [P, 4, P])
        inv_sc = sb("inv_sc", [P, P])
        wq, wk, pos, floor = sb("wq", [P, P]), sb("wk", [P, P]), sb("pos", [P, P]), sb("floor", [P, P])
        bias = sb("bias", [P, 1])
        xw = sb("xw", [P, U, P])
        base = sb("base", [P, 2, 3 * P])
        sqa, cube, sqb = sb("sqa", [P, 2, 3 * P]), sb("cube", [P, 2, 3 * P]), sb("sqb", [P, 2, 3 * P])
        norms, roots, factor = sb("norms", [P, 2, 12]), sb("roots", [P, 2, 12]), sb("factor", [P, 2, 12])
        kq = sb("kq", [P, 2, 2, 3 * P])
        val = sb("val", [P, U, P])
        valz = sb("valz", [P, U, KVW + 2])
        kvm = sb("kvm", [P, 2, 2, YW])
        qt = sb("qt", [P, 2, P])
        den = sb("den", [P, 2, 3, 2 * NH])
        ysum = sb("ysum", [P, U, P])
        yt = sb("yt", [P, UW])
        proj = sb("proj", [P, UW])
        names = ("ready0 act_ready0 zeroed ind xw_ready qkv_done base_ready sqa_ready cube_ready s2_ready "
                 "sqb_ready s6_ready root_ready inv_ready factor_ready kq_ready v_ready kv_done kvm_ready "
                 "qt_done qt_ready y_done den_ready ysum_ready conv_done conv_added yt_done yt_ready proj_done "
                 "proj_ready out_ready").split()
        s = {n: sem(n) for n in names}
        block = c.enter_context(nc.Block())
        bank = m.bank
        conv_bank = [0, 1, 2, 5]
        chunks = [(0, 4), (4, 4), (8, 4), (12, 4), (16, 2)]
        yt_bank, proj_bank = [0, 1, 2, 5, 3], [4, 6, 7, 4, 6]

        @block.gpsimd
        def _(pool):
            pool.sem_inc(s["out_ready"], 1)
            pool.memset(xw[:], 0.0).then_inc(s["zeroed"], 1)
            pool.memset(valz[:], 0.0).then_inc(s["zeroed"], 1)
            pool.wait_ge(s["zeroed"], 2)
            pool.wait_ge(m.attn_landed, 16)
            for u in range(U):
                pool.tensor_copy(valz[:, u, 2 * P:KVW], p["slots"]).then_inc(s["ind"], 1)
            with pool.Fori(0, TILES // 2) as i:
                pool.wait_ge(s["qkv_done"], 6 * i + 1)
                for u in range(U):
                    k, w = u // NWIN, u % NWIN
                    pool.tensor_copy(region(xw[:, u, :], w // 3, w % 3, True),
                                     region(tile_of(x2, 2 * i + k), w // 3, w % 3, False))\
                        .then_inc(s["xw_ready"], 1)
                pool.wait_ge(s["proj_ready"], 5 * i + 6)
                for u in range(U):
                    k, w = u // NWIN, u % NWIN
                    (r0, nr), (c0, ncol) = SEG[w // 3], SEG[w % 3]
                    pool.tensor_tensor(padded(m.xpad, 2 * i + k, 0, 0)[:, :, r0:r0 + nr, c0:c0 + ncol],
                                       region(proj[:, u * P:(u + 1) * P], w // 3, w % 3, True),
                                       region(tile_of(x2, 2 * i + k), w // 3, w % 3, False), ALU.add)\
                        .then_inc(s["out_ready"], 1)

        @block.tensor
        def _(pe):
            pe.sem_inc(s["yt_done"], 1)
            pe.sem_inc(s["qt_done"], 1)
            pe.sem_inc(s["y_done"], 1)
            pe.sem_inc(s["kv_done"], 1)
            pe.sem_inc(s["conv_done"], 1)
            pe.sem_inc(s["qkv_done"], 1)
            def qkv(i, g):
                pe.wait_ge(s["xw_ready"], U * i + 3 * g + 3)
                pe.wait_ge(s["base_ready"], 6 * i + g + 1)
                pe.wait_ge(s["v_ready"], 6 * i + g + 1)
                for u in range(3):
                    x = xw[:, 3 * g + u, :]
                    o = slice(u * P, (u + 1) * P)
                    pe.matmul(bank[0][:, o], x, wk[:], start=True, stop=True)
                    pe.matmul(bank[1][:, o], x, wq[:], start=True, stop=True)
                    mm = pe.matmul(bank[2][:, o], x, p["wv"], start=True, stop=True)
                mm.then_inc(s["qkv_done"], 1)

            def kv_and_turn(i, n):
                g, u = n // 3, n % 3
                pe.wait_ge(s["kq_ready"], 6 * i + g + 1)
                pe.wait_ge(s["kvm_ready"], U * i + n + 1)
                pe.matmul(bank[3 + n % 2][:, 0:KVW], kq[:, g % 2, 0, u * P:(u + 1) * P], valz[:, n, 0:KVW],
                          start=True, stop=True).then_inc(s["kv_done"], 1)
                pe.wait_ge(s["qt_ready"], U * i + n + 1)
                pe.transpose(bank[5][:, 0:P], kq[:, g % 2, 1, u * P:(u + 1) * P], p["ident"])\
                  .then_inc(s["qt_done"], 1)

            def attend(i, n):
                pe.wait_ge(s["kvm_ready"], U * i + n + 3)
                pe.wait_ge(s["qt_ready"], U * i + n + 2)
                if n % 3 == 0:
                    pe.wait_ge(s["ysum_ready"], 6 * i + n // 3 + 1)
                for a in range(2):
                    o = bank[6][SLOT * a:SLOT * (a + 1), (n % 3) * YW:(n % 3 + 1) * YW]
                    mm = pe.matmul(o, qt[:, n % 2, SLOT * a:SLOT * (a + 1)], kvm[:, n % 2, a, :],
                                   start=True, stop=True)
                mm.then_inc(s["y_done"], 1)

            pe.wait_ge(s["inv_ready"], 4)
            pe.wait_ge(m.attn_landed, 16)
            pe.matmul(bank[7][:, 0:1], p["proj"], p["dwc_b"], start=True, stop=True).then_inc(s["ready0"], 1)
            pe.wait_ge(s["ind"], U)
            pe.wait_ge(s["act_ready0"], 5)
            with pe.Fori(0, TILES // 2) as i:
                pe.wait_ge(s["proj_ready"], 5 * i + 1)
                qkv(i, 0)
                for g in range(6):
                    if g < 5:
                        qkv(i, g + 1)
                    else:
                        pe.wait_ge(s["v_ready"], 6 * i + 7)
                    for u in range(3):
                        kv_and_turn(i, 3 * g + u)
                        if u:
                            attend(i, 3 * g + u - 1)
                    attend(i, 3 * g + 2)
                pe.wait_ge(s["base_ready"], 6 * i + 7)
                pe.wait_ge(s["qt_ready"], U * i + U + 1)
                for dg in range(HD // 2):
                    pe.wait_ge(s["conv_added"], 8 * i + dg + 1)
                    for e in range(2):
                        d = 2 * dg + e
                        rhs = val[:].rearrange("p u (n d) -> p (u n) d", d=HD)[:, :, d]
                        mm = pe.matmul(bank[conv_bank[dg % 4]][:, e * 144:(e + 1) * 144],
                                       p["toep"][:, d * P:(d + 1) * P], rhs, start=True, stop=True)
                    mm.then_inc(s["conv_done"], 1)
                pe.wait_ge(s["conv_added"], 8 * i + 8 + 4)
                pe.wait_ge(s["kvm_ready"], U * i + U + 2)
                for j, (u0, nu) in enumerate(chunks):
                    for u in range(nu):
                        mm = pe.transpose(bank[yt_bank[j]][:, u * P:(u + 1) * P], ysum[:, u0 + u, :], p["ident"])
                    mm.then_inc(s["yt_done"], 1)
                pe.wait_ge(s["ysum_ready"], 6 * i + 7)
                for j, (u0, nu) in enumerate(chunks):
                    pe.wait_ge(s["yt_ready"], 5 * i + j + 1)
                    if j >= 3:
                        pe.wait_ge(s["proj_ready"], 5 * i + j - 1)
                    pe.matmul(bank[proj_bank[j]][:, 0:nu * P], p["proj"], yt[:, u0 * P:(u0 + nu) * P],
                              start=True, stop=True).then_inc(s["proj_done"], 1)

        @block.scalar
        def _(act):
            act.sem_inc(s["proj_ready"], 1)
            act.sem_inc(s["v_ready"], 1)
            act.sem_inc(s["qt_ready"], 1)
            act.wait_ge(m.attn_landed, 16)
            act.activation(sc[:, 0, :], p["scale"], ACT.Abs).then_inc(s["act_ready0"], 1)
            act.wait_ge(s["act_ready0"], 1)
            act.activation(sc[:, 1, :], sc[:, 0, :], ACT.Exp, scale=-1.0).then_inc(s["act_ready0"], 1)
            act.wait_ge(s["act_ready0"], 2)
            act.activation(sc[:, 2, :], sc[:, 1, :], ACT.Ln, bias=1.0).then_inc(s["act_ready0"], 1)
            act.activation(sc[:, 3, :], p["scale"], ACT.Relu).then_inc(s["act_ready0"], 1)
            act.wait_ge(s["ready0"], 1)
            act.activation(bias[:], bank[7][:, 0:1], ACT.Identity, bias=p["proj_b"][:, 0:1])\
               .then_inc(s["act_ready0"], 1)
            act.activation(sc[:, 0, 0:1], sc[:, 3, 0:1], ACT.Sqrt).then_inc(s["act_ready0"], 1)
            act.wait_ge(s["act_ready0"], 6)

            def values(i, g):
                act.wait_ge(s["qkv_done"], 6 * i + g + 2)
                if g == 0:
                    act.wait_ge(s["conv_done"], 8 * i + 1)
                    act.wait_ge(s["kv_done"], U * i + 1)
                v3 = bank[2][:, 0:3 * P].rearrange("p (u n) -> p u n", u=3)
                act.activation(val[:, 3 * g:3 * g + 3, :], v3, ACT.Copy)
                act.activation(valz[0:SLOT, 3 * g:3 * g + 3, 0:P], v3[0:SLOT], ACT.Copy)
                act.activation(valz[SLOT:P, 3 * g:3 * g + 3, P:2 * P], v3[SLOT:P], ACT.Copy)\
                   .then_inc(s["v_ready"], 1)

            def turned(i, n):
                act.wait_ge(s["qt_done"], U * i + n + 2)
                act.wait_ge(s["y_done"], U * i + n + 1)
                act.activation(qt[:, n % 2, :], bank[5][:, 0:P], ACT.Copy).then_inc(s["qt_ready"], 1)

            def square_base(i, g):
                act.wait_ge(s["base_ready"], 6 * i + g + 2)
                act.activation(sqa[:], base[:], ACT.Square).then_inc(s["sqa_ready"], 1)

            def square_cube(i, g):
                act.wait_ge(s["cube_ready"], 6 * i + g + 1)
                act.activation(sqb[:], cube[:], ACT.Square).then_inc(s["sqb_ready"], 1)

            def root(i, g):
                act.wait_ge(s["s2_ready"], 6 * i + g + 1)
                act.wait_ge(s["s6_ready"], 6 * i + g + 1)
                act.activation(roots[:], norms[:], ACT.Sqrt).then_inc(s["root_ready"], 1)

            act.wait_ge(s["ind"], U)
            with act.Fori(0, TILES // 2) as i:
                values(i, 0)
                square_base(i, 0)
                square_cube(i, 0)
                root(i, 0)
                for g in range(6):
                    if g < 5:
                        values(i, g + 1)
                        square_base(i, g + 1)
                    turned(i, 3 * g)
                    if g < 5:
                        square_cube(i, g + 1)
                    turned(i, 3 * g + 1)
                    if g < 5:
                        root(i, g + 1)
                    turned(i, 3 * g + 2)
                for j, (u0, nu) in enumerate(chunks):
                    act.wait_ge(s["yt_done"], 5 * i + j + 2)
                    act.activation(yt[:, u0 * P:(u0 + nu) * P], bank[yt_bank[j]][:, 0:nu * P], ACT.Copy)\
                       .then_inc(s["yt_ready"], 1)
                act.wait_ge(s["out_ready"], U * i + 1)
                for j, (u0, nu) in enumerate(chunks):
                    act.wait_ge(s["proj_done"], 5 * i + j + 1)
                    act.activation(proj[:, u0 * P:(u0 + nu) * P], bank[proj_bank[j]][:, 0:nu * P], ACT.Identity,
                                   bias=bias[:, 0:1]).then_inc(s["proj_ready"], 1)

        @block.vector
        def _(dve):
            dve.sem_inc(s["base_ready"], 1)
            dve.sem_inc(s["kvm_ready"], 2)
            dve.sem_inc(s["ysum_ready"], 1)
            dve.sem_inc(s["conv_added"], 4)
            dve.wait_ge(s["act_ready0"], 4)
            dve.tensor_tensor(inv_sc[:], sc[:, 2, :], sc[:, 3, :], ALU.add).then_inc(s["inv_ready"], 1)
            dve.wait_ge(s["inv_ready"], 1)
            dve.reciprocal(inv_sc[:], inv_sc[:]).then_inc(s["inv_ready"], 1)
            dve.wait_ge(s["inv_ready"], 2)
            dve.tensor_tensor(wq[:], p["wq"], inv_sc[:], ALU.mult)
            dve.tensor_tensor(wk[:], p["wk"], inv_sc[:], ALU.mult)
            dve.tensor_tensor(pos[:], p["pos"], inv_sc[:], ALU.mult).then_inc(s["inv_ready"], 1)
            dve.tensor_scalar(floor[:], inv_sc[:], 1e-6, None, ALU.mult).then_inc(s["inv_ready"], 1)
            dve.wait_ge(s["inv_ready"], 4)

            def over3(ap):
                return ap.unsqueeze(1).broadcast_to([P, 3, P])

            def grouped(ap):
                return ap.rearrange("p z (n c) -> p (z n) c", c=C)

            def base_of(i, g):
                dve.wait_ge(s["qkv_done"], 6 * i + g + 2)
                kps = bank[0][:, 0:3 * P].rearrange("p (u n) -> p u n", u=3)
                qps = bank[1][:, 0:3 * P].rearrange("p (u n) -> p u n", u=3)
                b = base[:].rearrange("p z (u n) -> p z u n", u=3)
                dve.tensor_tensor(b[:, 0], kps, over3(pos[:]), ALU.add).then_inc(s["inv_ready"], 1)
                dve.scalar_tensor_tensor(b[:, 1], qps, 0.0, over3(floor[:]), ALU.max, ALU.add)
                dve.wait_ge(s["inv_ready"], 6 * i + g + 5)
                dve.scalar_tensor_tensor(b[:, 0], b[:, 0], 0.0, over3(floor[:]), ALU.max, ALU.add)\
                   .then_inc(s["base_ready"], 1)

            def cube_of(i, g):
                dve.wait_ge(s["sqa_ready"], 6 * i + g + 1)
                dve.wait_ge(s["base_ready"], 6 * i + g + 2)
                dve.tensor_tensor(cube[:], sqa[:], base[:], ALU.mult).then_inc(s["cube_ready"], 1)
                dve.tensor_reduce(norms[:, 0, :], grouped(sqa[:]), AXX, ALU.add).then_inc(s["s2_ready"], 1)

            def sum6(i, g):
                dve.wait_ge(s["sqb_ready"], 6 * i + g + 1)
                dve.tensor_reduce(norms[:, 1, :], grouped(sqb[:]), AXX, ALU.add).then_inc(s["s6_ready"], 1)

            def normalise(i, g):
                dve.wait_ge(s["root_ready"], 6 * i + g + 1)
                dve.reciprocal(factor[:, 0, :], roots[:, 1, :]).then_inc(s["factor_ready"], 1)
                dve.wait_ge(s["factor_ready"], 12 * i + 2 * g + 1)
                dve.tensor_tensor(factor[:, 1, :], roots[:, 0, :], factor[:, 0, :], ALU.mult)\
                   .then_inc(s["factor_ready"], 1)
                dve.wait_ge(s["factor_ready"], 12 * i + 2 * g + 2)
                if g >= 2:
                    dve.wait_ge(s["qt_done"], U * i + 3 * (g - 1) + 1)
                else:
                    dve.wait_ge(s["qt_done"], U * i + 1)
                dve.tensor_tensor(grouped(kq[:, g % 2]), grouped(cube[:]),
                                  factor[:, 1, :].unsqueeze(2).broadcast_to([P, 12, C]), ALU.mult)\
                   .then_inc(s["kq_ready"], 1)

            def mask_kv(i, n):
                dve.wait_ge(s["kv_done"], U * i + n + 2)
                dve.wait_ge(s["y_done"], U * i + max(n - 1, 0) + 1)
                b = bank[3 + n % 2]
                dve.tensor_tensor(kvm[:, n % 2, :, 0:P], b[:, 0:2 * P].rearrange("p (a n) -> p a n", a=2),
                                  p["headmask"].unsqueeze(1).broadcast_to([P, 2, P]), ALU.mult)
                dve.tensor_tensor(kvm[:, n % 2, :, P:YW],
                                  b[:, 2 * P:KVW].unsqueeze(2).broadcast_to([P, 2, 2 * NH]),
                                  p["headind"].unsqueeze(1).broadcast_to([P, 2, 2 * NH]), ALU.mult)\
                   .then_inc(s["kvm_ready"], 1)

            def divide(i, g):
                dve.wait_ge(s["y_done"], U * i + 3 * g + 4)
                ps = bank[6][:, 0:3 * YW].rearrange("p (u n) -> p u n", u=3)
                dve.tensor_scalar(den[:, 0], ps[:, :, P:YW], 1e-6, None, ALU.add).then_inc(s["den_ready"], 1)
                dve.wait_ge(s["den_ready"], 12 * i + 2 * g + 1)
                dve.reciprocal(den[:, 1], den[:, 0]).then_inc(s["den_ready"], 1)
                dve.wait_ge(s["den_ready"], 12 * i + 2 * g + 2)
                if g == 0:
                    dve.wait_ge(s["yt_done"], 5 * i + 1)
                dve.tensor_tensor(ysum[:, 3 * g:3 * g + 3, :].rearrange("p u (n d) -> p u n d", d=HD),
                                  ps[:, :, 0:P].rearrange("p u (n d) -> p u n d", d=HD),
                                  den[:, 1].unsqueeze(3).broadcast_to([P, 3, 2 * NH, HD]), ALU.mult)\
                   .then_inc(s["ysum_ready"], 1)

            with dve.Fori(0, TILES // 2) as i:
                base_of(i, 0)
                cube_of(i, 0)
                sum6(i, 0)
                normalise(i, 0)
                for g in range(6):
                    if g < 5:
                        base_of(i, g + 1)
                    mask_kv(i, 3 * g)
                    if g < 5:
                        cube_of(i, g + 1)
                    mask_kv(i, 3 * g + 1)
                    if g < 5:
                        sum6(i, g + 1)
                    mask_kv(i, 3 * g + 2)
                    if g < 5:
                        normalise(i, g + 1)
                    divide(i, g)
                dve.wait_ge(s["ysum_ready"], 6 * i + 7)
                for dg in range(HD // 2):
                    dve.wait_ge(s["conv_done"], 8 * i + dg + 2)
                    y = ysum[:].rearrange("p u (n d) -> p d (u n)", d=HD)[:, 2 * dg:2 * dg + 2, :]
                    dve.tensor_tensor(y, y, bank[conv_bank[dg % 4]][:, 0:288].rearrange("p (e n) -> p e n", e=2),
                                      ALU.add).then_inc(s["conv_added"], 1)


def weight_scale_stage(nc, m):
    p = m.par
    with ExitStack() as c:
        sem = c.enter_context(StageSemaphores(nc, "ws"))
        top = c.enter_context(nc.sbuf_tensor("ws_top", [P, 4], F32))
        ones = c.enter_context(nc.sbuf_tensor("ws_ones", [1, P], F32))
        step, turned, spread = sem("step"), sem("turned"), sem("spread")
        block = c.enter_context(nc.Block())

        @block.tensor
        def _(pe):
            pe.wait_ge(step, 3)
            pe.transpose(m.bank[0][0:1, 0:P], top[:, 1:2], p["ident"]).then_inc(turned, 1)
            pe.wait_ge(step, 5)
            pe.matmul(m.bank[1][:, 0:1], ones[:], top[0:1, 3:4], start=True, stop=True).then_inc(spread, 1)

        @block.vector
        def _(dve):
            dve.wait_ge(m.moe_landed, 32)
            dve.memset(ones[:], 1.0).then_inc(step, 1)
            dve.tensor_scalar(top[:, 0:1], m.wrange[:, 1:2], -1.0, None, ALU.mult).then_inc(step, 1)
            dve.wait_ge(step, 2)
            dve.tensor_tensor(top[:, 1:2], top[:, 0:1], m.wrange[:, 0:1], ALU.max).then_inc(step, 1)
            dve.wait_ge(turned, 1)
            dve.tensor_reduce(top[0:1, 2:3], m.bank[0][0:1, 0:P], AXX, ALU.max).then_inc(step, 1)
            dve.wait_ge(step, 4)
            dve.tensor_scalar(top[0:1, 3:4], top[0:1, 2:3], 1e-30, None, ALU.max).then_inc(step, 1)
            dve.wait_ge(spread, 1)
            dve.tensor_copy(m.wscale[:], m.bank[1][:, 0:1]).then_inc(step, 1)
            dve.wait_ge(step, 6)
            bits = m.wscale[:].bitcast(mybir.dt.int32)
            dve.tensor_scalar(bits, bits, 0x7F800000, None, ALU.bitwise_and).then_inc(step, 1)
            dve.wait_ge(step, 7)
            dve.tensor_scalar(m.unscale[:], m.wscale[:], 2.0 ** -12 / XSCALE, None, ALU.mult).then_inc(step, 1)
            dve.reciprocal(top[:, 0:1], m.wscale[:]).then_inc(step, 1)
            dve.wait_ge(step, 9)
            dve.tensor_scalar(m.wscale[:], top[:, 0:1], 2.0 ** 12, None, ALU.mult).then_inc(step, 1)


def whiten_stage(nc, m):
    p = m.par
    with ExitStack() as c:
        def sb(name, shape, dt=F32):
            return c.enter_context(nc.sbuf_tensor(f"wh_{name}", shape, dt))

        sem = c.enter_context(StageSemaphores(nc, "wh"))

        mv = sb("mv", [P, HB, 2])
        st = sb("st", [P, 2, HB])
        gst = sb("gst", [P, 2, HB])
        gvar, a, b, bc, xv, tmp = (sb(n, [P, HB]) for n in ("gvar", "a", "b", "bc", "xv", "tmp"))
        sums = sb("sums", [P, 4])
        scal = sb("scal", [P, 8])
        h = sb("h", [HB, 8, 2 * HD])
        hs = sb("hs", [HB, 4, 2])
        hT = sb("hT", [2 * HD, HB])
        gate = sb("gate", [P, HB])
        xc = sb("xc", [P, 2, TW])
        xt = sb("xt", [P, 2, TW])
        zero = sb("zero", [P, P])
        gram = sb("gram", [P, P])
        half = sb("half", [P, C])
        sigma = sb("sigma", [P, P])
        pw = sb("pw", [P, 4, P])
        wP = sb("wP", [P, P])
        ga, bias = sb("ga", [P, HB]), sb("bias", [P, HB])
        mat = sb("mat", [P, 4, P])
        names = ("dve_step act_step st_ready pair_done var_ready std_ready sums_ready fold_done mu_ready xm_done "
                 "xv_ready fc1_done hvar_ready hstd_ready hrelu_ready turn_done ht_ready fc2_done sig_ready "
                 "centre_ready xc_ready xt_done xt_ready gram_done tile_gram mask_ready folded trace_in trace_done "
                 "sig_mat prod_done pw_ready wp_ready wb_done b_ready scaled mat_ready app_done out_ready "
                 "scale_in scale_ready").split()
        s = {n: sem(n) for n in names}
        block = c.enter_context(nc.Block())
        bank = m.bank

        @block.tensor
        def _(pe):
            pe.sem_inc(s["app_done"], 1)
            pe.sem_inc(s["tile_gram"], 1)
            pe.sem_inc(s["xt_done"], 1)
            pe.wait_ge(s["st_ready"], 1)
            pe.matmul(bank[0][:, 0:2 * HB], p["pair"], st[:], start=True, stop=True).then_inc(s["pair_done"], 1)
            pe.wait_ge(s["sums_ready"], 1)
            pe.matmul(bank[1][:, 0:2], p["fold"], sums[:, 0:2], start=True, stop=True).then_inc(s["fold_done"], 1)
            pe.matmul(bank[2][0:HB, 0:2 * HD], xv[:], p["fc1"], start=True, stop=True).then_inc(s["fc1_done"], 1)
            pe.wait_ge(s["mu_ready"], 1)
            pe.matmul(bank[3][:, 0:1], p["mean"], sums[:, 3:4], start=True, stop=True).then_inc(s["xm_done"], 1)
            pe.wait_ge(s["hrelu_ready"], 1)
            pe.transpose(bank[2][0:2 * HD, 0:HB], h[:, 7, :], p["ident"][0:HB, 0:HB]).then_inc(s["turn_done"], 1)
            pe.wait_ge(s["ht_ready"], 1)
            pe.matmul(bank[4][:, 0:HB], p["fc2"][0:2 * HD, :], hT[:], start=True, stop=True)\
              .then_inc(s["fc2_done"], 1)
            pe.matmul(bank[7][:, 0:P], zero[:], zero[:], start=True, stop=False, skip_group_check=True)
            with pe.Fori(0, TILES // 2) as i:
                for k in range(2):
                    t = 2 * i + k
                    pe.wait_ge(s["xc_ready"], 2 * t + 2 + 4)
                    pe.wait_ge(s["xt_ready"], t + 1)
                    for q in range(4):
                        mm = pe.transpose(bank[5 + k][:, q * P:(q + 1) * P], xc[:, k, q * P:(q + 1) * P], p["ident"])
                    mm.then_inc(s["xt_done"], 1)
                for k in range(2):
                    t = 2 * i + k
                    pe.wait_ge(s["xt_ready"], t + 3)
                    for q in range(4):
                        o = xt[:, k, q * P:(q + 1) * P]
                        mm = pe.matmul(bank[7][:, 0:P], o, o, start=False, stop=False, skip_group_check=True)
                    mm.then_inc(s["tile_gram"], 1)
            pe.matmul(bank[7][:, 0:P], zero[:], zero[:], start=False, stop=True, skip_group_check=True)\
              .then_inc(s["gram_done"], 1)
            pe.wait_ge(s["mask_ready"], 1)
            pe.matmul(bank[0][:, 0:P], p["fold"], gram[:], start=True, stop=True).then_inc(s["folded"], 1)
            pe.wait_ge(s["trace_in"], 1)
            pe.matmul(bank[1][:, 0:1], p["group16"], sums[:, 2:3], start=True, stop=True).then_inc(s["trace_done"], 1)
            for n in range(2):
                pe.wait_ge(s["pw_ready"], 4 * n + 1)
                pe.matmul(bank[2][:, 0:P], pw[:, 0, :], pw[:, 0, :], start=True, stop=True).then_inc(s["prod_done"], 1)
                pe.wait_ge(s["pw_ready"], 4 * n + 2)
                pe.matmul(bank[3][:, 0:P], pw[:, 1, :], pw[:, 0, :], start=True, stop=True).then_inc(s["prod_done"], 1)
                pe.wait_ge(s["pw_ready"], 4 * n + 3)
                pe.matmul(bank[4][:, 0:P], pw[:, 2, :], sigma[:], start=True, stop=True).then_inc(s["prod_done"], 1)
            pe.wait_ge(s["wp_ready"], 1)
            pe.matmul(bank[0][:, 0:HB], wP[:], b[:], start=True, stop=True).then_inc(s["wb_done"], 1)
            pe.wait_ge(s["b_ready"], 1)
            with pe.Fori(0, HB // 4) as i:
                for k in range(4):
                    n = 4 * i + k
                    pe.wait_ge(s["mat_ready"], n + 1 + 4)
                    pe.wait_ge(s["out_ready"], n + 1)
                    pe.matmul(bank[k + 1][:, 0:HW], mat[:, k, :], m.xa[:, bass.ds(n * HW, HW)],
                              start=True, stop=True).then_inc(s["app_done"], 1)

        @block.scalar
        def _(act):
            act.sem_inc(s["xc_ready"], 4)
            act.wait_ge(s["var_ready"], 1)
            act.activation(a[:], gvar[:], ACT.Sqrt).then_inc(s["std_ready"], 1)
            act.wait_ge(s["xm_done"], 1)
            act.activation(scal[:, 0:1], bank[3][:, 0:1], ACT.Sqrt).then_inc(s["scale_ready"], 1)
            act.wait_ge(s["hvar_ready"], 1)
            act.activation(hs[:, 2, :], hs[:, 1, :], ACT.Sqrt).then_inc(s["hstd_ready"], 1)
            act.activation(scal[:, 1:2], p["x_weight"], ACT.Sigmoid).then_inc(s["sig_ready"], 1)
            act.wait_ge(s["fc2_done"], 1)
            act.activation(gate[:], bank[4][:, 0:HB], ACT.Sigmoid).then_inc(s["sig_ready"], 1)
            act.wait_ge(s["centre_ready"], 1)
            with act.Fori(0, TILES // 2) as i:
                for k in range(2):
                    t = 2 * i + k
                    act.wait_ge(s["xt_done"], 2 * i + 1)
                    for q in range(2):
                        n = 2 * t + q
                        act.activation(xc[:, k, q * HW:(q + 1) * HW], m.xa[:, bass.ds(n * HW, HW)], ACT.Identity,
                                       scale=a[:, bass.ds(n, 1)], bias=bc[:, bass.ds(n, 1)])\
                           .then_inc(s["xc_ready"], 1)

        @block.vector
        def _(dve):
            count = [0]

            def link(ins):
                count[0] += 1
                ins.then_inc(s["dve_step"], 1)
                dve.wait_ge(s["dve_step"], count[0])

            dve.sem_inc(s["xt_ready"], 2)
            dve.sem_inc(s["mat_ready"], 4)
            dve.sem_inc(s["out_ready"], 4)
            for n in range(HB):
                ins = dve.bn_aggr(mv[:, n, :], m.stats[:, n, :])
            link(ins)
            mean_c, var_c = mv[:, :, 0], mv[:, :, 1]
            dve.memset(zero[:], 0.0)
            link(dve.tensor_copy(st[:, 0, :], mean_c))
            link(dve.tensor_tensor(tmp[:], mean_c, mean_c, ALU.mult))
            dve.tensor_tensor(st[:, 1, :], tmp[:], var_c, ALU.add).then_inc(s["st_ready"], 1)
            dve.wait_ge(s["pair_done"], 1)
            link(dve.tensor_copy(gst[:].rearrange("p a b -> p (a b)"), bank[0][:, 0:2 * HB]))
            link(dve.tensor_tensor(tmp[:], gst[:, 0, :], gst[:, 0, :], ALU.mult))
            link(dve.tensor_tensor(gvar[:], gst[:, 1, :], tmp[:], ALU.subtract))
            link(dve.tensor_scalar(gvar[:], gvar[:], 0.0, None, ALU.max))
            dve.tensor_scalar(gvar[:], gvar[:], 1e-5, None, ALU.add).then_inc(s["var_ready"], 1)
            dve.wait_ge(s["std_ready"], 1)
            link(dve.reciprocal(a[:], a[:]))
            link(dve.scalar_tensor_tensor(b[:], gst[:, 0, :], -1.0, a[:], ALU.mult, ALU.mult))
            link(dve.tensor_tensor(tmp[:], a[:], a[:], ALU.mult))
            link(dve.scalar_tensor_tensor(xv[:], tmp[:], float(HW) / (HW - 1), var_c, ALU.mult, ALU.mult))
            link(dve.tensor_tensor(tmp[:], a[:], mean_c, ALU.mult))
            link(dve.tensor_tensor(tmp[:], tmp[:], b[:], ALU.add))
            link(dve.tensor_reduce(sums[:, 0:1], tmp[:], AXX, ALU.add))
            dve.tensor_reduce(sums[:, 1:2], xv[:], AXX, ALU.add).then_inc(s["sums_ready"], 1)
            dve.wait_ge(s["fold_done"], 1)
            link(dve.tensor_scalar(scal[:, 2:3], bank[1][:, 0:1], 1.0 / B, None, ALU.mult))
            dve.tensor_scalar(sums[:, 3:4], bank[1][:, 1:2], 1.0 / B, None, ALU.mult).then_inc(s["mu_ready"], 1)
            dve.tensor_scalar(bc[:], b[:], scal[:, 2:3], None, ALU.subtract).then_inc(s["centre_ready"], 1)
            def two(v):
                return v.rearrange("p (h j) -> p h j", h=2)

            def over16(v):
                return v.unsqueeze(2).broadcast_to([HB, 2, HD])

            dve.wait_ge(s["fc1_done"], 1)
            link(dve.tensor_copy(h[:, 0, :], bank[2][0:HB, 0:2 * HD]))
            link(dve.tensor_reduce(hs[:, 0, :], two(h[:, 0, :]), AXX, ALU.add))
            link(dve.tensor_scalar(hs[:, 0, :], hs[:, 0, :], 1.0 / HD, None, ALU.mult))
            link(dve.tensor_tensor(two(h[:, 1, :]), two(h[:, 0, :]), over16(hs[:, 0, :]), ALU.subtract))
            link(dve.tensor_tensor(h[:, 2, :], h[:, 1, :], h[:, 1, :], ALU.mult))
            link(dve.tensor_reduce(hs[:, 1, :], two(h[:, 2, :]), AXX, ALU.add))
            dve.tensor_scalar(hs[:, 1, :], hs[:, 1, :], 1.0 / HD, 1e-5, ALU.mult, ALU.add).then_inc(s["hvar_ready"], 1)
            dve.wait_ge(s["hstd_ready"], 1)
            link(dve.reciprocal(hs[:, 3, :], hs[:, 2, :]))
            link(dve.tensor_tensor(two(h[:, 3, :]), two(h[:, 1, :]), over16(hs[:, 3, :]), ALU.mult))
            link(dve.tensor_tensor(h[:, 4, :], h[:, 3, :], p["ln_g"][0:HB, :], ALU.mult))
            link(dve.tensor_tensor(h[:, 5, :], h[:, 4, :], p["ln_b"][0:HB, :], ALU.add))
            dve.tensor_scalar(h[:, 7, :], h[:, 5, :], 0.0, None, ALU.max).then_inc(s["hrelu_ready"], 1)
            dve.wait_ge(s["turn_done"], 1)
            dve.tensor_copy(hT[:], bank[2][0:2 * HD, 0:HB]).then_inc(s["ht_ready"], 1)
            with dve.Fori(0, TILES // 2) as i:
                for k in range(2):
                    t = 2 * i + k
                    dve.wait_ge(s["xt_done"], t + 2)
                    dve.wait_ge(s["tile_gram"], 2 * i + 1)
                    dve.tensor_copy(xt[:, k, :], bank[5 + k][:]).then_inc(s["xt_ready"], 1)
            dve.wait_ge(s["scale_ready"], 1)
            link(dve.reciprocal(scal[:, 3:4], scal[:, 0:1]))
            dve.wait_ge(s["sig_ready"], 2)
            link(dve.tensor_scalar(scal[:, 4:5], scal[:, 1:2], -1.0, 1.0, ALU.mult, ALU.add))
            link(dve.tensor_tensor(scal[:, 5:6], scal[:, 4:5], scal[:, 3:4], ALU.mult))
            link(dve.tensor_scalar(gate[:], gate[:], scal[:, 5:6], None, ALU.mult))
            link(dve.tensor_tensor(ga[:], gate[:], a[:], ALU.mult))
            dve.wait_ge(s["gram_done"], 1)
            dve.tensor_tensor(gram[:], bank[7][:, 0:P], p["group16"], ALU.mult).then_inc(s["mask_ready"], 1)
            dve.wait_ge(s["folded"], 1)
            link(dve.tensor_copy(pw[:, 3, :], bank[0][:, 0:P]))
            link(dve.tensor_tensor(half[:], pw[:, 3, 0:C], pw[:, 3, C:P], ALU.add))
            link(dve.tensor_tensor(sigma[:].rearrange("p (h n) -> p h n", h=2),
                                   half[:].unsqueeze(1).broadcast_to([P, 2, C]),
                                   p["group16"].rearrange("p (h n) -> p h n", h=2), ALU.mult))
            link(dve.tensor_scalar(sigma[:], sigma[:], 1e-5, None, ALU.mult))
            link(dve.scalar_tensor_tensor(sigma[:], p["ident"], 1.0 / (B * HW), sigma[:], ALU.mult, ALU.add))
            link(dve.tensor_tensor(pw[:, 3, :], sigma[:], p["ident"], ALU.mult))
            dve.tensor_reduce(sums[:, 2:3], pw[:, 3, :], AXX, ALU.add).then_inc(s["trace_in"], 1)
            dve.wait_ge(s["trace_done"], 1)
            link(dve.reciprocal(scal[:, 6:7], bank[1][:, 0:1]))
            link(dve.tensor_scalar(sigma[:], sigma[:], scal[:, 6:7], None, ALU.mult))
            link(dve.tensor_scalar(pw[:, 3, :], sigma[:], 1.5, None, ALU.mult))
            dve.scalar_tensor_tensor(pw[:, 0, :], p["ident"], -0.5, pw[:, 3, :], ALU.mult, ALU.add)\
               .then_inc(s["pw_ready"], 1)
            for n in range(2):
                dve.wait_ge(s["prod_done"], 3 * n + 1)
                dve.tensor_copy(pw[:, 1, :], bank[2][:, 0:P]).then_inc(s["pw_ready"], 1)
                dve.wait_ge(s["prod_done"], 3 * n + 2)
                dve.tensor_copy(pw[:, 2, :], bank[3][:, 0:P]).then_inc(s["pw_ready"], 1)
                dve.wait_ge(s["prod_done"], 3 * n + 3)
                link(dve.tensor_scalar(pw[:, 3, :], bank[4][:, 0:P], 1.5, None, ALU.mult))
                link(dve.scalar_tensor_tensor(pw[:, 0, :], pw[:, 0, :], -0.5, pw[:, 3, :], ALU.mult, ALU.add))
                dve.sem_inc(s["pw_ready"], 2)
            dve.tensor_scalar(wP[:], pw[:, 0, :], scal[:, 1:2], None, ALU.mult).then_inc(s["wp_ready"], 1)
            link(dve.tensor_tensor(bias[:], gate[:], b[:], ALU.mult))
            dve.wait_ge(s["wb_done"], 1)
            link(dve.tensor_tensor(bias[:], bias[:], bank[0][:, 0:HB], ALU.add))
            dve.sem_inc(s["b_ready"], 1)

            def matrix(n, k):
                dve.tensor_scalar(mat[:, k, :], wP[:], a[:, bass.ds(n, 1)], None, ALU.mult).then_inc(s["scaled"], 1)
                dve.wait_ge(s["scaled"], n + 1)
                dve.scalar_tensor_tensor(mat[:, k, :], p["ident"], ga[:, bass.ds(n, 1)], mat[:, k, :],
                                         ALU.mult, ALU.add).then_inc(s["mat_ready"], 1)

            dve.wait_ge(s["wp_ready"], 1)
            with dve.Fori(0, HB // 4) as i:
                for k in range(4):
                    dve.wait_ge(s["app_done"], 4 * i + 1)
                    matrix(4 * i + k, k)
                for k in range(4):
                    n = 4 * i + k
                    dve.wait_ge(s["app_done"], n + 2)
                    x = m.xa[:, bass.ds(n * HW, HW)]
                    dve.scalar_tensor_tensor(x, bank[k + 1][:, 0:HW], bias[:, bass.ds(n, 1)], x, ALU.add, ALU.add)\
                       .then_inc(s["out_ready"], 1)

def layer_norm_stage(nc, m, prefix, out_tile):
    p = m.par
    R = 8
    with ExitStack() as c:
        sem = c.enter_context(StageSemaphores(nc, prefix))
        sq = c.enter_context(nc.sbuf_tensor(f"{prefix}_sq", [P, 4, TW], F32))
        std = c.enter_context(nc.sbuf_tensor(f"{prefix}_std", [P, 2, TW], F32))
        s = {n: sem(n) for n in ("warm", "zeroed", "centred", "sq_ready", "copied", "var_done", "std_ready",
                                 "inv_ready", "spread_done", "xn_ready")}
        block = c.enter_context(nc.Block())
        bank = m.bank
        GROUPS = TILES // 4

        @block.tensor
        def _(pe):
            for i in range(GROUPS):
                for k in range(4):
                    t = 4 * i + k
                    if i:
                        pe.wait_ge(s["copied"], t - 3)
                        pe.wait_ge(s["sq_ready"], t - 3)
                    pe.matmul(bank[k][:], p["center"], tile_of(m.xa, t), start=True, stop=True)\
                      .then_inc(s["centred"], 1)
                for k in range(4):
                    pe.wait_ge(s["sq_ready"], 4 * i + k + 1)
                    mm = pe.matmul(bank[4 + i][0:R, :], p["var_rows"][:, k * R:(k + 1) * R], sq[:, k, :],
                                   start=(k == 0), stop=(k == 3))
                    mm.then_inc(s["var_done"], 1)
            pe.wait_ge(s["zeroed"], 1)
            for t in range(TILES):
                pe.wait_ge(s["inv_ready"], t // 4 + 1)
                if t >= 2:
                    pe.wait_ge(s["xn_ready"], t - 1)
                pe.matmul(bank[6 + t % 2][:], p["spread"][:, (t % 4) * P:(t % 4 + 1) * P], std[:, t // 4, :],
                          start=True, stop=True).then_inc(s["spread_done"], 1)

        @block.scalar
        def _(act):
            act.activation(sq[:, 0, 0:1], p["ident"][:, 0:1], ACT.Sqrt).then_inc(s["warm"], 1)
            act.wait_ge(s["warm"], 1)
            for i in range(GROUPS):
                for k in range(4):
                    t = 4 * i + k
                    act.wait_ge(s["centred"], t + 1)
                    if i:
                        act.wait_ge(s["var_done"], t - 3)
                    act.activation(sq[:, k, :], bank[k][:], ACT.Square).then_inc(s["sq_ready"], 1)
                act.wait_ge(s["zeroed"], 1)
                act.wait_ge(s["var_done"], 4 * i + 4)
                act.activation(std[0:R, i, :], bank[4 + i][0:R, :], ACT.Sqrt, bias=m.eps5[0:R, 0:1])\
                   .then_inc(s["std_ready"], 1)

        @block.vector
        def _(dve):
            dve.memset(std[:], 0.0).then_inc(s["zeroed"], 1)
            for i in range(GROUPS):
                for k in range(4):
                    t = 4 * i + k
                    dve.wait_ge(s["sq_ready"], t + 1)
                    dve.tensor_copy(out_tile(t), bank[k][:].rearrange("p (b t) -> p b t", b=2))\
                       .then_inc(s["copied"], 1)
                dve.wait_ge(s["std_ready"], i + 1)
                dve.reciprocal(std[0:R, i, :], std[0:R, i, :]).then_inc(s["inv_ready"], 1)
            for t in range(TILES):
                dve.wait_ge(s["spread_done"], t + 1)
                dve.wait_ge(s["copied"], t + 1)
                dve.tensor_tensor(out_tile(t), bank[6 + t % 2][:].rearrange("p (b t) -> p b t", b=2), out_tile(t),
                                  ALU.mult).then_inc(s["xn_ready"], 1)


def slice_attention_stage(nc, m):
    p = m.par
    LOG_NEG_LOG_EPS = float(np.log(-np.log(np.float32(1e-6)), dtype=np.float32))
    with ExitStack() as c:
        def sb(name, shape, dt=F32):
            return c.enter_context(nc.sbuf_tensor(f"sl_{name}", shape, dt))

        b_slice = sb("b_slice", [P, 1])
        x = sb("x", [P, 2, TW])
        xps = sb("xps", [P, 2, TW])
        clip, logit = sb("clip", [P, 2, TW]), sb("logit", [P, 2, TW])
        negmax = sb("negmax", [P, 2, 2])
        ex = sb("ex", [P, 2, 2, TW])
        tot, f = sb("tot", [P, 2, 4]), sb("f", [P, 4, 4])
        xpt = sb("xpt", [P, 2, 4, 2 * P])
        et = sb("et", [P, 2, TW])
        gtm, bm = sb("gtm", [P, 4, P]), sb("bm", [P, 4, P])
        names = ("x_ready bs_ready xp_done xps_ready lt_done clip1 clip2 inv_temp logit_ready max_ready negmax_ready "
                 "ex_ready xpt_done xpt_ready et_done et_ready gt_done gtm_ready b_done f_step bm_ready o_done "
                 "out_ready").split()
        sem = c.enter_context(StageSemaphores(nc, "sl"))
        s = {n: sem(n) for n in names}
        block = c.enter_context(nc.Block())
        bank = m.bank
        XP, XT, TM, LG, ET, GT, OB = bank[0], bank[1], bank[2], bank[3:5], bank[5], bank[6], bank[7]

        def run(engine, step):
            step(-1, 1, True, False)
            with engine.Fori(0, TILES // 2 - 1) as i:
                for k in range(2):
                    step(2 * i + k, k, True, True)
            step(TILES - 2, 0, True, True)
            step(TILES - 1, 1, False, True)

        @block.tensor
        def _(pe):
            def step(t, k, first, second):
                u = t + 1

                def x_of(q, n=1):
                    return x[:, 1 - k, q * P:(q + n) * P]

                def project(h):
                    pe.wait_ge(s["x_ready"], u + 1)
                    pe.wait_ge(s["xps_ready"], 2 * u + h + 1)
                    pe.matmul(XP[:], p["w_x"][:, h * P:(h + 1) * P], x_of(0, 4), start=True, stop=True)\
                      .then_inc(s["xp_done"], 1)

                def project_by_token(j):
                    pe.wait_ge(s["xpt_ready"], 2 * u + j + 1)
                    for q in range(2):
                        mm = pe.matmul(XT[:, q * 2 * P:(q + 1) * 2 * P], x_of(2 * j + q), p["w_x"],
                                       start=True, stop=True)
                    mm.then_inc(s["xpt_done"], 1)

                def logits(h):
                    pe.wait_ge(s["xps_ready"], 2 * u + h + 2)
                    pe.wait_ge(s["clip1"], 2 * u + h + 1)
                    pe.wait_ge(s["logit_ready"], 2 * u + h + 1)
                    pe.matmul(TM[:], p["w_temp"], xps[:, h, :], start=True, stop=True)
                    pe.matmul(LG[h][:], p["w_slice"], xps[:, h, :], start=True, stop=True)\
                      .then_inc(s["lt_done"], 1)

                def turn(h):
                    pe.wait_ge(s["ex_ready"], 4 * t + 2 * h + 2 + 4)
                    pe.wait_ge(s["et_ready"], 2 * t + h + 1)
                    for q in range(4):
                        mm = pe.transpose(ET[:, q * P:(q + 1) * P], ex[:, k, h, q * P:(q + 1) * P], p["ident"])
                    mm.then_inc(s["et_done"], 1)

                if first:
                    project(0)
                    project_by_token(0)
                    project(1)
                if second:
                    turn(0)
                if first:
                    logits(0)
                if second:
                    turn(1)
                if first:
                    project_by_token(1)
                if second:
                    pe.wait_ge(s["gtm_ready"], t + 1)
                    pe.wait_ge(s["xpt_ready"], 2 * t + 3)
                    for h in range(2):
                        pe.wait_ge(s["et_ready"], 2 * t + h + 2)
                        for b in range(2):
                            for q in (2 * b, 2 * b + 1):
                                mm = pe.matmul(GT[:, (2 * h + b) * P:(2 * h + b + 1) * P],
                                               xpt[:, k, q, h * P:(h + 1) * P], et[:, h, q * P:(q + 1) * P],
                                               start=(q == 2 * b), stop=(q == 2 * b + 1))
                    mm.then_inc(s["gt_done"], 1)
                if first:
                    logits(1)
                if second:
                    pe.wait_ge(s["gtm_ready"], t + 2)
                    pe.wait_ge(s["out_ready"], t + 1)
                    for n in range(4):
                        mm = pe.matmul(OB[:, n * P:(n + 1) * P], gtm[:, n, :],
                                       p["w_out"][:, (n // 2) * P:(n // 2 + 1) * P], start=True, stop=True)
                    mm.then_inc(s["b_done"], 1)
                    pe.wait_ge(s["bm_ready"], t + 2)
                    for b in range(2):
                        for h in range(2):
                            mm = pe.matmul(OB[:, b * HW:(b + 1) * HW], bm[:, 2 * h + b, :],
                                           ex[:, k, h, b * HW:(b + 1) * HW], start=(h == 0), stop=(h == 1))
                    mm.then_inc(s["o_done"], 1)

            run(pe, step)

        @block.scalar
        def _(act):
            act.sem_inc(s["xps_ready"], 1)
            act.sem_inc(s["et_ready"], 1)
            act.sem_inc(s["ex_ready"], 4)

            def step(t, k, first, second):
                u = t + 1

                def turned(h):
                    act.wait_ge(s["et_done"], 2 * t + h + 1)
                    act.wait_ge(s["gt_done"], t + 2)
                    act.activation(et[:, h, :], ET[:], ACT.Copy).then_inc(s["et_ready"], 1)

                def exponentials(h):
                    act.wait_ge(s["negmax_ready"], 2 * u + h + 1)
                    act.wait_ge(s["o_done"], u + 1)
                    for b in range(2):
                        act.activation(ex[:, 1 - k, h, b * HW:(b + 1) * HW], logit[:, h, b * HW:(b + 1) * HW],
                                       ACT.Exp, bias=negmax[:, h, b:b + 1],
                                       accum_out=tot[:, 1 - k, 2 * h + b:2 * h + b + 1]).then_inc(s["ex_ready"], 1)

                if first:
                    for h in range(2):
                        act.wait_ge(s["xp_done"], 2 * u + h + 1)
                        act.wait_ge(s["lt_done"], 2 * u + h + 1)
                        act.activation(xps[:, h, :], XP[:], ACT.Identity, bias=p["b_x"][:, 0:1])\
                           .then_inc(s["xps_ready"], 1)
                if second:
                    turned(0)
                    turned(1)
                if first:
                    exponentials(0)
                    exponentials(1)

            run(act, step)

        @block.vector
        def _(dve):
            for n, start in (("clip1", 1), ("logit_ready", 2), ("xpt_ready", 1), ("gtm_ready", 1), ("out_ready", 1),
                             ("bm_ready", 1)):
                dve.sem_inc(s[n], start)
            dve.tensor_scalar(b_slice[:], p["b_slice"], LOG_NEG_LOG_EPS, None, ALU.subtract).then_inc(s["bs_ready"], 1)
            dve.wait_ge(s["bs_ready"], 1)

            def step(t, k, first, second):
                u = t + 1

                def tokens(j):
                    dve.wait_ge(s["xpt_done"], 2 * u + j + 1 + 3)
                    dve.wait_ge(s["gt_done"], u + 1)
                    dve.tensor_tensor(xpt[:, 1 - k, 2 * j:2 * j + 2, :], XT[:].rearrange("p (q n) -> p q n", q=2),
                                      p["b_x_row"].unsqueeze(1).broadcast_to([P, 2, 2 * P]), ALU.add)\
                       .then_inc(s["xpt_ready"], 1)

                def clips(h):
                    n = 2 * u + h
                    dve.wait_ge(s["lt_done"], n + 3)
                    dve.tensor_scalar(clip[:, h, :], TM[:], p["b_temp"][:, 0:1], 0.4, ALU.add, ALU.min)\
                       .then_inc(s["clip1"], 1)
                    if second and h == 0:
                        normaliser(0)
                    dve.wait_ge(s["clip1"], n + 2)
                    dve.tensor_scalar(clip[:, h, :], clip[:, h, :], -0.4, 0.5, ALU.max, ALU.add)\
                       .then_inc(s["clip2"], 1)
                    if second and h == 0:
                        normaliser(1)
                    dve.wait_ge(s["clip2"], n + 1)
                    dve.reciprocal(clip[:, h, :], clip[:, h, :]).then_inc(s["inv_temp"], 1)

                def scaled(h):
                    n = 2 * u + h
                    dve.wait_ge(s["inv_temp"], n + 1)
                    dve.wait_ge(s["ex_ready"], 4 * u + 2 * h + 2)
                    dve.scalar_tensor_tensor(logit[:, h, :], LG[h][:], b_slice[:, 0:1], clip[:, h, :],
                                             ALU.add, ALU.mult).then_inc(s["logit_ready"], 1)

                def largest(h):
                    n = 2 * u + h
                    dve.wait_ge(s["logit_ready"], n + 3)
                    dve.tensor_reduce(negmax[:, h, :], logit[:, h, :].rearrange("p (b n) -> p b n", b=2),
                                      AXX, ALU.max).then_inc(s["max_ready"], 1)
                    dve.wait_ge(s["max_ready"], n + 1)
                    dve.tensor_scalar(negmax[:, h, :], negmax[:, h, :], -1.0, None, ALU.mult)\
                       .then_inc(s["negmax_ready"], 1)

                def normaliser(j):
                    if j:
                        dve.wait_ge(s["f_step"], 6 * t + j)
                    else:
                        dve.wait_ge(s["ex_ready"], 4 * t + 8)
                    if j == 0:
                        ins = dve.reciprocal(f[:, 0, :], tot[:, k, :])
                    elif j == 1:
                        ins = dve.tensor_tensor(f[:, 1, :], tot[:, k, :], f[:, 0, :], ALU.mult)
                    elif j == 2:
                        ins = dve.tensor_scalar(f[:, 1, :], f[:, 1, :], 1e-5, None, ALU.add)
                    elif j == 3:
                        ins = dve.reciprocal(f[:, 2, :], f[:, 1, :])
                    elif j == 4:
                        ins = dve.tensor_tensor(f[:, 2, :], f[:, 2, :], f[:, 0, :], ALU.mult)
                    else:
                        ins = dve.tensor_tensor(f[:, 3, :], f[:, 2, :], f[:, 0, :], ALU.mult)
                    ins.then_inc(s["f_step"], 1)

                if first:
                    tokens(0)
                    clips(0)
                elif second:
                    normaliser(0)
                    normaliser(1)
                if second:
                    normaliser(2)
                if first:
                    scaled(0)
                if second:
                    normaliser(3)
                if first:
                    tokens(1)
                if second:
                    normaliser(4)
                if first:
                    largest(0)
                if second:
                    normaliser(5)
                    dve.wait_ge(s["gt_done"], t + 3)
                    dve.wait_ge(s["bm_ready"], t + 1)
                    dve.tensor_tensor(gtm[:], GT[:].rearrange("p (n g) -> p n g", n=4),
                                      p["headmask"].unsqueeze(1).broadcast_to([P, 4, P]), ALU.mult)\
                       .then_inc(s["gtm_ready"], 1)
                if first:
                    clips(1)
                if second:
                    dve.wait_ge(s["b_done"], t + 1)
                    dve.wait_ge(s["f_step"], 6 * t + 6)
                    dve.wait_ge(s["o_done"], t + 2)
                    dve.tensor_tensor(bm[:], OB[:].rearrange("p (n g) -> p n g", n=4),
                                      f[:, 3, :].unsqueeze(2).broadcast_to([P, 4, P]), ALU.mult)\
                       .then_inc(s["bm_ready"], 1)
                if first:
                    scaled(1)
                    largest(1)
                if second:
                    dve.wait_ge(s["o_done"], t + 3)
                    xa = tile_of(m.xa, t)
                    dve.scalar_tensor_tensor(xa, OB[:], p["b_out"][:, 0:1], xa, ALU.add, ALU.add)\
                       .then_inc(s["out_ready"], 1)

            run(dve, step)

        @block.gpsimd
        def _(pool):
            pool.sem_inc(s["lt_done"], 2)
            pool.sem_inc(s["gt_done"], 2)
            pool.sem_inc(s["o_done"], 2)
            pool.sem_inc(s["xpt_done"], 3)
            with pool.Fori(0, TILES // 2) as i:
                for k in range(2):
                    t = 2 * i + k
                    pool.wait_ge(s["xpt_done"], 2 * t + 1)
                    pool.tensor_copy(x[:, k, :], tile_of(m.xn, t)).then_inc(s["x_ready"], 1)


def lstm_stage(nc, m):
    p = m.par
    STEPS = 8
    CH = STEPS * HB
    SC = 2.0 ** 12
    with ExitStack() as c:
        def sb(name, shape, dt=F32):
            return c.enter_context(nc.sbuf_tensor(f"ls_{name}", shape, dt))

        xn = m.xn_steps
        hs = sb("hs", [P, COLS])
        wscaled = sb("wscaled", [P, 2 * E * HID])
        u = sb("u", [P, 3, P])
        bias = sb("bias", [P, P])
        vs, rest = sb("vs", [P, 3, P]), sb("rest", [P, 3, P])
        vp = [sb(f"v{k}", [P, 3, P], BF16) for k in range(3)]
        gates, ig, cell, hc, tc = (sb("gates", [P, 3, HB]), sb("ig", [P, HB]), sb("cell", [P, HB]),
                                   sb("hc", [P, HB]), sb("tc", [P, HB]))
        og = sb("og", [P, HB])
        h1, h2 = sb("h1", [P, HB], F16), sb("h2", [P, HB], F16)
        names = ("split_step w_step u_ready zeros warm z_done "
                 "gates_ready ig_ready cell_ready tc_ready og_ready h1_ready h32_ready h2_ready hc_ready "
                 "out_ready").split()
        sem = c.enter_context(StageSemaphores(nc, "ls"))
        s = {n: sem(n) for n in names}
        block = c.enter_context(nc.Block())
        bank = m.bank
        hs_bt = hs[:].rearrange("p (t b) -> p b t", b=HB)
        xa_bt = m.xa[:].rearrange("p (b t) -> p b t", b=HB)

        @block.tensor
        def _(pe):
            def prepare(chunk, b, part):
                if part == 0:
                    pe.matmul(bank[b][:, 0:3 * CH], bias[0:3, :], p["gate_sel"][0:3, :], start=True, stop=False,
                              skip_group_check=True)
                else:
                    o = bank[b][:, 0:3 * CH].rearrange("p (s g b) -> p s g b", s=STEPS, g=3)[:, :, part - 1, :]
                    pe.matmul(o, u[:, part - 1, :], xn[:, bass.ds(chunk * CH, CH)], start=False, stop=False,
                              skip_group_check=True)

            pe.wait_ge(s["u_ready"], 1)
            pe.wait_ge(s["zeros"], 1)
            for part in range(4):
                prepare(0, 0, part)
            with pe.Fori(0, HW // (2 * STEPS)) as i:
                for b in range(2):
                    for q in range(STEPS):
                        t = 2 * STEPS * i + STEPS * b + q
                        pe.wait_ge(s["h1_ready"], t + 1)
                        for part in range(3):
                            for g in range(3):
                                o = bank[b][:, (3 * q + g) * HB:(3 * q + g + 1) * HB]
                                pe.matmul(o, vp[part][:, g, :], h1[:], start=False, stop=False,
                                          skip_group_check=True)
                        pe.wait_ge(s["h2_ready"], t + 1)
                        for part in range(2):
                            for g in range(3):
                                o = bank[b][:, (3 * q + g) * HB:(3 * q + g + 1) * HB]
                                mm = pe.matmul(o, vp[part][:, g, :], h2[:], start=False, stop=(part == 1),
                                               skip_group_check=True)
                        mm.then_inc(s["z_done"], 1)
                        if q < 4:
                            prepare(2 * i + b + 1, 1 - b, q)

        @block.scalar
        def _(act):
            act.activation(tc[:, 0:1], p["ident"][:, 0:1], ACT.Tanh).then_inc(s["warm"], 1)
            with act.Fori(0, HW // (2 * STEPS)) as i:
                for b in range(2):
                    for q in range(STEPS):
                        t = 2 * STEPS * i + STEPS * b + q
                        act.wait_ge(s["z_done"], t + 1)
                        act.activation(gates[:], bank[b][:, 3 * q * HB:3 * (q + 1) * HB].rearrange(
                            "p (g b) -> p g b", g=3), ACT.Tanh).then_inc(s["gates_ready"], 1)
                        act.wait_ge(s["cell_ready"], t + 1)
                        act.activation(tc[:], cell[:], ACT.Tanh).then_inc(s["tc_ready"], 1)

        @block.gpsimd
        def _(pool):
            scaled = wscaled[:]
            pool.tensor_scalar(scaled, m.w12[:], m.wscale[:, 0:1], None, ALU.mult).then_inc(s["split_step"], 1)
            pool.wait_ge(s["split_step"], 1)
            pool.tensor_copy(m.wp[0][:], scaled).then_inc(s["split_step"], 1)
            pool.wait_ge(s["split_step"], 2)
            pool.tensor_tensor(m.wp[1][:], scaled, m.wp[0][:], ALU.subtract).then_inc(s["split_step"], 1)

        @block.vector
        def _(dve):
            count = [0]

            def link(ins):
                count[0] += 1
                ins.then_inc(s["w_step"], 1)
                dve.wait_ge(s["w_step"], count[0])

            for g, n in enumerate("igo"):
                half = 1.0 if n == "g" else 0.5
                dve.tensor_scalar(u[:, g, :], p[f"u_{n}"], half, None, ALU.mult)
                dve.tensor_scalar(vs[:, g, :], p[f"v_{n}"], half / SC, None, ALU.mult)
            link(dve.tensor_scalar(bias[0:3, :], p["lstm_b"][0:3, :], p["lstm_half"][0:3, :], None, ALU.mult))
            link(dve.tensor_copy(vp[0][:], vs[:]))
            link(dve.tensor_tensor(rest[:], vs[:], vp[0][:], ALU.subtract))
            link(dve.tensor_copy(vp[1][:], rest[:]))
            link(dve.tensor_tensor(vs[:], rest[:], vp[1][:], ALU.subtract))
            dve.tensor_copy(vp[2][:], vs[:])
            dve.memset(xn[:, COLS:COLS + CH], 0.0)
            dve.memset(hc[:], 0.0)
            dve.memset(h1[:], 0.0)
            link(dve.memset(h2[:], 0.0))
            dve.sem_inc(s["u_ready"], 1)
            dve.sem_inc(s["zeros"], 1)
            dve.sem_inc(s["h1_ready"], 1)
            dve.sem_inc(s["h2_ready"], 1)
            dve.sem_inc(s["hc_ready"], 1)
            with dve.Fori(0, HW // (2 * STEPS)) as i:
                for b in range(2):
                    for q in range(STEPS):
                        t = 2 * STEPS * i + STEPS * b + q
                        dve.wait_ge(s["gates_ready"], t + 1)
                        dve.scalar_tensor_tensor(ig[:], gates[:, 0, :], 1.0, gates[:, 1, :], ALU.add, ALU.mult)\
                           .then_inc(s["ig_ready"], 1)
                        dve.wait_ge(s["ig_ready"], t + 1)
                        dve.wait_ge(s["hc_ready"], t + 1)
                        dve.scalar_tensor_tensor(cell[:], ig[:], 0.5, hc[:], ALU.mult, ALU.add)\
                           .then_inc(s["cell_ready"], 1)
                        dve.tensor_scalar(og[:], gates[:, 2, :], SC / 2, SC / 2, ALU.mult, ALU.add)\
                           .then_inc(s["og_ready"], 1)
                        dve.wait_ge(s["og_ready"], t + 1)
                        dve.wait_ge(s["tc_ready"], t + 1)
                        h32 = hs[:, bass.ds(t * HB, HB)]
                        dve.tensor_tensor(h1[:], og[:], tc[:], ALU.mult).then_inc(s["h1_ready"], 1)
                        dve.tensor_tensor(h32, og[:], tc[:], ALU.mult).then_inc(s["h32_ready"], 1)
                        dve.wait_ge(s["h32_ready"], t + 1)
                        dve.tensor_tensor(h2[:], h32, h1[:], ALU.subtract).then_inc(s["h2_ready"], 1)
                        dve.scalar_tensor_tensor(hc[:], h32, 1.0 / SC, cell[:], ALU.mult, ALU.mult)\
                           .then_inc(s["hc_ready"], 1)
                    t0 = 2 * STEPS * i + STEPS * b
                    x = xa_bt[:, :, bass.ds(t0, STEPS)]
                    dve.scalar_tensor_tensor(x, hs_bt[:, :, bass.ds(t0, STEPS)], 1.0 / SC, x, ALU.mult, ALU.add)\
                       .then_inc(s["out_ready"], 1)

def sigmoid_attention_stage(nc, m):
    p = m.par
    with ExitStack() as c:
        def sb(name, shape, dt=F32):
            return c.enter_context(nc.sbuf_tensor(f"sg_{name}", shape, dt))

        sem = c.enter_context(StageSemaphores(nc, "sg"))
        x = sb("x", [P, 2, TW])
        qz = sb("qz", [P, 2, 2, TW])
        xt = sb("xt", [P, 2, TW])
        att = sb("att", [P, 4, TW])
        names = "zeroed warm x_ready q_done q_ready xt_done xt_ready s_done att_ready v_done out_ready".split()
        s = {n: sem(n) for n in names}
        block = c.enter_context(nc.Block())
        bank = m.bank
        SB = (6, 7, 3, 2)

        def run(engine, step):
            step(-1, 1, True, False)
            with engine.Fori(0, TILES // 2 - 1) as i:
                for k in range(2):
                    step(2 * i + k, k, True, True)
            step(TILES - 2, 0, True, True)
            step(TILES - 1, 1, False, True)

        @block.gpsimd
        def _(pool):
            pool.sem_inc(s["v_done"], 8)
            with pool.Fori(0, TILES // 2) as i:
                for k in range(2):
                    t = 2 * i + k
                    pool.wait_ge(s["v_done"], 4 * t + 4)
                    pool.tensor_copy(x[:, k, :], tile_of(m.xn, t)).then_inc(s["x_ready"], 1)

        @block.tensor
        def _(pe):
            def step(t, k, prepare, attend):
                u = t + 1

                def scores(n):
                    h, b = n // 2, n % 2
                    pe.wait_ge(s["att_ready"], 4 * t + n + 1)
                    for q in range(2):
                        mm = pe.matmul(bank[SB[n]][:, q * HW:(q + 1) * HW],
                                       x[:, k, (2 * b + q) * P:(2 * b + q + 1) * P],
                                       qz[:, k, h, b * HW:(b + 1) * HW], start=True, stop=True)
                    mm.then_inc(s["s_done"], 1)

                def values(n):
                    h, b = n // 2, n % 2
                    pe.wait_ge(s["att_ready"], 4 * t + n + 5)
                    for q in range(2):
                        mm = pe.matmul(bank[k][C * h:C * (h + 1), b * HW:(b + 1) * HW],
                                       xt[:, k, (2 * b + q) * P + C * h:(2 * b + q) * P + C * (h + 1)],
                                       att[:, n, q * HW:(q + 1) * HW], start=(q == 0), stop=(q == 1))
                    mm.then_inc(s["v_done"], 1)

                if attend:
                    pe.wait_ge(s["q_ready"], 2 * t + 3)
                    scores(0)
                    scores(1)
                if prepare:
                    pe.wait_ge(s["x_ready"], u + 1)
                    pe.wait_ge(s["q_ready"], 2 * u + 1)
                    pe.matmul(bank[4][:], p["q_w"], x[:, 1 - k, :], start=True, stop=True).then_inc(s["q_done"], 1)
                if attend:
                    scores(2)
                    scores(3)
                if prepare:
                    pe.wait_ge(s["xt_ready"], u + 1)
                    for q in range(4):
                        mm = pe.transpose(bank[5][:, q * P:(q + 1) * P], x[:, 1 - k, q * P:(q + 1) * P], p["ident"])
                    mm.then_inc(s["xt_done"], 1)
                if attend:
                    pe.wait_ge(s["xt_ready"], t + 2)
                    pe.wait_ge(s["out_ready"], t + 1)
                    for n in range(4):
                        values(n)

            run(pe, step)

        @block.scalar
        def _(act):
            act.sem_inc(s["q_ready"], 1)
            act.sem_inc(s["att_ready"], 4)
            act.activation(att[:, 0, 0:1], p["ident"][:, 0:1], ACT.Sigmoid).then_inc(s["warm"], 1)
            act.wait_ge(s["warm"], 1)
            act.wait_ge(s["zeroed"], 1)

            def step(t, k, prepare, attend):
                u = t + 1

                def weights(n):
                    act.wait_ge(s["s_done"], 4 * t + n + 1)
                    act.wait_ge(s["v_done"], 4 * t + n + 1 + 4)
                    act.activation(att[:, n, :], bank[SB[n]][:], ACT.Sigmoid).then_inc(s["att_ready"], 1)

                if attend:
                    weights(0)
                    weights(1)
                if prepare:
                    act.wait_ge(s["q_done"], u + 1)
                    act.wait_ge(s["v_done"], 4 * u + 4)
                    for h in range(2):
                        r = slice(C * h, C * (h + 1))
                        act.activation(qz[r, 1 - k, h, :], bank[4][r, :], ACT.Copy).then_inc(s["q_ready"], 1)
                if attend:
                    weights(2)
                    weights(3)

            run(act, step)

        @block.vector
        def _(dve):
            dve.sem_inc(s["xt_ready"], 1)
            dve.sem_inc(s["out_ready"], 2)
            dve.memset(qz[:], 0.0).then_inc(s["zeroed"], 1)

            def step(t, k, prepare, attend):
                u = t + 1
                if prepare:
                    dve.wait_ge(s["xt_done"], u + 1)
                    dve.wait_ge(s["v_done"], 4 * u + 4)
                    dve.tensor_copy(xt[:, 1 - k, :], bank[5][:]).then_inc(s["xt_ready"], 1)
                if attend:
                    dve.wait_ge(s["v_done"], 4 * t + 4 + 8)
                    xa = tile_of(m.xa, t)
                    dve.tensor_tensor(xa, bank[k][:], xa, ALU.add).then_inc(s["out_ready"], 1)

            run(dve, step)


def route_stage(nc, m):
    p = m.par
    G = TILES * 4 * 2
    with ExitStack() as c:
        def sb(name, shape, dt=F32):
            return c.enter_context(nc.sbuf_tensor(f"ro_{name}", shape, dt))

        sem = c.enter_context(StageSemaphores(nc, "ro"))
        sq, std, xn = sb("sq", [P, 2, TW]), sb("std", [P, 2, TW]), sb("xn", [P, 2, TW])
        x1 = sb("x1", [P, 2, TW], F16)
        lg = sb("lg", [P, G, E])
        e, e2, pick = sb("e", [P, G, E]), sb("e2", [P, G, E]), sb("pick", [P, G, E])
        masks = sb("masks", [P, 2, G, E])
        top = sb("top", [P, 4, G])
        dt = sb("dt", [2 * E, TILES, TW])
        names = ("warm centred sq_ready var_done std_ready inv_ready xn_ready x1_ready parts_ready gate_done "
                 "lg_ready exp_in e_ready step d_ready dt_done dt_ready stored").split()
        s = {n: sem(n) for n in names}
        block = c.enter_context(nc.Block())
        bank = m.bank

        @block.tensor
        def _(pe):
            pe.sem_inc(s["gate_done"], 1)
            with pe.Fori(0, TILES // 2) as i:
                for k in range(2):
                    pe.wait_ge(s["xn_ready"], 2 * i + 1)
                    pe.matmul(bank[k][:], p["center"], tile_of(m.xa, 2 * i + k), start=True, stop=True)\
                      .then_inc(s["centred"], 1)
                for k in range(2):
                    pe.wait_ge(s["sq_ready"], 2 * i + k + 1)
                    pe.matmul(bank[2 + k][:], p["mean"], sq[:, k, :], start=True, stop=True)\
                      .then_inc(s["var_done"], 1)
                for k in range(2):
                    pe.wait_ge(s["xn_ready"], 2 * i + k + 2)
                    pe.wait_ge(s["lg_ready"], 2 * i + 1)
                    for q in range(4):
                        mm = pe.matmul(bank[4 + k][:, q * 2 * E:(q + 1) * 2 * E], xn[:, k, q * P:(q + 1) * P],
                                       p["gate_w"], start=True, stop=True)
                    mm.then_inc(s["gate_done"], 1)
            pe.wait_ge(s["d_ready"], 1)
            for t in range(TILES):
                if t >= 2:
                    pe.wait_ge(s["dt_ready"], t - 1)
                for q in range(4):
                    g = 2 * (4 * t + q)
                    mm = pe.transpose(bank[6 + t % 2][0:2 * E, q * P:(q + 1) * P],
                                      e2[:, g:g + 2, :].rearrange("p g e -> p (g e)"), p["ident"])
                mm.then_inc(s["dt_done"], 1)

        @block.scalar
        def _(act):
            act.activation(std[:, 0, 0:1], p["ident"][:, 0:1], ACT.Sqrt).then_inc(s["warm"], 1)
            act.wait_ge(s["warm"], 1)
            with act.Fori(0, TILES // 2) as i:
                for k in range(2):
                    act.wait_ge(s["centred"], 2 * i + k + 1)
                    act.activation(sq[:, k, :], bank[k][:], ACT.Square).then_inc(s["sq_ready"], 1)
                for k in range(2):
                    act.wait_ge(s["var_done"], 2 * i + k + 1)
                    act.activation(std[:, k, :], bank[2 + k][:], ACT.Sqrt, bias=m.eps5[:, 0:1])\
                       .then_inc(s["std_ready"], 1)
            act.wait_ge(s["exp_in"], 1)
            act.activation(e[:], lg[:], ACT.Exp).then_inc(s["e_ready"], 1)
            for t in range(TILES):
                act.wait_ge(s["dt_done"], t + 1)
                act.activation(dt[:, t, :], bank[6 + t % 2][0:2 * E, :], ACT.Copy).then_inc(s["dt_ready"], 1)

        @block.sync
        def _(sp):
            for t in range(TILES):
                sp.wait_ge(s["dt_ready"], t + 1)
                sp.dma_start(m.route[:, :, t, :].rearrange("h e n -> (h e) n"), dt[:, t, :])\
                  .then_inc(s["stored"], 16)
            sp.wait_ge(s["stored"], 16 * TILES)

        @block.vector
        def _(dve):
            dve.sem_inc(s["lg_ready"], 1)
            dve.sem_inc(s["xn_ready"], 1)
            with dve.Fori(0, TILES // 2) as i:
                for k in range(2):
                    t = 2 * i + k
                    dve.wait_ge(s["std_ready"], t + 1)
                    dve.reciprocal(std[:, k, :], std[:, k, :]).then_inc(s["inv_ready"], 1)
                    dve.wait_ge(s["inv_ready"], t + 1)
                    dve.wait_ge(s["gate_done"], 2 * i + 1)
                    dve.tensor_tensor(xn[:, k, :], bank[k][:], std[:, k, :], ALU.mult).then_inc(s["xn_ready"], 1)
                for k in range(2):
                    t = 2 * i + k
                    dve.wait_ge(s["xn_ready"], t + 2)
                    dve.tensor_scalar(x1[:, k, :], xn[:, k, :], XSCALE, None, ALU.mult).then_inc(s["x1_ready"], 1)
                    dve.wait_ge(s["x1_ready"], t + 1)
                    for h in range(2):
                        r = slice(C * h, C * (h + 1))
                        o = m.xs[h][:, bass.ds(t * TW, TW)]
                        dve.tensor_copy(o[0:C, :], x1[r, k, :])
                        dve.scalar_tensor_tensor(o[C:P, :], xn[r, k, :], XSCALE, x1[r, k, :],
                                                 ALU.mult, ALU.subtract).then_inc(s["parts_ready"], 1)
                for k in range(2):
                    t = 2 * i + k
                    dve.wait_ge(s["gate_done"], t + 2)
                    dve.tensor_tensor(lg[:, bass.ds(t * 8, 8), :].rearrange("p (q h) e -> p q (h e)", h=2),
                                      bank[4 + k][:, 0:8 * E].rearrange("p (q n) -> p q n", q=4),
                                      p["gate_b"].unsqueeze(1).broadcast_to([P, 4, 2 * E]), ALU.add)\
                       .then_inc(s["lg_ready"], 1)
            count = [0]

            def link(ins):
                count[0] += 1
                ins.then_inc(s["step"], 1)
                dve.wait_ge(s["step"], count[0])

            def over(v):
                return v.unsqueeze(2).broadcast_to([P, G, E])

            idx = p["idx_w"][:, 0:E].unsqueeze(1).broadcast_to([P, G, E])
            dve.wait_ge(s["lg_ready"], TILES + 1)
            link(dve.tensor_reduce(top[:, 0, :], lg[:], AXX, ALU.max))
            dve.tensor_tensor(lg[:], lg[:], over(top[:, 0, :]), ALU.subtract).then_inc(s["exp_in"], 1)
            dve.wait_ge(s["e_ready"], 1)

            def choose(src, mask):
                link(dve.tensor_reduce(top[:, 1, :], src, AXX, ALU.max))
                link(dve.tensor_tensor(pick[:], src, over(top[:, 1, :]), ALU.is_equal))
                link(dve.tensor_tensor(pick[:], pick[:], idx, ALU.mult))
                link(dve.tensor_reduce(top[:, 2, :], pick[:], AXX, ALU.max))
                link(dve.tensor_tensor(mask, pick[:], over(top[:, 2, :]), ALU.is_equal))

            choose(e[:], masks[:, 0])
            link(dve.scalar_tensor_tensor(e2[:], masks[:, 0], -2.0, e[:], ALU.mult, ALU.add))
            choose(e2[:], masks[:, 1])
            link(dve.tensor_tensor(pick[:], masks[:, 0], masks[:, 1], ALU.add))
            link(dve.tensor_tensor(e2[:], pick[:], e[:], ALU.mult))
            link(dve.tensor_reduce(top[:, 3, :], e2[:], AXX, ALU.add))
            link(dve.reciprocal(top[:, 0, :], top[:, 3, :]))
            dve.tensor_tensor(e2[:], e2[:], over(top[:, 0, :]), ALU.mult).then_inc(s["d_ready"], 1)


def expert_stage(nc, m):
    p = m.par
    with ExitStack() as c:
        def sb(name, shape, dt=F32):
            return c.enter_context(nc.sbuf_tensor(f"ex_{name}", shape, dt))

        sem = c.enter_context(StageSemaphores(nc, "ex"))
        d = sb("d", [P, 2, E, TW])
        gated, hid = sb("gated", [P, 2, TW]), sb("hid", [P, 2, TW])
        part, acc = sb("part", [P, 2, TW]), sb("acc", [P, 2, TW])
        s = {n: sem(n) for n in ("warm", "up1_done", "up2_done", "gated_ready", "hid_ready", "down_done",
                                 "part_ready", "acc_ready")}
        d_landed = [sem(f"d_landed{k}") for k in range(2)]
        stored = [sem(f"stored{k}") for k in range(2)]
        block = c.enter_context(nc.Block())
        bank = m.bank
        N = 2 * E

        @block.sync
        def _(sp):
            od = m.out.rearrange("(h g b) c n -> g h c b n", h=2, b=2)
            sp.sem_inc(stored[0], 1)
            sp.sem_inc(stored[1], 1)

            def load_dispatch(t, k):
                for h in range(2):
                    src = m.route[h:h + 1, :, bass.ds(t, 1), :].rearrange("h e t n -> (h t) e n")
                    sp.dma_start(d[C * h:C * (h + 1), k], src.broadcast_to([C, E, TW])).then_inc(d_landed[k], 16)

            def store(t, k):
                sp.wait_ge(s["acc_ready"], E * (t + 1) + 2)
                for h in range(2):
                    sp.dma_start(od[bass.ds(t, 1), h].rearrange("g c b n -> (g c) b n"),
                                 acc[C * h:C * (h + 1), k, :].rearrange("p (b n) -> p b n", b=2))\
                      .then_inc(stored[k], 16)

            for k in range(2):
                load_dispatch(k, k)
            with sp.Fori(0, TILES // 2 - 1) as i:
                for k in range(2):
                    store(2 * i + k, k)
                    load_dispatch(2 * i + k + 2, k)
            for k in range(2):
                store(TILES - 2 + k, k)
            for k in range(2):
                sp.wait_ge(stored[k], 32 * (TILES // 2) + 1)

        @block.gpsimd
        def _(pool):
            pool.sem_inc(s["acc_ready"], 2)
            with pool.Fori(0, TILES // 2) as i:
                for k in range(2):
                    t = 2 * i + k
                    pool.wait_ge(stored[k], 32 * i + 1)
                    for e in range(E):
                        pool.wait_ge(s["part_ready"], E * t + e + 3)
                        if e:
                            pool.wait_ge(s["acc_ready"], E * t + e + 2)
                        pool.tensor_tensor(acc[:, k, :], part[:, e % 2, :],
                                           acc[:, k, :] if e else tile_of(m.xa, t), ALU.add)\
                            .then_inc(s["acc_ready"], 1)

        @block.tensor
        def _(pe):
            pe.sem_inc(s["down_done"], 1)
            def up(t, n):
                e, h = n // 2, n % 2
                x = m.xs[h][:, bass.ds(t * TW, TW)]
                for w in range(2):
                    pe.wait_ge(s["gated_ready"] if w == 0 else s["hid_ready"], N * t + n + 1)
                    for q in range(2):
                        mm = pe.matmul(bank[2 * w + n % 2][:], m.wp[q][:, (2 * e + w) * HID:(2 * e + w + 1) * HID],
                                       x, start=(q == 0), stop=(q == 1))
                    mm.then_inc(s["up1_done"] if w == 0 else s["up2_done"], 1)

            def down(t, n):
                e, h = n // 2, n % 2
                pe.wait_ge(s["hid_ready"], N * t + n + 3)
                if h == 0:
                    pe.wait_ge(s["part_ready"], E * t + e + 1)
                mm = pe.matmul(bank[4 + e % 2][C * h:C * (h + 1), :], m.w3[:, e * C:(e + 1) * C],
                               hid[:, n % 2, :], start=True, stop=True)
                mm.then_inc(s["down_done"], 1)

            with pe.Fori(0, TILES // 2) as i:
                for r in range(2 * N + 2):
                    if r < 2 * N:
                        up(2 * i + r // N, r % N)
                    if r >= 2:
                        down(2 * i + (r - 2) // N, (r - 2) % N)

        @block.scalar
        def _(act):
            act.sem_inc(s["gated_ready"], 2)
            act.activation(gated[:, 0, 0:1], p["ident"][:, 0:1], ACT.Silu).then_inc(s["warm"], 1)
            act.wait_ge(s["warm"], 1)
            with act.Fori(0, TILES // 2) as i:
                for k in range(2):
                    for n in range(N):
                        r = N * (2 * i + k) + n
                        act.wait_ge(s["up1_done"], r + 1)
                        act.wait_ge(s["hid_ready"], r + 1)
                        act.activation(gated[:, n % 2, :], bank[n % 2][:], ACT.Silu, scale=m.unscale[:, 0:1])\
                           .then_inc(s["gated_ready"], 1)

        @block.vector
        def _(dve):
            dve.sem_inc(s["hid_ready"], 2)
            dve.sem_inc(s["part_ready"], 2)
            with dve.Fori(0, TILES // 2) as i:
                for k in range(2):
                    t = 2 * i + k

                    def hidden(n):
                        r = N * t + n
                        dve.wait_ge(s["up2_done"], r + 1)
                        dve.wait_ge(s["gated_ready"], r + 3)
                        dve.wait_ge(s["down_done"], N * t + max(n - 1, 0) + 1)
                        dve.tensor_tensor(hid[:, n % 2, :], bank[2 + n % 2][:], gated[:, n % 2, :], ALU.mult)\
                           .then_inc(s["hid_ready"], 1)

                    def gather(e):
                        dve.wait_ge(s["down_done"], N * t + 2 * e + 3)
                        dve.wait_ge(s["acc_ready"], E * t + e + 1)
                        if e == 0:
                            dve.wait_ge(d_landed[k], 32 * (i + 1))
                        dve.scalar_tensor_tensor(part[:, e % 2, :], bank[4 + e % 2][:], m.unscale[:, 0:1], d[:, k, e, :],
                                                 ALU.mult, ALU.mult)\
                           .then_inc(s["part_ready"], 1)

                    for e in range(E):
                        hidden(2 * e)
                        hidden(2 * e + 1)
                        if e:
                            gather(e - 1)
                    gather(E - 1)



def param_views(m):
    views = {}
    for chunk, cols in LAYOUT.items():
        at = 0
        for name, n in cols.items():
            views[name] = m.chunk[chunk][:, at:at + n]
            at += n
    return views


def build(nc, x, dram, out):
    m = Mem()
    m.x, m.dram, m.out = x, dram, out
    with ExitStack() as c:
        m.chunk = {n: c.enter_context(nc.sbuf_tensor(f"par_{n}", [P, widths(n)], F32)) for n in LAYOUT}
        m.w12 = c.enter_context(nc.sbuf_tensor("w12", [P, 2 * E * HID], F32))
        m.w3 = c.enter_context(nc.sbuf_tensor("w3", [P, E * C], F32))
        m.xpad = c.enter_context(nc.sbuf_tensor("xpad", [P, (HB + 1) * PADI + 2 * PADW + 2], F32))
        m.xa = c.enter_context(nc.sbuf_tensor("xa", [P, COLS], F32))
        m.bank = [c.enter_context(nc.psum_tensor(f"bank{k}", [P, TW], F32)) for k in range(8)]
        m.conv0_landed = c.enter_context(nc.semaphore("conv0_landed"))
        m.attn_landed = c.enter_context(nc.semaphore("attn_landed"))
        m.rest_landed = c.enter_context(nc.semaphore("rest_landed"))
        m.moe_landed = c.enter_context(nc.semaphore("moe_landed"))
        m.par = param_views(m)
        m.eps5 = m.par["eps5"]
        conv_ffn_stage(nc, m, 0, m.xa)
        attention_stage(nc, m, m.xa)
        m.stats = c.enter_context(nc.sbuf_tensor("stats", [P, HB, 6], F32))
        m.wrange = c.enter_context(nc.sbuf_tensor("wrange", [P, 2], F32))
        m.wscale = c.enter_context(nc.sbuf_tensor("wscale", [P, 1], F32))
        m.unscale = c.enter_context(nc.sbuf_tensor("unscale", [P, 1], F32))
        conv_ffn_stage(nc, m, 1, m.xa, m.stats)
        weight_scale_stage(nc, m)
        whiten_stage(nc, m)
        m.xn = m.xpad[:, 0:COLS]

        def normed(t):
            return tile_of(m.xn, t).rearrange("p (b t) -> p b t", b=2)

        layer_norm_stage(nc, m, "ln2", normed)
        slice_attention_stage(nc, m)
        m.wp = [c.enter_context(nc.sbuf_tensor(f"wp{q}", [P, 2 * E * HID], F16)) for q in range(2)]
        CH = 8 * HB
        with nc.sbuf_tensor("xn_steps", [P, COLS + CH], F32) as xn_steps:
            m.xn_steps = xn_steps

            def normed_by_step(t):
                return xn_steps[:, 0:COLS].rearrange("p (t b) -> p b t", b=HB)[:, 2 * t:2 * t + 2, :]

            layer_norm_stage(nc, m, "ln3", normed_by_step)
            lstm_stage(nc, m)
        layer_norm_stage(nc, m, "ln4", normed)
        sigmoid_attention_stage(nc, m)
        m.route = nc.dram_tensor("route", (2, E, TILES, TW), F32, kind="Internal").ap()
        m.xs = [c.enter_context(nc.sbuf_tensor(f"xs{h}", [P, COLS], F16)) for h in range(2)]
        route_stage(nc, m)
        expert_stage(nc, m)


def both(w, cols=None):
    o = np.zeros((2 * w.shape[0], 2 * w.shape[1]), w.dtype)
    o[:w.shape[0], :w.shape[1]] = w
    o[w.shape[0]:, w.shape[1]:] = w
    return o


def twice(v):
    return np.concatenate([v, v], 0)


def rows(v):
    return np.ascontiguousarray(np.broadcast_to(v[None, :], (P, v.size)))


def by_half(w):
    o = np.zeros((P, 2 * w.shape[1]), w.dtype)
    o[:C, :w.shape[1]] = w
    o[C:, w.shape[1]:] = w
    return o


def out_by_half(w):
    o = np.zeros((w.shape[0], 2 * P), w.dtype)
    o[:, :C] = w
    o[:, P + C:] = w
    return o


def padded_rows(a, n=P):
    o = np.zeros((n, a.shape[1]), a.dtype)
    o[:a.shape[0]] = a
    return o


def lay_out(v):
    f = np.float32
    q = {}
    for n in (0, 1):
        q[f"dw{n}_w"] = twice(v[f"L0_conv_dw{n}_w"].reshape(C, 9))
        q[f"dw{n}_s"] = twice(v[f"L0_conv_dw{n}_s"][:, None])
        q[f"dw{n}_b"] = twice(v[f"L0_conv_dw{n}_b"][:, None])
        q[f"f{n}_w1"] = by_half(v[f"L0_conv_f{n}_w1"][:, :, 0, 0].T)
        q[f"f{n}_s1"] = v[f"L0_conv_f{n}_s1"][:, None]
        q[f"f{n}_b1"] = v[f"L0_conv_f{n}_b1"][:, None]
        q[f"f{n}_w2"] = out_by_half(v[f"L0_conv_f{n}_w2"][:, :, 0, 0].T)
        q[f"f{n}_s2"] = twice(v[f"L0_conv_f{n}_s2"][:, None])
        q[f"f{n}_b2"] = twice(v[f"L0_conv_f{n}_b2"][:, None])
    q["wq"] = both(v["L0_conv_wq"].T)
    q["wk"] = both(v["L0_conv_wkv"][:C].T)
    q["wv"] = both(v["L0_conv_wkv"][C:].T)
    q["scale"] = rows(np.tile(v["L0_conv_scale_p"].reshape(C), 2))
    pos = np.zeros((P, P), f)
    for a in range(2):
        for h in range(2):
            pos[SLOT * a:SLOT * a + WR * WR, C * h:C * h + C] = v["L0_conv_pos"][0]
    q["pos"] = pos
    toep = np.zeros((P, HD, P), f)
    w = v["L0_conv_dwc_w"][:, 0]
    for ro in range(WR):
        for co in range(WR):
            for ky in range(5):
                for kx in range(5):
                    ri, ci = ro + ky - 2, co + kx - 2
                    if 0 <= ri < WR and 0 <= ci < WR:
                        for a in range(2):
                            toep[SLOT * a + ri * WR + ci, :, SLOT * a + ro * WR + co] = w[:, ky, kx]
    q["toep"] = toep.reshape(P, HD * P)
    q["dwc_b"] = np.tile(v["L0_conv_dwc_b"], 2 * NH)[:, None]
    q["proj"] = both(v["L0_conv_proj_w"].T)
    q["proj_b"] = twice(v["L0_conv_proj_b"][:, None])
    i = np.arange(P)
    q["ident"] = np.eye(P, dtype=f)
    q["headmask"] = (i[:, None] // HD == i[None, :] // HD).astype(f)
    q["headind"] = (i[:, None] // HD == np.arange(2 * NH)[None, :]).astype(f)
    valid = (i % SLOT < WR * WR).astype(f)
    q["slots"] = np.stack([valid * (i < SLOT), valid * (i >= SLOT)], 1).astype(f)
    same = (i[:, None] // C == i[None, :] // C).astype(f)
    q["mean"] = same / f(C)
    q["center"] = np.eye(P, dtype=f) - same / f(C)
    half = (i[:, None] // C == np.arange(8)[None, :] % 2)
    tile = np.arange(8)[None, :] // 2
    q["var_rows"] = np.concatenate([(half & (tile == k)) / f(C) for k in range(4)], 1).astype(f)
    q["spread"] = np.concatenate([padded_rows((half & (tile == k)).T.astype(f)) for k in range(4)], 1)
    q["pair"] = (i[:, None] // 2 == i[None, :] // 2).astype(f) / f(2)
    q["fold"] = (i[:, None] % C == i[None, :] % C).astype(f)
    q["group16"] = q["headmask"]
    q["fc1"] = both(v["L1_conv_fc1_w"].T)
    q["ln_g"] = rows(np.tile(v["L1_conv_ln_g"], 2))
    q["ln_b"] = rows(np.tile(v["L1_conv_ln_b"], 2))
    q["fc2"] = padded_rows(both(v["L1_conv_fc2_w"].T))
    q["x_weight"] = np.repeat(v["L1_conv_x_weight"], P)[:, None]
    q["w_x"] = by_half(v["L2_attn_W_x"].T)
    q["b_x"] = v["L2_attn_b_x"][:, None]
    q["b_x_row"] = rows(np.tile(v["L2_attn_b_x"], 2))
    q["w_slice"] = heads8(v["L2_attn_W_slice"].T)
    q["b_slice"] = np.tile(v["L2_attn_b_slice"], 8)[:, None]
    q["w_temp"] = heads8(np.repeat(v["L2_attn_W_temp"].T, 16, 1))
    q["b_temp"] = np.repeat(v["L2_attn_b_temp"], P)[:, None]
    q["w_out"] = out_by_half(v["L2_attn_W_out"].T)
    q["b_out"] = twice(v["L2_attn_b_out"][:, None])
    lstm_b = np.zeros((3, P), f)
    for n, g in enumerate(("i", "c", "o")):
        q["u_" + "igo"[n]] = both(v[f"L2_ffn_U_{g}"])
        q["v_" + "igo"[n]] = both(v[f"L2_ffn_V_{g}"])
        lstm_b[n] = np.tile(v[f"L2_ffn_b_{g}"], 2)
    q["lstm_b"] = padded_rows(lstm_b)
    q["lstm_half"] = padded_rows(np.array([[0.5], [1.0], [0.5]], f))
    q["eps5"] = np.full((P, 1), 1e-5, f)
    q["gate_sel"] = padded_rows(np.tile(np.repeat(np.eye(3, dtype=f), HB, 1), (1, 8)))
    q["q_w"] = both(v["L3_attn_q_weight"])
    q["gate_w"] = both(v["L3_ffn_gate_w"])
    q["gate_b"] = rows(np.tile(v["L3_ffn_gate_b"], 2))
    q["idx_w"] = rows(np.tile(np.arange(E, 0, -1), 2).astype(f))
    arrays = {}
    for chunk, cols in LAYOUT.items():
        for name, n in cols.items():
            assert q[name].shape == (P, n), (name, q[name].shape)
        arrays[chunk] = np.concatenate([q[name] for name in cols], 1)
    w12 = np.stack([v["L3_ffn_w1"], v["L3_ffn_w2"]], 1).transpose(2, 0, 1, 3).reshape(C, 2 * E * HID)
    arrays["w12"] = twice(w12)
    arrays["w3"] = v["L3_ffn_w3"].transpose(1, 0, 2).reshape(HID, E * C)
    return {n: np.ascontiguousarray(a) for n, a in arrays.items()}


def heads8(w):
    o = np.zeros((P, P), w.dtype)
    for h in range(8):
        o[16 * h:16 * h + 16, 16 * h:16 * h + 16] = w
    return o


def kernel(**inputs):
    import concourse.bacc as bacc
    from concourse.bass_utils import run_bass_kernel_spmd

    v = {n: np.ascontiguousarray(a) for n, a in inputs.items()}
    nc = bacc.Bacc("TRN2", target_bir_lowering=False, num_devices=1)
    arrays = {"in_x": v["x"].reshape(B, C, HW)}
    arrays.update({f"in_{n}": a for n, a in lay_out(v).items()})
    aps = {n: nc.dram_tensor(n, a.shape, mybir.dt.from_np(a.dtype), kind="ExternalInput").ap()
           for n, a in arrays.items()}
    out = nc.dram_tensor("out", (B, C, HW), F32, kind="ExternalOutput").ap()
    build(nc, aps["in_x"], {n[3:]: a for n, a in aps.items() if n != "in_x"}, out)
    r = run_bass_kernel_spmd(nc, [arrays], core_ids=[0])
    return r.results[0]["out"].reshape(B, C, SIDE, SIDE)
```

```python
from contextlib import ExitStack

import numpy as np

import concourse.bass as bass
from concourse import mybir

ALU = mybir.AluOpType
ACT = mybir.ActivationFunctionType
AXX = mybir.AxisListType.X
F32 = mybir.dt.float32
F16 = mybir.dt.float16
BF16 = mybir.dt.bfloat16

P = 128
C = 64
B = 32
HB = B // 2
SIDE = 16
HW = SIDE * SIDE
COLS = HB * HW
TW = 512
TILES = COLS // TW
PADW = SIDE + 1
PADI = PADW * PADW
WR = 7
NWIN = 9
SLOT = 64
NH = 4
HD = 16
HEADS = 8
E = 16
HID = 128
SEG = [(0, 7), (7, 7), (14, 2)]
XSCALE = 2.0 ** 10

LAYOUT = {
    "conv0": dict(ident=128, dw0_w=9, dw0_s=1, dw0_b=1, f0_w1=256, f0_s1=1, f0_b1=1, f0_w2=64, f0_s2=1,
                  f0_b2=1),
    "attn": dict(wq=128, wk=128, wv=128, scale=128, pos=128, toep=16 * 128, dwc_b=1, proj=128, proj_b=1,
                 headmask=128, headind=8, slots=2),
    "rest": dict(dw1_w=9, dw1_s=1, dw1_b=1, f1_w1=256, f1_s1=1, f1_b1=1, f1_w2=64, f1_s2=1, f1_b2=1,
                 center=128, mean=128, var_rows=4 * 8, spread=4 * 128, pair=128, fold=128, group16=128, fc1=32, ln_g=32, ln_b=32, fc2=128,
                 x_weight=1, eps5=1, lstm_half=1, w_x=256, b_x=1, w_slice=128, b_slice=1,
                 temp_rows=2 * 2 * HEADS, temp_spread=256, b_temp=1,
                 w_out=256, b_out=1, u_i=128, u_g=128, u_o=128, v_i=128, v_g=128, v_o=128,
                 lstm_b=128, gate_sel=384, q_w=128, gate_w=32, gate_b=32, idx_w=32),
}


def widths(chunk):
    return sum(LAYOUT[chunk].values())


class StageSemaphores:

    def __init__(self, nc, prefix):
        self.nc, self.prefix, self.made = nc, prefix, []

    def __call__(self, name):
        self.made.append(self.nc.alloc_semaphore(f"{self.prefix}_{name}"))
        return self.made[-1]

    def __enter__(self):
        return self

    def __exit__(self, *_):
        self.nc.clear_and_free_semaphores(self.made)
        self.nc.all_engine_barrier()


class Mem:
    pass


def tile_of(ap, t):
    return ap[:, bass.ds(t * TW, TW)]


def padded(ap, t, dy, dx):
    off = (1 + dy) * PADW + 1 + dx
    v = ap[:, bass.ds(t * (2 * PADI) + off, 2 * PADI)]
    return v.rearrange("p (a r c) -> p a r c", a=2, r=PADW)[:, :, 0:SIDE, 0:SIDE]


def conv_ffn_stage(nc, m, layer, out, stats=None):
    p = m.par
    dw_w, dw_s, dw_b = (p[f"dw{layer}_{n}"] for n in "wsb")
    w1, s1, b1 = (p[f"f{layer}_{n}"] for n in ("w1", "s1", "b1"))
    w2, s2, b2 = (p[f"f{layer}_{n}"] for n in ("w2", "s2", "b2"))
    DVE_TAPS = range(1, 6)
    PE_TAPS = range(6, 9)
    with ExitStack() as c:
        def sb(name, shape, dt=F32):
            return c.enter_context(nc.sbuf_tensor(f"L{layer}_{name}", shape, dt))

        sem = c.enter_context(StageSemaphores(nc, f"L{layer}"))

        taps = sb("taps", [P, 9])
        diag = sb("diag", [P, len(PE_TAPS), P])
        acc = sb("acc", [P, 2, 2 * PADW * SIDE])
        hid = sb("hid", [P, 2, 2, TW])
        branch = sb("branch", [P, 2, TW])
        if layer == 0:
            xin = sb("xin", [P, COLS])
        taps_ready, diag_ready = sem("taps_ready"), sem("diag_ready")
        x_landed = [sem(f"x_landed{g}") for g in range(4)]
        pad_zeroed, pad_ready = sem("pad_zeroed"), sem("pad_ready")
        acc_ready, tap_step = sem("acc_ready"), sem("tap_step")
        conv_done, y_ready, up_done, hid_ready = sem("conv_done"), sem("y_ready"), sem("up_done"), sem("hid_ready")
        down_done, branch_ready, out_ready, stat_ready = (sem("down_done"), sem("branch_ready"),
                                                          sem("out_ready"), sem("stat_ready"))
        block = c.enter_context(nc.Block())
        PAIRS = TILES // 2

        def images(ap):
            return ap.rearrange("p (a r c) -> p a r c", a=2, r=SIDE)

        def shifted(t, q):
            return padded(m.xpad, t, q // 3 - 1, q % 3 - 1)

        def rows_of(t, q):
            off = (q // 3) * PADW + q % 3
            v = m.xpad[:, bass.ds(t * (2 * PADI) + off, 2 * PADI)].rearrange("p (r c) -> p r c", c=PADW)
            return v[:, 0:2 * SIDE + 1, 0:SIDE]

        def acc_rows(k):
            return acc[:, k, 0:(2 * SIDE + 1) * SIDE].rearrange("p (r c) -> p r c", c=SIDE)

        if layer == 0:
            @block.sync
            def _(sp):
                xd = m.x.rearrange("(h g b) c n -> g h c b n", h=2, b=4)
                for g in range(4):
                    if g == 0:
                        sp.dma_start(m.chunk["conv0"][:], m.dram["conv0"]).then_inc(m.conv0_landed, 16)
                    for h in range(2):
                        sp.dma_start(xin[C * h:C * h + C, g * 1024:(g + 1) * 1024].rearrange(
                            "p (b n) -> p b n", b=4), xd[g, h]).then_inc(x_landed[g], 16)
                for name, s in (("attn", m.attn_landed), ("rest", m.rest_landed)):
                    sp.dma_start(m.chunk[name][:], m.dram[name]).then_inc(s, 16)
                sp.dma_start(m.w12[:], m.dram["w12"]).then_inc(m.moe_landed, 16)
                sp.dma_start(m.w3[:], m.dram["w3"]).then_inc(m.moe_landed, 16)

        @block.gpsimd
        def _(pool):
            if layer == 0:
                pool.memset(m.xpad[:], 0.0).then_inc(pad_zeroed, 1)
                pool.wait_ge(pad_zeroed, 1)
                for g in range(4):
                    pool.wait_ge(x_landed[g], 32)
                    for a in range(2):
                        t = 2 * g + a
                        pool.tensor_copy(padded(m.xpad, t, 0, 0), images(xin[:, t * TW:(t + 1) * TW]))\
                            .then_inc(pad_ready, 1)

        @block.tensor
        def _(pe):
            def conv(i):
                for k in range(2):
                    t = 2 * i + k
                    if layer == 0:
                        pe.wait_ge(pad_ready, t + 1)
                    pe.wait_ge(y_ready, t + 1)
                    for n, q in enumerate(PE_TAPS):
                        mm = pe.matmul(m.bank[k][:], diag[:, n, :], shifted(t, q), start=(n == 0),
                                       stop=(n == len(PE_TAPS) - 1))
                    mm.then_inc(conv_done, 1)

            def up(i):
                for k in range(2):
                    t = 2 * i + k
                    pe.wait_ge(y_ready, t + 3)
                    for h in range(2):
                        pe.wait_ge(hid_ready, 2 * t + h + 1)
                        pe.matmul(m.bank[2 + 2 * k + h][:], w1[:, h * HID:(h + 1) * HID], tile_of(out, t),
                                  start=True, stop=True).then_inc(up_done, 1)

            def down(i):
                for k in range(2):
                    t = 2 * i + k
                    pe.wait_ge(branch_ready, t + 1)
                    for h in range(2):
                        pe.wait_ge(hid_ready, 2 * t + h + 5)
                        mm = pe.matmul(m.bank[6 + k][C * h:C * (h + 1), :], w2, hid[:, k, h, :],
                                       start=True, stop=True)
                    mm.then_inc(down_done, 1)

            pe.wait_ge(diag_ready, len(PE_TAPS))
            conv(0)
            with pe.Fori(0, PAIRS - 1) as i:
                up(i)
                conv(i + 1)
                down(i)
            up(PAIRS - 1)
            down(PAIRS - 1)

        @block.scalar
        def _(act):
            def first_tap(i):
                for k in range(2):
                    t = 2 * i + k
                    if layer == 0:
                        act.wait_ge(pad_ready, t + 1)
                    act.wait_ge(y_ready, t + 1)
                    act.activation(acc_rows(k), rows_of(t, 0), ACT.Identity, bias=dw_b[:, 0:1],
                                   scale=taps[:, 0:1]).then_inc(acc_ready, 1)

            def hidden(i):
                for k in range(2):
                    t = 2 * i + k
                    act.wait_ge(down_done, t + 1)
                    for h in range(2):
                        act.wait_ge(up_done, 2 * t + h + 1)
                        act.activation(hid[:, k, h, :], m.bank[2 + 2 * k + h][:], ACT.Relu, bias=b1[:, 0:1],
                                       scale=s1[:, 0:1]).then_inc(hid_ready, 1)

            def ffn_out(i):
                for k in range(2):
                    t = 2 * i + k
                    act.wait_ge(down_done, t + 3)
                    act.wait_ge(out_ready, t + 1)
                    act.activation(branch[:, k, :], m.bank[6 + k][:], ACT.Identity, bias=b2[:, 0:1],
                                   scale=s2[:, 0:1]).then_inc(branch_ready, 1)

            act.sem_inc(hid_ready, 4)
            act.sem_inc(branch_ready, 2)
            if layer == 0:
                act.wait_ge(m.conv0_landed, 16)
            else:
                act.wait_ge(m.rest_landed, 16)
            act.wait_ge(taps_ready, 1)
            first_tap(0)
            with act.Fori(0, PAIRS - 1) as i:
                first_tap(i + 1)
                hidden(i)
                ffn_out(i)
            hidden(PAIRS - 1)
            ffn_out(PAIRS - 1)

        @block.vector
        def _(dve):
            def conv(i):
                N = 2 * len(DVE_TAPS)
                for n, q in enumerate(DVE_TAPS):
                    for k in range(2):
                        t = 2 * i + k
                        if n == 0:
                            dve.wait_ge(acc_ready, t + 1)
                        else:
                            dve.wait_ge(tap_step, N * i + 2 * (n - 1) + k + 1)
                        dve.scalar_tensor_tensor(acc_rows(k), rows_of(t, q), taps[:, q:q + 1], acc_rows(k),
                                                 ALU.mult, ALU.add).then_inc(tap_step, 1)
                for k in range(2):
                    t = 2 * i + k
                    dve.wait_ge(conv_done, t + 1)
                    dve.wait_ge(tap_step, N * i + N - 1 + k)
                    a = acc[:, k, :].rearrange("p (a r c) -> p a r c", a=2, r=PADW)[:, :, 0:SIDE, :]
                    dve.tensor_tensor(images(tile_of(out, t)), images(m.bank[k][:]), a, ALU.add).then_inc(y_ready, 1)

            def finish(i):
                for k in range(2):
                    t = 2 * i + k
                    dve.wait_ge(branch_ready, t + 3)
                    y = tile_of(out, t)
                    dve.tensor_tensor(y, branch[:, k, :], y, ALU.add).then_inc(out_ready, 1)
                for k in range(2):
                    t = 2 * i + k
                    if stats is not None:
                        dve.wait_ge(out_ready, t + 3)
                        for a in range(2):
                            o = out[:, bass.ds(t * TW + a * HW, HW)]
                            dve.bn_stats(stats[:, bass.ds(t * 2 + a, 1), :], o).then_inc(stat_ready, 1)

            dve.sem_inc(y_ready, 2)
            dve.sem_inc(down_done, 2)
            dve.sem_inc(out_ready, 2)
            if layer == 0:
                dve.wait_ge(m.conv0_landed, 16)
            else:
                dve.wait_ge(m.rest_landed, 16)
            dve.tensor_scalar(taps[:], dw_w, dw_s[:, 0:1], None, ALU.mult).then_inc(taps_ready, 1)
            dve.wait_ge(taps_ready, 1)
            dve.tensor_scalar(taps[:, 4:5], taps[:, 4:5], 1.0, None, ALU.add).then_inc(taps_ready, 1)
            dve.wait_ge(taps_ready, 2)
            for n, q in enumerate(PE_TAPS):
                dve.tensor_scalar(diag[:, n, :], p["ident"], taps[:, q:q + 1], None, ALU.mult)\
                   .then_inc(diag_ready, 1)
            conv(0)
            with dve.Fori(0, PAIRS - 1) as i:
                conv(i + 1)
                finish(i)
            finish(PAIRS - 1)


def region(ap3, wi, wj, windowed):
    (r0, nr), (c0, ncol) = SEG[wi], SEG[wj]
    if windowed:
        v = ap3.rearrange("p (a s) -> p a s", a=2)[:, :, 0:WR * WR].rearrange("p a (r c) -> p a r c", r=WR)
        return v[:, :, 0:nr, 0:ncol]
    return ap3.rearrange("p (a r c) -> p a r c", a=2, r=SIDE)[:, :, r0:r0 + nr, c0:c0 + ncol]


def attention_stage(nc, m, x2):
    p = m.par
    U = 2 * NWIN
    UW = U * P
    KVW = 2 * P + 2
    YW = P + 2 * NH
    with ExitStack() as c:
        def sb(name, shape, dt=F32):
            return c.enter_context(nc.sbuf_tensor(f"att_{name}", shape, dt))

        sem = c.enter_context(StageSemaphores(nc, "att"))

        sc = sb("sc", [P, 4, P])
        inv_sc = sb("inv_sc", [P, P])
        wq, wk, pos, floor = sb("wq", [P, P]), sb("wk", [P, P]), sb("pos", [P, 3 * P]), sb("floor", [P, P])
        bias = sb("bias", [P, 1])
        xw = sb("xw", [P, U, P])
        base = sb("base", [P, 2, 3 * P])
        sqa, cube, sqb = sb("sqa", [P, 2, 3 * P]), sb("cube", [P, 2, 3 * P]), sb("sqb", [P, 2, 3 * P])
        norms, roots, factor = sb("norms", [P, 2, 12]), sb("roots", [P, 2, 12]), sb("factor", [P, 2, 12])
        kq = sb("kq", [P, 2, 2, 3 * P])
        val = sb("val", [P, U, P])
        valz = sb("valz", [P, U, KVW + 2])
        kvm = sb("kvm", [P, 3, 2, YW])
        qt = sb("qt", [P, 3, P])
        den = sb("den", [P, 2, 3, 2 * NH])
        ysum = sb("ysum", [P, U, P])
        conv = sb("conv", [P, U, P])
        yt = sb("yt", [P, UW])
        proj = sb("proj", [P, UW])
        names = ("ready0 act_ready0 zeroed ind xw_ready qkv_done base_ready sqa_ready cube_ready s2_ready "
                 "sqb_ready s6_ready root_ready inv_ready factor_ready kq_ready v_ready kv_done kvm_ready "
                 "qt_done qt_ready y_done den_ready ysum_ready conv_done conv_ready conv_added yt_done yt_ready proj_done "
                 "proj_ready out_ready").split()
        s = {n: sem(n) for n in names}
        block = c.enter_context(nc.Block())
        bank = m.bank
        kv_bank = [3, 4, 7]
        chunks = [(0, 4), (4, 4), (8, 4), (12, 4), (16, 2)]
        yt_bank = [3, 4, 5, 7, 6]

        @block.gpsimd
        def _(pool):
            pool.sem_inc(s["out_ready"], 1)
            pool.memset(xw[:], 0.0).then_inc(s["zeroed"], 1)
            pool.memset(valz[:], 0.0).then_inc(s["zeroed"], 1)
            pool.wait_ge(s["zeroed"], 2)
            pool.wait_ge(m.attn_landed, 16)
            for u in range(U):
                pool.tensor_copy(valz[:, u, 2 * P:KVW], p["slots"]).then_inc(s["ind"], 1)

            def windows(i):
                pool.wait_ge(s["qkv_done"], 6 * i + 1)
                for u in range(U):
                    k, w = u // NWIN, u % NWIN
                    pool.tensor_copy(region(xw[:, u, :], w // 3, w % 3, True),
                                     region(tile_of(x2, 2 * i + k), w // 3, w % 3, False))\
                        .then_inc(s["xw_ready"], 1)

            def add_up(i):
                for u in range(U):
                    j = min(u // 4, 4)
                    if u % 4 == 0:
                        pool.wait_ge(s["proj_ready"], 5 * i + j + 2)
                    k, w = u // NWIN, u % NWIN
                    (r0, nr), (c0, ncol) = SEG[w // 3], SEG[w % 3]
                    pool.tensor_tensor(padded(m.xpad, 2 * i + k, 0, 0)[:, :, r0:r0 + nr, c0:c0 + ncol],
                                       region(proj[:, u * P:(u + 1) * P], w // 3, w % 3, True),
                                       region(tile_of(x2, 2 * i + k), w // 3, w % 3, False), ALU.add)\
                        .then_inc(s["out_ready"], 1)

            windows(0)
            with pool.Fori(0, TILES // 2 - 1) as i:
                windows(i + 1)
                add_up(i)
            add_up(TILES // 2 - 1)

        @block.tensor
        def _(pe):
            pe.sem_inc(s["yt_done"], 1)
            pe.sem_inc(s["qt_done"], 1)
            pe.sem_inc(s["y_done"], 3)
            pe.sem_inc(s["kv_done"], 1)
            pe.sem_inc(s["conv_done"], 1)
            pe.sem_inc(s["qkv_done"], 1)
            def qkv(i, g, units=(0, 1, 2)):
                if 0 in units:
                    pe.wait_ge(s["xw_ready"], U * i + 3 * g + 3)
                    pe.wait_ge(s["base_ready"], 6 * i + g + 1)
                    pe.wait_ge(s["v_ready"], 6 * i + g + 1)
                    pe.matmul(bank[0][:, 0:3 * P], p["ident"], pos[:], start=True, stop=False, skip_group_check=True)
                for u in units:
                    x = xw[:, 3 * g + u, :]
                    o = slice(u * P, (u + 1) * P)
                    pe.matmul(bank[0][:, o], x, wk[:], start=False, stop=True, skip_group_check=True)
                    pe.matmul(bank[1][:, o], x, wq[:], start=True, stop=True)
                    mm = pe.matmul(bank[2][:, o], x, p["wv"], start=True, stop=True)
                if 2 in units:
                    mm.then_inc(s["qkv_done"], 1)

            def kv_and_turn(i, n):
                g, u = n // 3, n % 3
                pe.wait_ge(s["kq_ready"], 6 * i + g + 1)
                pe.wait_ge(s["kvm_ready"], U * i + n + 1)
                pe.matmul(bank[kv_bank[n % 3]][:, 0:KVW], kq[:, g % 2, 0, u * P:(u + 1) * P], valz[:, n, 0:KVW],
                          start=True, stop=True).then_inc(s["kv_done"], 1)
                pe.wait_ge(s["qt_ready"], U * i + n + 1)
                pe.transpose(bank[5][:, 0:P], kq[:, g % 2, 1, u * P:(u + 1) * P], p["ident"])\
                  .then_inc(s["qt_done"], 1)

            def attend(i, n):
                pe.wait_ge(s["kvm_ready"], U * i + n + 4)
                pe.wait_ge(s["qt_ready"], U * i + n + 2)
                if n % 3 == 0:
                    pe.wait_ge(s["ysum_ready"], 6 * i + n // 3 + 1)
                for a in range(2):
                    o = bank[6][SLOT * a:SLOT * (a + 1), (n % 3) * YW:(n % 3 + 1) * YW]
                    mm = pe.matmul(o, qt[:, n % 3, SLOT * a:SLOT * (a + 1)], kvm[:, n % 3, a, :],
                                   start=True, stop=True)
                mm.then_inc(s["y_done"], 1)

            pe.wait_ge(s["inv_ready"], 4)
            pe.wait_ge(m.attn_landed, 16)
            pe.matmul(bank[7][:, 0:1], p["proj"], p["dwc_b"], start=True, stop=True).then_inc(s["ready0"], 1)
            pe.wait_ge(s["ind"], U)
            pe.wait_ge(s["act_ready0"], 5)

            def convolve(i, dg):
                pe.wait_ge(s["conv_ready"], 8 * i + dg + 1)
                for e in range(2):
                    d = 2 * dg + e
                    rhs = val[:].rearrange("p u (n d) -> p (u n) d", d=HD)[:, :, d]
                    mm = pe.matmul(bank[dg % 3][:, e * 144:(e + 1) * 144],
                                   p["toep"][:, d * P:(d + 1) * P], rhs, start=True, stop=True)
                mm.then_inc(s["conv_done"], 1)

            def iteration(i, last):
                qkv(i, 1)
                pe.wait_ge(s["proj_ready"], 5 * i + 1)
                for g in range(6):
                    if g == 4:
                        pe.wait_ge(s["v_ready"], 6 * i + 7)
                        pe.wait_ge(s["base_ready"], 6 * i + 7)
                    for u in range(3):
                        kv_and_turn(i, 3 * g + u)
                    for u in range(3):
                        if g < 4:
                            qkv(i, g + 2, (u,))
                        else:
                            convolve(i, 4 * (g - 4) + u)
                        attend(i, 3 * g + u)
                    if g >= 4:
                        convolve(i, 4 * (g - 4) + 3)
                if not last:
                    pe.wait_ge(s["conv_ready"], 8 * i + 8 + 3)
                    qkv(i + 1, 0)
                pe.wait_ge(s["qt_ready"], U * i + U + 1)
                pe.wait_ge(s["kvm_ready"], U * i + U + 3)
                for j, (u0, nu) in enumerate(chunks):
                    pe.wait_ge(s["conv_added"], 5 * i + j + 2)
                    for u in range(nu):
                        mm = pe.transpose(bank[yt_bank[j]][:, u * P:(u + 1) * P], ysum[:, u0 + u, :], p["ident"])
                    mm.then_inc(s["yt_done"], 1)
                for j, (u0, nu) in enumerate(chunks):
                    pe.wait_ge(s["yt_ready"], 5 * i + j + 1)
                    pe.matmul(bank[yt_bank[j]][:, 0:nu * P], p["proj"], yt[:, u0 * P:(u0 + nu) * P],
                              start=True, stop=True).then_inc(s["proj_done"], 1)

            qkv(0, 0)
            with pe.Fori(0, TILES // 2 - 1) as i:
                iteration(i, False)
            iteration(TILES // 2 - 1, True)

        @block.scalar
        def _(act):
            act.sem_inc(s["proj_ready"], 1)
            act.sem_inc(s["v_ready"], 1)
            act.sem_inc(s["conv_ready"], 3)
            act.sem_inc(s["qt_ready"], 1)
            act.wait_ge(m.attn_landed, 16)
            act.activation(sc[:, 0, :], p["scale"], ACT.Abs).then_inc(s["act_ready0"], 1)
            act.wait_ge(s["act_ready0"], 1)
            act.activation(sc[:, 1, :], sc[:, 0, :], ACT.Exp, scale=-1.0).then_inc(s["act_ready0"], 1)
            act.wait_ge(s["act_ready0"], 2)
            act.activation(sc[:, 2, :], sc[:, 1, :], ACT.Ln, bias=1.0).then_inc(s["act_ready0"], 1)
            act.activation(sc[:, 3, :], p["scale"], ACT.Relu).then_inc(s["act_ready0"], 1)
            act.wait_ge(s["ready0"], 1)
            act.activation(bias[:], bank[7][:, 0:1], ACT.Identity, bias=p["proj_b"][:, 0:1])\
               .then_inc(s["act_ready0"], 1)
            act.activation(sc[:, 0, 0:1], sc[:, 3, 0:1], ACT.Sqrt).then_inc(s["act_ready0"], 1)
            act.wait_ge(s["act_ready0"], 6)

            def values(i, g):
                act.wait_ge(s["qkv_done"], 6 * i + g + 2)
                if g == 0:
                    act.wait_ge(s["conv_done"], 8 * i + 1)
                    act.wait_ge(s["kv_done"], U * i + 1)
                v3 = bank[2][:, 0:3 * P].rearrange("p (u n) -> p u n", u=3)
                act.activation(val[:, 3 * g:3 * g + 3, :], v3, ACT.Copy)
                act.activation(valz[0:SLOT, 3 * g:3 * g + 3, 0:P], v3[0:SLOT], ACT.Copy)
                act.activation(valz[SLOT:P, 3 * g:3 * g + 3, P:2 * P], v3[SLOT:P], ACT.Copy)\
                   .then_inc(s["v_ready"], 1)

            def turned(i, n):
                act.wait_ge(s["qt_done"], U * i + n + 2)
                act.wait_ge(s["y_done"], U * i + n + 1)
                act.activation(qt[:, n % 3, :], bank[5][:, 0:P], ACT.Copy).then_inc(s["qt_ready"], 1)

            def square_base(i, g):
                act.wait_ge(s["base_ready"], 6 * i + g + 2)
                act.activation(sqa[:], base[:], ACT.Square).then_inc(s["sqa_ready"], 1)

            def square_cube(i, g):
                act.wait_ge(s["cube_ready"], 6 * i + g + 1)
                act.activation(sqb[:], cube[:], ACT.Square).then_inc(s["sqb_ready"], 1)

            def root(i, g):
                act.wait_ge(s["s2_ready"], 6 * i + g + 1)
                act.wait_ge(s["s6_ready"], 6 * i + g + 1)
                act.activation(roots[:], norms[:], ACT.Sqrt).then_inc(s["root_ready"], 1)

            act.wait_ge(s["ind"], U)

            def convolved(i, dg):
                if dg == 0:
                    act.wait_ge(s["conv_added"], 5 * i + 1)
                act.wait_ge(s["conv_done"], 8 * i + dg + 2)
                act.activation(conv[:].rearrange("p u (n d) -> p d (u n)", d=HD)[:, 2 * dg:2 * dg + 2, :],
                               bank[dg % 3][:, 0:288].rearrange("p (e n) -> p e n", e=2), ACT.Copy)\
                   .then_inc(s["conv_ready"], 1)

            def iteration(i, last):
                for g in range(6):
                    if g < 5:
                        values(i, g + 1)
                        square_base(i, g + 1)
                    turned(i, 3 * g)
                    turned(i, 3 * g + 1)
                    turned(i, 3 * g + 2)
                    if g == 4:
                        convolved(i, 0)
                    if g < 5:
                        square_cube(i, g + 1)
                        root(i, g + 1)
                    if g == 4:
                        for dg in range(1, 4):
                            convolved(i, dg)
                    elif g == 5:
                        for dg in range(4, 8):
                            convolved(i, dg)
                if not last:
                    values(i + 1, 0)
                for j, (u0, nu) in enumerate(chunks):
                    act.wait_ge(s["yt_done"], 5 * i + j + 2)
                    act.activation(yt[:, u0 * P:(u0 + nu) * P], bank[yt_bank[j]][:, 0:nu * P], ACT.Copy)\
                       .then_inc(s["yt_ready"], 1)
                if not last:
                    square_base(i + 1, 0)
                act.wait_ge(s["out_ready"], U * i + 1)
                for j, (u0, nu) in enumerate(chunks):
                    if j == 2 and not last:
                        square_cube(i + 1, 0)
                    act.wait_ge(s["proj_done"], 5 * i + j + 1)
                    act.activation(proj[:, u0 * P:(u0 + nu) * P], bank[yt_bank[j]][:, 0:nu * P], ACT.Identity,
                                   bias=bias[:, 0:1]).then_inc(s["proj_ready"], 1)
                if not last:
                    root(i + 1, 0)

            values(0, 0)
            square_base(0, 0)
            square_cube(0, 0)
            root(0, 0)
            with act.Fori(0, TILES // 2 - 1) as i:
                iteration(i, False)
            iteration(TILES // 2 - 1, True)

        @block.vector
        def _(dve):
            dve.sem_inc(s["base_ready"], 1)
            dve.sem_inc(s["kvm_ready"], 3)
            dve.sem_inc(s["ysum_ready"], 1)
            dve.sem_inc(s["conv_added"], 1)
            dve.wait_ge(s["act_ready0"], 4)
            dve.tensor_tensor(inv_sc[:], sc[:, 2, :], sc[:, 3, :], ALU.add).then_inc(s["inv_ready"], 1)
            dve.wait_ge(s["inv_ready"], 1)
            dve.reciprocal(inv_sc[:], inv_sc[:]).then_inc(s["inv_ready"], 1)
            dve.wait_ge(s["inv_ready"], 2)
            dve.tensor_tensor(wq[:], p["wq"], inv_sc[:], ALU.mult)
            dve.tensor_tensor(wk[:], p["wk"], inv_sc[:], ALU.mult)
            for u in range(3):
                ins = dve.tensor_tensor(pos[:, u * P:(u + 1) * P], p["pos"], inv_sc[:], ALU.mult)
            ins.then_inc(s["inv_ready"], 1)
            dve.tensor_scalar(floor[:], inv_sc[:], 1e-6, None, ALU.mult).then_inc(s["inv_ready"], 1)
            dve.wait_ge(s["inv_ready"], 4)

            def over3(ap):
                return ap.unsqueeze(1).broadcast_to([P, 3, P])

            def grouped(ap):
                return ap.rearrange("p z (n c) -> p (z n) c", c=C)

            def base_of(i, g):
                dve.wait_ge(s["qkv_done"], 6 * i + g + 2)
                kps = bank[0][:, 0:3 * P].rearrange("p (u n) -> p u n", u=3)
                qps = bank[1][:, 0:3 * P].rearrange("p (u n) -> p u n", u=3)
                b = base[:].rearrange("p z (u n) -> p z u n", u=3)
                dve.scalar_tensor_tensor(b[:, 1], qps, 0.0, over3(floor[:]), ALU.max, ALU.add)
                dve.scalar_tensor_tensor(b[:, 0], kps, 0.0, over3(floor[:]), ALU.max, ALU.add)\
                   .then_inc(s["base_ready"], 1)

            def cube_of(i, g):
                dve.wait_ge(s["sqa_ready"], 6 * i + g + 1)
                dve.wait_ge(s["base_ready"], 6 * i + g + 2)
                dve.tensor_tensor(cube[:], sqa[:], base[:], ALU.mult).then_inc(s["cube_ready"], 1)
                dve.tensor_reduce(norms[:, 0, :], grouped(sqa[:]), AXX, ALU.add).then_inc(s["s2_ready"], 1)

            def sum6(i, g):
                dve.wait_ge(s["sqb_ready"], 6 * i + g + 1)
                dve.tensor_reduce(norms[:, 1, :], grouped(sqb[:]), AXX, ALU.add).then_inc(s["s6_ready"], 1)

            def normalise(i, g):
                dve.wait_ge(s["root_ready"], 6 * i + g + 1)
                dve.reciprocal(factor[:, 0, :], roots[:, 1, :]).then_inc(s["factor_ready"], 1)
                dve.wait_ge(s["factor_ready"], 12 * i + 2 * g + 1)
                dve.tensor_tensor(factor[:, 1, :], roots[:, 0, :], factor[:, 0, :], ALU.mult)\
                   .then_inc(s["factor_ready"], 1)
                dve.wait_ge(s["factor_ready"], 12 * i + 2 * g + 2)
                if g >= 2:
                    dve.wait_ge(s["qt_done"], U * i + 3 * (g - 1) + 1)
                else:
                    dve.wait_ge(s["qt_done"], U * i + 1)
                dve.tensor_tensor(grouped(kq[:, g % 2]), grouped(cube[:]),
                                  factor[:, 1, :].unsqueeze(2).broadcast_to([P, 12, C]), ALU.mult)\
                   .then_inc(s["kq_ready"], 1)

            def mask_kv(i, n):
                dve.wait_ge(s["kv_done"], U * i + n + 2)
                dve.wait_ge(s["y_done"], U * i + n + 1)
                b = bank[kv_bank[n % 3]]
                dve.tensor_tensor(kvm[:, n % 3, :, 0:P], b[:, 0:2 * P].rearrange("p (a n) -> p a n", a=2),
                                  p["headmask"].unsqueeze(1).broadcast_to([P, 2, P]), ALU.mult)
                dve.tensor_tensor(kvm[:, n % 3, :, P:YW],
                                  b[:, 2 * P:KVW].unsqueeze(2).broadcast_to([P, 2, 2 * NH]),
                                  p["headind"].unsqueeze(1).broadcast_to([P, 2, 2 * NH]), ALU.mult)\
                   .then_inc(s["kvm_ready"], 1)

            def divide(i, g):
                dve.wait_ge(s["y_done"], U * i + 3 * g + 6)
                ps = bank[6][:, 0:3 * YW].rearrange("p (u n) -> p u n", u=3)
                dve.tensor_scalar(den[:, 0], ps[:, :, P:YW], 1e-6, None, ALU.add).then_inc(s["den_ready"], 1)
                dve.wait_ge(s["den_ready"], 12 * i + 2 * g + 1)
                dve.reciprocal(den[:, 1], den[:, 0]).then_inc(s["den_ready"], 1)
                dve.wait_ge(s["den_ready"], 12 * i + 2 * g + 2)
                if g == 0:
                    dve.wait_ge(s["yt_done"], 5 * i + 1)
                dve.tensor_tensor(ysum[:, 3 * g:3 * g + 3, :].rearrange("p u (n d) -> p u n d", d=HD),
                                  ps[:, :, 0:P].rearrange("p u (n d) -> p u n d", d=HD),
                                  den[:, 1].unsqueeze(3).broadcast_to([P, 3, 2 * NH, HD]), ALU.mult)\
                   .then_inc(s["ysum_ready"], 1)

            dve.wait_ge(m.moe_landed, 32)
            dve.tensor_reduce(m.wrange[:, 0:1], m.w12[:], AXX, ALU.max)
            dve.tensor_reduce(m.wrange[:, 1:2], m.w12[:], AXX, ALU.min)
            with dve.Fori(0, TILES // 2) as i:
                base_of(i, 0)
                cube_of(i, 0)
                sum6(i, 0)
                normalise(i, 0)
                for g in range(6):
                    if g < 5:
                        base_of(i, g + 1)
                    if g:
                        divide(i, g - 1)
                    mask_kv(i, 3 * g)
                    if g < 5:
                        cube_of(i, g + 1)
                    mask_kv(i, 3 * g + 1)
                    if g < 5:
                        sum6(i, g + 1)
                    mask_kv(i, 3 * g + 2)
                    if g < 5:
                        normalise(i, g + 1)
                divide(i, 5)
                dve.wait_ge(s["ysum_ready"], 6 * i + 7)
                dve.wait_ge(s["conv_ready"], 8 * i + 8 + 3)
                for u0, nu in chunks:
                    y = ysum[:, u0:u0 + nu, :]
                    dve.tensor_tensor(y, y, conv[:, u0:u0 + nu, :], ALU.add).then_inc(s["conv_added"], 1)


def weight_scale_stage(nc, m):
    p = m.par
    with ExitStack() as c:
        sem = c.enter_context(StageSemaphores(nc, "ws"))
        top = c.enter_context(nc.sbuf_tensor("ws_top", [P, 4], F32))
        ones = c.enter_context(nc.sbuf_tensor("ws_ones", [1, P], F32))
        step, turned, spread = sem("step"), sem("turned"), sem("spread")
        block = c.enter_context(nc.Block())

        @block.tensor
        def _(pe):
            pe.wait_ge(step, 3)
            pe.transpose(m.bank[0][0:1, 0:P], top[:, 1:2], p["ident"]).then_inc(turned, 1)
            pe.wait_ge(step, 5)
            pe.matmul(m.bank[1][:, 0:1], ones[:], top[0:1, 3:4], start=True, stop=True).then_inc(spread, 1)

        @block.vector
        def _(dve):
            dve.wait_ge(m.moe_landed, 32)
            dve.memset(ones[:], 1.0).then_inc(step, 1)
            dve.tensor_scalar(top[:, 0:1], m.wrange[:, 1:2], -1.0, None, ALU.mult).then_inc(step, 1)
            dve.wait_ge(step, 2)
            dve.tensor_tensor(top[:, 1:2], top[:, 0:1], m.wrange[:, 0:1], ALU.max).then_inc(step, 1)
            dve.wait_ge(turned, 1)
            dve.tensor_reduce(top[0:1, 2:3], m.bank[0][0:1, 0:P], AXX, ALU.max).then_inc(step, 1)
            dve.wait_ge(step, 4)
            dve.tensor_scalar(top[0:1, 3:4], top[0:1, 2:3], 1e-30, None, ALU.max).then_inc(step, 1)
            dve.wait_ge(spread, 1)
            dve.tensor_copy(m.wscale[:], m.bank[1][:, 0:1]).then_inc(step, 1)
            dve.wait_ge(step, 6)
            bits = m.wscale[:].bitcast(mybir.dt.int32)
            dve.tensor_scalar(bits, bits, 0x7F800000, None, ALU.bitwise_and).then_inc(step, 1)
            dve.wait_ge(step, 7)
            dve.tensor_scalar(m.unscale[:], m.wscale[:], 2.0 ** -12 / XSCALE, None, ALU.mult).then_inc(step, 1)
            dve.reciprocal(top[:, 0:1], m.wscale[:]).then_inc(step, 1)
            dve.wait_ge(step, 9)
            dve.tensor_scalar(m.wscale[:], top[:, 0:1], 2.0 ** 12, None, ALU.mult).then_inc(step, 1)


def whiten_stage(nc, m):
    p = m.par
    with ExitStack() as c:
        def sb(name, shape, dt=F32):
            return c.enter_context(nc.sbuf_tensor(f"wh_{name}", shape, dt))

        sem = c.enter_context(StageSemaphores(nc, "wh"))

        mv = sb("mv", [P, HB, 2])
        st = sb("st", [P, 2, HB])
        gst = sb("gst", [P, 2, HB])
        gvar, a, b, bc, xv, tmp = (sb(n, [P, HB]) for n in ("gvar", "a", "b", "bc", "xv", "tmp"))
        sums = sb("sums", [P, 4])
        scal = sb("scal", [P, 8])
        h = sb("h", [HB, 8, 2 * HD])
        hs = sb("hs", [HB, 4, 2])
        hT = sb("hT", [2 * HD, HB])
        gate = sb("gate", [P, HB])
        xc = sb("xc", [P, 2, TW])
        xt = sb("xt", [P, 2, TW])
        zero = sb("zero", [P, P])
        gram = sb("gram", [P, P])
        half = sb("half", [P, C])
        sigma = sb("sigma", [P, P])
        pw = sb("pw", [P, 4, P])
        wP = sb("wP", [P, P])
        ga, gb = sb("ga", [P, HB]), sb("gb", [P, HB])
        rest = sb("rest", [P, 4, TW])
        names = ("dve_step act_step st_ready pair_done var_ready std_ready sums_ready fold_done mu_ready xm_done "
                 "xv_ready fc1_done hvar_ready hstd_ready hrelu_ready turn_done ht_ready fc2_done sig_ready "
                 "centre_ready xc_ready xt_done xt_ready gram_done tile_gram mask_ready folded trace_in trace_done "
                 "sig_mat prod_done pw_ready wp_ready gate_ready x_ready rest_ready app_done out_ready "
                 "scale_ready").split()
        s = {n: sem(n) for n in names}
        block = c.enter_context(nc.Block())
        bank = m.bank

        @block.tensor
        def _(pe):
            pe.sem_inc(s["tile_gram"], 2)
            pe.sem_inc(s["xt_done"], 2)
            pe.wait_ge(s["st_ready"], 1)
            pe.matmul(bank[0][:, 0:2 * HB], p["pair"], st[:], start=True, stop=True).then_inc(s["pair_done"], 1)
            pe.wait_ge(s["sums_ready"], 1)
            pe.matmul(bank[1][:, 0:2], p["fold"], sums[:, 0:2], start=True, stop=True).then_inc(s["fold_done"], 1)
            pe.matmul(bank[2][0:HB, 0:2 * HD], xv[:], p["fc1"], start=True, stop=True).then_inc(s["fc1_done"], 1)
            pe.wait_ge(s["mu_ready"], 1)
            pe.matmul(bank[3][:, 0:1], p["mean"], sums[:, 3:4], start=True, stop=True).then_inc(s["xm_done"], 1)
            pe.wait_ge(s["hrelu_ready"], 1)
            pe.transpose(bank[2][0:2 * HD, 0:HB], h[:, 7, :], p["ident"][0:HB, 0:HB]).then_inc(s["turn_done"], 1)
            pe.wait_ge(s["ht_ready"], 1)
            pe.matmul(bank[4][:, 0:HB], p["fc2"][0:2 * HD, :], hT[:], start=True, stop=True)\
              .then_inc(s["fc2_done"], 1)
            pe.matmul(bank[7][:, 0:P], zero[:], zero[:], start=True, stop=False, skip_group_check=True)
            with pe.Fori(0, TILES // 2) as i:
                for k in range(2):
                    t = 2 * i + k
                    pe.wait_ge(s["xc_ready"], 2 * t + 2)
                    pe.wait_ge(s["xt_ready"], t + 1)
                    for q in range(4):
                        mm = pe.transpose(bank[5 + k][:, q * P:(q + 1) * P], xc[:, k, q * P:(q + 1) * P], p["ident"])
                    mm.then_inc(s["xt_done"], 1)
                for k in range(2):
                    t = 2 * i + k
                    pe.wait_ge(s["xt_ready"], t + 3)
                    for q in range(4):
                        o = xt[:, k, q * P:(q + 1) * P]
                        mm = pe.matmul(bank[7][:, 0:P], o, o, start=False, stop=False, skip_group_check=True)
                    mm.then_inc(s["tile_gram"], 1)
            pe.matmul(bank[7][:, 0:P], zero[:], zero[:], start=False, stop=True, skip_group_check=True)\
              .then_inc(s["gram_done"], 1)
            pe.wait_ge(s["mask_ready"], 1)
            pe.matmul(bank[0][:, 0:P], p["fold"], gram[:], start=True, stop=True).then_inc(s["folded"], 1)
            pe.wait_ge(s["trace_in"], 1)
            pe.matmul(bank[1][:, 0:1], p["group16"], sums[:, 2:3], start=True, stop=True).then_inc(s["trace_done"], 1)
            for n in range(2):
                pe.wait_ge(s["pw_ready"], 4 * n + 1)
                pe.matmul(bank[2][:, 0:P], pw[:, 0, :], pw[:, 0, :], start=True, stop=True).then_inc(s["prod_done"], 1)
                pe.wait_ge(s["pw_ready"], 4 * n + 2)
                pe.matmul(bank[3][:, 0:P], pw[:, 1, :], pw[:, 0, :], start=True, stop=True).then_inc(s["prod_done"], 1)
                pe.wait_ge(s["pw_ready"], 4 * n + 3)
                pe.matmul(bank[4][:, 0:P], pw[:, 2, :], sigma[:], start=True, stop=True).then_inc(s["prod_done"], 1)
            pe.wait_ge(s["wp_ready"], 1)
            with pe.Fori(0, TILES // 4) as i:
                for k in range(4):
                    t = 4 * i + k
                    pe.wait_ge(s["x_ready"], 2 * t + 2)
                    pe.wait_ge(s["out_ready"], t + 1)
                    pe.matmul(bank[k + 1][:], wP[:], tile_of(m.xn, t), start=True, stop=True)\
                      .then_inc(s["app_done"], 1)

        @block.scalar
        def _(act):
            act.sem_inc(s["xt_ready"], 2)
            act.wait_ge(s["var_ready"], 1)
            act.activation(a[:], gvar[:], ACT.Sqrt).then_inc(s["std_ready"], 1)
            act.wait_ge(s["xm_done"], 1)
            act.activation(scal[:, 0:1], bank[3][:, 0:1], ACT.Sqrt).then_inc(s["scale_ready"], 1)
            act.wait_ge(s["hvar_ready"], 1)
            act.activation(hs[:, 2, :], hs[:, 1, :], ACT.Sqrt).then_inc(s["hstd_ready"], 1)
            act.activation(scal[:, 1:2], p["x_weight"], ACT.Sigmoid).then_inc(s["sig_ready"], 1)
            act.wait_ge(s["fc2_done"], 1)
            act.activation(gate[:], bank[4][:, 0:HB], ACT.Sigmoid).then_inc(s["sig_ready"], 1)
            with act.Fori(0, TILES // 2) as i:
                for k in range(2):
                    t = 2 * i + k
                    act.wait_ge(s["xt_done"], t + 3)
                    act.wait_ge(s["tile_gram"], t + 1)
                    act.activation(xt[:, k, :], bank[5 + k][:], ACT.Copy).then_inc(s["xt_ready"], 1)
            with act.Fori(0, HB // 4) as i:
                for k in range(4):
                    n = 4 * i + k
                    act.activation(m.xn[:, bass.ds(n * HW, HW)], m.xa[:, bass.ds(n * HW, HW)], ACT.Identity,
                                   scale=a[:, bass.ds(n, 1)], bias=b[:, bass.ds(n, 1)]).then_inc(s["x_ready"], 1)
            act.wait_ge(s["gate_ready"], 1)
            with act.Fori(0, TILES // 4) as i:
                for k in range(4):
                    t = 4 * i + k
                    act.wait_ge(s["out_ready"], t + 1)
                    for q in range(2):
                        n = 2 * t + q
                        act.activation(rest[:, k, q * HW:(q + 1) * HW], m.xa[:, bass.ds(n * HW, HW)], ACT.Identity,
                                       scale=ga[:, bass.ds(n, 1)], bias=gb[:, bass.ds(n, 1)])\
                           .then_inc(s["rest_ready"], 1)

        @block.vector
        def _(dve):
            count = [0]

            def link(ins):
                count[0] += 1
                ins.then_inc(s["dve_step"], 1)
                dve.wait_ge(s["dve_step"], count[0])

            dve.sem_inc(s["out_ready"], 4)
            for n in range(HB):
                ins = dve.bn_aggr(mv[:, n, :], m.stats[:, n, :])
            link(ins)
            mean_c, var_c = mv[:, :, 0], mv[:, :, 1]
            dve.memset(zero[:], 0.0)
            link(dve.tensor_copy(st[:, 0, :], mean_c))
            link(dve.tensor_tensor(tmp[:], mean_c, mean_c, ALU.mult))
            dve.tensor_tensor(st[:, 1, :], tmp[:], var_c, ALU.add).then_inc(s["st_ready"], 1)
            dve.wait_ge(s["pair_done"], 1)
            link(dve.tensor_copy(gst[:].rearrange("p a b -> p (a b)"), bank[0][:, 0:2 * HB]))
            link(dve.tensor_tensor(tmp[:], gst[:, 0, :], gst[:, 0, :], ALU.mult))
            link(dve.tensor_tensor(gvar[:], gst[:, 1, :], tmp[:], ALU.subtract))
            link(dve.tensor_scalar(gvar[:], gvar[:], 0.0, None, ALU.max))
            dve.tensor_scalar(gvar[:], gvar[:], 1e-5, None, ALU.add).then_inc(s["var_ready"], 1)
            dve.wait_ge(s["std_ready"], 1)
            link(dve.reciprocal(a[:], a[:]))
            link(dve.scalar_tensor_tensor(b[:], gst[:, 0, :], -1.0, a[:], ALU.mult, ALU.mult))
            link(dve.tensor_tensor(tmp[:], a[:], a[:], ALU.mult))
            link(dve.scalar_tensor_tensor(xv[:], tmp[:], float(HW) / (HW - 1), var_c, ALU.mult, ALU.mult))
            link(dve.tensor_tensor(tmp[:], a[:], mean_c, ALU.mult))
            link(dve.tensor_tensor(tmp[:], tmp[:], b[:], ALU.add))
            link(dve.tensor_reduce(sums[:, 0:1], tmp[:], AXX, ALU.add))
            dve.tensor_reduce(sums[:, 1:2], xv[:], AXX, ALU.add).then_inc(s["sums_ready"], 1)
            dve.wait_ge(s["fold_done"], 1)
            link(dve.tensor_scalar(scal[:, 2:3], bank[1][:, 0:1], 1.0 / B, None, ALU.mult))
            dve.tensor_scalar(sums[:, 3:4], bank[1][:, 1:2], 1.0 / B, None, ALU.mult).then_inc(s["mu_ready"], 1)
            dve.tensor_scalar(bc[:], b[:], scal[:, 2:3], None, ALU.subtract).then_inc(s["centre_ready"], 1)
            def two(v):
                return v.rearrange("p (h j) -> p h j", h=2)

            def over16(v):
                return v.unsqueeze(2).broadcast_to([HB, 2, HD])

            dve.wait_ge(s["fc1_done"], 1)
            link(dve.tensor_copy(h[:, 0, :], bank[2][0:HB, 0:2 * HD]))
            link(dve.tensor_reduce(hs[:, 0, :], two(h[:, 0, :]), AXX, ALU.add))
            link(dve.tensor_scalar(hs[:, 0, :], hs[:, 0, :], 1.0 / HD, None, ALU.mult))
            link(dve.tensor_tensor(two(h[:, 1, :]), two(h[:, 0, :]), over16(hs[:, 0, :]), ALU.subtract))
            link(dve.tensor_tensor(h[:, 2, :], h[:, 1, :], h[:, 1, :], ALU.mult))
            link(dve.tensor_reduce(hs[:, 1, :], two(h[:, 2, :]), AXX, ALU.add))
            dve.tensor_scalar(hs[:, 1, :], hs[:, 1, :], 1.0 / HD, 1e-5, ALU.mult, ALU.add).then_inc(s["hvar_ready"], 1)
            dve.wait_ge(s["hstd_ready"], 1)
            link(dve.reciprocal(hs[:, 3, :], hs[:, 2, :]))
            link(dve.tensor_tensor(two(h[:, 3, :]), two(h[:, 1, :]), over16(hs[:, 3, :]), ALU.mult))
            link(dve.tensor_tensor(h[:, 4, :], h[:, 3, :], p["ln_g"][0:HB, :], ALU.mult))
            link(dve.tensor_tensor(h[:, 5, :], h[:, 4, :], p["ln_b"][0:HB, :], ALU.add))
            dve.tensor_scalar(h[:, 7, :], h[:, 5, :], 0.0, None, ALU.max).then_inc(s["hrelu_ready"], 1)
            dve.wait_ge(s["turn_done"], 1)
            dve.tensor_copy(hT[:], bank[2][0:2 * HD, 0:HB]).then_inc(s["ht_ready"], 1)
            dve.wait_ge(s["centre_ready"], 1)
            with dve.Fori(0, TILES // 2) as i:
                for k in range(2):
                    t = 2 * i + k
                    dve.wait_ge(s["xt_done"], t + 1)
                    for q in range(2):
                        n = 2 * t + q
                        dve.tensor_scalar(xc[:, k, q * HW:(q + 1) * HW], m.xa[:, bass.ds(n * HW, HW)],
                                          a[:, bass.ds(n, 1)], bc[:, bass.ds(n, 1)], ALU.mult, ALU.add)\
                           .then_inc(s["xc_ready"], 1)
            dve.wait_ge(s["scale_ready"], 1)
            link(dve.reciprocal(scal[:, 3:4], scal[:, 0:1]))
            dve.wait_ge(s["sig_ready"], 2)
            link(dve.tensor_scalar(scal[:, 4:5], scal[:, 1:2], -1.0, 1.0, ALU.mult, ALU.add))
            link(dve.tensor_tensor(scal[:, 5:6], scal[:, 4:5], scal[:, 3:4], ALU.mult))
            link(dve.tensor_scalar(gate[:], gate[:], scal[:, 5:6], None, ALU.mult))
            link(dve.tensor_tensor(ga[:], gate[:], a[:], ALU.mult))
            link(dve.tensor_scalar(ga[:], ga[:], 1.0, None, ALU.add))
            dve.tensor_tensor(gb[:], gate[:], b[:], ALU.mult).then_inc(s["gate_ready"], 1)
            dve.wait_ge(s["gram_done"], 1)
            dve.tensor_tensor(gram[:], bank[7][:, 0:P], p["group16"], ALU.mult).then_inc(s["mask_ready"], 1)
            dve.wait_ge(s["folded"], 1)
            link(dve.tensor_copy(pw[:, 3, :], bank[0][:, 0:P]))
            link(dve.tensor_tensor(half[:], pw[:, 3, 0:C], pw[:, 3, C:P], ALU.add))
            link(dve.tensor_tensor(sigma[:].rearrange("p (h n) -> p h n", h=2),
                                   half[:].unsqueeze(1).broadcast_to([P, 2, C]),
                                   p["group16"].rearrange("p (h n) -> p h n", h=2), ALU.mult))
            link(dve.tensor_scalar(sigma[:], sigma[:], 1e-5, None, ALU.mult))
            link(dve.scalar_tensor_tensor(sigma[:], p["ident"], 1.0 / (B * HW), sigma[:], ALU.mult, ALU.add))
            link(dve.tensor_tensor(pw[:, 3, :], sigma[:], p["ident"], ALU.mult))
            dve.tensor_reduce(sums[:, 2:3], pw[:, 3, :], AXX, ALU.add).then_inc(s["trace_in"], 1)
            dve.wait_ge(s["trace_done"], 1)
            link(dve.reciprocal(scal[:, 6:7], bank[1][:, 0:1]))
            link(dve.tensor_scalar(sigma[:], sigma[:], scal[:, 6:7], None, ALU.mult))
            link(dve.tensor_scalar(pw[:, 3, :], sigma[:], 1.5, None, ALU.mult))
            dve.scalar_tensor_tensor(pw[:, 0, :], p["ident"], -0.5, pw[:, 3, :], ALU.mult, ALU.add)\
               .then_inc(s["pw_ready"], 1)
            for n in range(2):
                dve.wait_ge(s["prod_done"], 3 * n + 1)
                dve.tensor_copy(pw[:, 1, :], bank[2][:, 0:P]).then_inc(s["pw_ready"], 1)
                dve.wait_ge(s["prod_done"], 3 * n + 2)
                dve.tensor_copy(pw[:, 2, :], bank[3][:, 0:P]).then_inc(s["pw_ready"], 1)
                dve.wait_ge(s["prod_done"], 3 * n + 3)
                link(dve.tensor_scalar(pw[:, 3, :], bank[4][:, 0:P], 1.5, None, ALU.mult))
                link(dve.scalar_tensor_tensor(pw[:, 0, :], pw[:, 0, :], -0.5, pw[:, 3, :], ALU.mult, ALU.add))
                dve.sem_inc(s["pw_ready"], 2)
            dve.tensor_scalar(wP[:], pw[:, 0, :], scal[:, 1:2], None, ALU.mult).then_inc(s["wp_ready"], 1)
            with dve.Fori(0, TILES // 4) as i:
                for k in range(4):
                    t = 4 * i + k
                    dve.wait_ge(s["app_done"], t + 1)
                    dve.wait_ge(s["rest_ready"], 2 * t + 2)
                    dve.tensor_tensor(tile_of(m.xa, t), bank[k + 1][:], rest[:, k, :], ALU.add)\
                       .then_inc(s["out_ready"], 1)


def layer_norm_stage(nc, m, prefix, out_tile, scale=None):
    p = m.par
    R = 8
    with ExitStack() as c:
        sem = c.enter_context(StageSemaphores(nc, prefix))
        sq = c.enter_context(nc.sbuf_tensor(f"{prefix}_sq", [P, 4, TW], F32))
        std = c.enter_context(nc.sbuf_tensor(f"{prefix}_std", [P, 2, TW], F32))
        s = {n: sem(n) for n in ("warm", "zeroed", "centred", "sq_ready", "copied", "var_done", "std_ready",
                                 "unscaled", "inv_ready", "spread_done", "xn_ready")}
        block = c.enter_context(nc.Block())
        bank = m.bank
        GROUPS = TILES // 4
        SPREAD = (6, 7, 4, 0, 1, 2, 3, 5)

        @block.tensor
        def _(pe):
            for i in range(GROUPS):
                for k in range(4):
                    t = 4 * i + k
                    if i:
                        pe.wait_ge(s["copied"], t - 3)
                        pe.wait_ge(s["sq_ready"], t - 3)
                    pe.matmul(bank[k][:], p["center"], tile_of(m.xa, t), start=True, stop=True)\
                      .then_inc(s["centred"], 1)
                for k in range(4):
                    pe.wait_ge(s["sq_ready"], 4 * i + k + 1)
                    mm = pe.matmul(bank[4 + i][0:R, :], p["var_rows"][:, k * R:(k + 1) * R], sq[:, k, :],
                                   start=(k == 0), stop=(k == 3))
                    mm.then_inc(s["var_done"], 1)
            pe.wait_ge(s["zeroed"], 1)
            for t in range(TILES):
                pe.wait_ge(s["inv_ready"], t // 4 + 1)
                if 3 <= t < 7:
                    pe.wait_ge(s["copied"], 4 + t - 3 + 1)
                pe.matmul(bank[SPREAD[t]][:], p["spread"][:, (t % 4) * P:(t % 4 + 1) * P], std[:, t // 4, :],
                          start=True, stop=True).then_inc(s["spread_done"], 1)

        @block.scalar
        def _(act):
            act.activation(sq[:, 0, 0:1], p["ident"][:, 0:1], ACT.Sqrt).then_inc(s["warm"], 1)
            act.wait_ge(s["warm"], 1)
            for i in range(GROUPS):
                for k in range(4):
                    t = 4 * i + k
                    act.wait_ge(s["centred"], t + 1)
                    if i:
                        act.wait_ge(s["var_done"], t - 3)
                    act.activation(sq[:, k, :], bank[k][:], ACT.Square).then_inc(s["sq_ready"], 1)
                act.wait_ge(s["zeroed"], 1)
                act.wait_ge(s["var_done"], 4 * i + 4)
                act.activation(std[0:R, i, :], bank[4 + i][0:R, :], ACT.Sqrt, bias=m.eps5[0:R, 0:1])\
                   .then_inc(s["std_ready"], 1)

        @block.vector
        def _(dve):
            dve.memset(std[:], 0.0).then_inc(s["zeroed"], 1)
            for i in range(GROUPS):
                for k in range(4):
                    t = 4 * i + k
                    dve.wait_ge(s["sq_ready"], t + 1)
                    dve.tensor_copy(out_tile(t), bank[k][:].rearrange("p (b t) -> p b t", b=2))\
                       .then_inc(s["copied"], 1)
                dve.wait_ge(s["std_ready"], i + 1)
                inverse = dve.reciprocal(std[0:R, i, :], std[0:R, i, :])
                if scale is not None:
                    inverse.then_inc(s["unscaled"], 1)
                    dve.wait_ge(s["unscaled"], i + 1)
                    inverse = dve.tensor_scalar(std[0:R, i, :], std[0:R, i, :], scale, None, ALU.mult)
                inverse.then_inc(s["inv_ready"], 1)
            for t in range(TILES):
                dve.wait_ge(s["spread_done"], t + 1)
                dve.wait_ge(s["copied"], t + 1)
                dve.tensor_tensor(out_tile(t), bank[SPREAD[t]][:].rearrange("p (b t) -> p b t", b=2), out_tile(t),
                                  ALU.mult).then_inc(s["xn_ready"], 1)


def slice_attention_stage(nc, m):
    p = m.par
    LOG_NEG_LOG_EPS = float(np.log(-np.log(np.float32(1e-6)), dtype=np.float32))
    with ExitStack() as c:
        def sb(name, shape, dt=F32):
            return c.enter_context(nc.sbuf_tensor(f"sl_{name}", shape, dt))

        b_slice = sb("b_slice", [P, 1])
        xps = sb("xps", [P, 2, TW])
        temp = sb("temp", [P, TW])
        inv, logit = sb("inv", [P, 2, TW]), sb("logit", [P, 2, TW])
        negmax = sb("negmax", [P, 2, 2])
        ex = sb("ex", [P, 2, 2, TW])
        tot, f = sb("tot", [P, 2, 4]), sb("f", [P, 4, 4])
        xpt = sb("xpt", [P, 2, 4, 2 * P])
        et = sb("et", [P, 2, TW])
        gtm, bm = sb("gtm", [P, 4, P]), sb("bm", [P, 4, P])
        names = ("bs_ready xp_done xps_ready temp_done lt_done clip1 clip2 inv_temp spread_done iv_ready "
                 "logit_ready max_ready negmax_ready "
                 "ex_ready xpt_done xpt_ready et_done et_ready gt_done gtm_ready b_done f_step bm_ready o_done "
                 "out_ready").split()
        sem = c.enter_context(StageSemaphores(nc, "sl"))
        s = {n: sem(n) for n in names}
        block = c.enter_context(nc.Block())
        bank = m.bank
        R = 2 * HEADS
        XP, XT, TM, LG, ET, GT, OB = bank[0], bank[1], bank[2], bank[3:5], bank[5], bank[6], bank[7]

        def run(engine, step):
            step(-2, 0, True, False, False, False)
            step(-1, 1, True, True, False, False)
            step(0, 0, True, True, True, False)
            with engine.Fori(0, TILES // 2 - 2) as i:
                for k in range(1, 3):
                    step(2 * i + k, k % 2, True, True, True, True)
            step(TILES - 3, 1, True, True, True, True)
            step(TILES - 2, 0, False, True, True, True)
            step(TILES - 1, 1, False, False, True, True)
            step(TILES, 0, False, False, False, True)

        @block.tensor
        def _(pe):
            def step(t, k, ahead, first, second, third):
                u = t + 1

                def project(h):
                    pe.wait_ge(s["xps_ready"], 2 * (t + 2) + h + 1)
                    pe.matmul(XP[:], p["w_x"][:, h * P:(h + 1) * P], tile_of(m.xn, t + 2),
                              start=True, stop=True)\
                      .then_inc(s["xp_done"], 1)

                def by_token(h):
                    pe.wait_ge(s["xps_ready"], 2 * u + h + 2)
                    pe.wait_ge(s["xpt_ready"], 2 * u + h + 1)
                    for q in range(4):
                        mm = pe.transpose(XT[:, q * P:(q + 1) * P], xps[:, h, q * P:(q + 1) * P], p["ident"])
                    mm.then_inc(s["xpt_done"], 1)

                def temperatures():
                    pe.wait_ge(s["xps_ready"], 2 * u + 3)
                    pe.wait_ge(s["iv_ready"], 2 * u + 1)
                    for h in range(2):
                        mm = pe.matmul(TM[0:R, :], p["temp_rows"][:, h * R:(h + 1) * R], xps[:, h, :],
                                       start=(h == 0), stop=(h == 1))
                    mm.then_inc(s["temp_done"], 1)

                def logits(h):
                    pe.wait_ge(s["logit_ready"], 2 * u + h + 1)
                    pe.matmul(LG[h][:], p["w_slice"], xps[:, h, :], start=True, stop=True)\
                      .then_inc(s["lt_done"], 1)

                def spread(h):
                    pe.wait_ge(s["inv_temp"], u + 1)
                    if h:
                        pe.wait_ge(s["iv_ready"], 2 * u + 2)
                    pe.matmul(TM[:], p["temp_spread"][:, h * P:(h + 1) * P], temp[:], start=True, stop=True)\
                      .then_inc(s["spread_done"], 1)

                def turn(h):
                    pe.wait_ge(s["ex_ready"], 4 * t + 2 * h + 2 + 4)
                    pe.wait_ge(s["et_ready"], 2 * t + h + 1)
                    for q in range(4):
                        mm = pe.transpose(ET[:, q * P:(q + 1) * P], ex[:, k, h, q * P:(q + 1) * P], p["ident"])
                    mm.then_inc(s["et_done"], 1)

                if first:
                    by_token(0)
                    temperatures()
                    logits(0)
                if third:
                    pe.wait_ge(s["bm_ready"], t + 1)
                    for b in range(2):
                        for h in range(2):
                            mm = pe.matmul(OB[:, b * HW:(b + 1) * HW], bm[:, 2 * h + b, :],
                                           ex[:, 1 - k, h, b * HW:(b + 1) * HW], start=(h == 0), stop=(h == 1))
                    mm.then_inc(s["o_done"], 1)
                if first:
                    by_token(1)
                    logits(1)
                if second:
                    turn(0)
                    turn(1)
                    pe.wait_ge(s["gtm_ready"], t + 1)
                    pe.wait_ge(s["xpt_ready"], 2 * t + 3)
                    for h in range(2):
                        pe.wait_ge(s["et_ready"], 2 * t + h + 2)
                        for b in range(2):
                            for q in (2 * b, 2 * b + 1):
                                mm = pe.matmul(GT[:, (2 * h + b) * P:(2 * h + b + 1) * P],
                                               xpt[:, k, q, h * P:(h + 1) * P], et[:, h, q * P:(q + 1) * P],
                                               start=(q == 2 * b), stop=(q == 2 * b + 1))
                    mm.then_inc(s["gt_done"], 1)
                if ahead:
                    project(0)
                if first:
                    spread(0)
                if second:
                    pe.wait_ge(s["gtm_ready"], t + 2)
                    pe.wait_ge(s["out_ready"], t + 1)
                    for n in range(4):
                        mm = pe.matmul(OB[:, n * P:(n + 1) * P], gtm[:, n, :],
                                       p["w_out"][:, (n // 2) * P:(n // 2 + 1) * P], start=True, stop=True)
                    mm.then_inc(s["b_done"], 1)
                if ahead:
                    project(1)
                if first:
                    spread(1)

            run(pe, step)

        @block.scalar
        def _(act):
            act.sem_inc(s["xps_ready"], 1)
            act.sem_inc(s["et_ready"], 1)
            act.sem_inc(s["ex_ready"], 4)
            act.sem_inc(s["iv_ready"], 1)

            def step(t, k, ahead, first, second, third):
                u = t + 1

                def turned(h):
                    act.wait_ge(s["et_done"], 2 * t + h + 1)
                    act.wait_ge(s["gt_done"], t + 2)
                    act.activation(et[:, h, :], ET[:], ACT.Copy).then_inc(s["et_ready"], 1)

                def exponentials(h):
                    act.wait_ge(s["negmax_ready"], 2 * t + h + 1)
                    act.wait_ge(s["o_done"], t + 1)
                    for b in range(2):
                        act.activation(ex[:, k, h, b * HW:(b + 1) * HW], logit[:, h, b * HW:(b + 1) * HW],
                                       ACT.Exp, bias=negmax[:, h, b:b + 1],
                                       accum_out=tot[:, k, 2 * h + b:2 * h + b + 1]).then_inc(s["ex_ready"], 1)

                if second:
                    exponentials(0)
                    exponentials(1)
                    turned(0)
                    turned(1)
                for h in range(2):
                    if ahead:
                        n = 2 * (t + 2) + h
                        act.wait_ge(s["xp_done"], n + 1)
                        act.wait_ge(s["lt_done"], n + 1)
                        act.activation(xps[:, h, :], XP[:], ACT.Identity, bias=p["b_x"][:, 0:1])\
                           .then_inc(s["xps_ready"], 1)
                    if first:
                        act.wait_ge(s["spread_done"], 2 * u + h + 1)
                        act.wait_ge(s["logit_ready"], 2 * u + h + 1)
                        act.activation(inv[:, h, :], TM[:], ACT.Copy).then_inc(s["iv_ready"], 1)

            run(act, step)

        @block.vector
        def _(dve):
            for n, start in (("logit_ready", 2), ("xpt_ready", 1), ("gtm_ready", 1), ("out_ready", 1),
                             ("bm_ready", 1)):
                dve.sem_inc(s[n], start)
            dve.tensor_scalar(b_slice[:], p["b_slice"], LOG_NEG_LOG_EPS, None, ALU.subtract).then_inc(s["bs_ready"], 1)
            dve.memset(temp[:], 0.0).then_inc(s["bs_ready"], 1)
            dve.wait_ge(s["bs_ready"], 2)

            def step(t, k, ahead, first, second, third):
                u = t + 1

                def tokens(h):
                    dve.wait_ge(s["gt_done"], u + 1)
                    dve.wait_ge(s["xpt_done"], 2 * u + h + 1)
                    dve.tensor_copy(xpt[:, 1 - k, :, h * P:(h + 1) * P], XT[:].rearrange("p (q n) -> p q n", q=4))\
                       .then_inc(s["xpt_ready"], 1)

                def inverse_temperatures():
                    dve.wait_ge(s["temp_done"], u + 1)
                    dve.wait_ge(s["iv_ready"], 2 * u + 1)
                    dve.tensor_scalar(temp[0:R, :], TM[0:R, :], p["b_temp"][0:R, 0:1], 0.4, ALU.add, ALU.min)\
                       .then_inc(s["clip1"], 1)
                    dve.wait_ge(s["clip1"], u + 1)
                    dve.tensor_scalar(temp[0:R, :], temp[0:R, :], -0.4, 0.5, ALU.max, ALU.add)\
                       .then_inc(s["clip2"], 1)
                    dve.wait_ge(s["clip2"], u + 1)
                    dve.reciprocal(temp[0:R, :], temp[0:R, :]).then_inc(s["inv_temp"], 1)

                def scaled(h):
                    n = 2 * u + h
                    dve.wait_ge(s["iv_ready"], n + 2)
                    dve.wait_ge(s["lt_done"], n + 3)
                    dve.wait_ge(s["ex_ready"], 4 * u + 2 * h + 2)
                    dve.scalar_tensor_tensor(logit[:, h, :], LG[h][:], b_slice[:, 0:1], inv[:, h, :],
                                             ALU.add, ALU.mult).then_inc(s["logit_ready"], 1)

                def largest(h):
                    n = 2 * u + h
                    dve.wait_ge(s["logit_ready"], n + 3)
                    dve.tensor_reduce(negmax[:, h, :], logit[:, h, :].rearrange("p (b n) -> p b n", b=2),
                                      AXX, ALU.max).then_inc(s["max_ready"], 1)
                    dve.wait_ge(s["max_ready"], n + 1)
                    dve.tensor_scalar(negmax[:, h, :], negmax[:, h, :], -1.0, None, ALU.mult)\
                       .then_inc(s["negmax_ready"], 1)

                def normaliser(j):
                    if j:
                        dve.wait_ge(s["f_step"], 6 * t + j)
                    else:
                        dve.wait_ge(s["ex_ready"], 4 * t + 8)
                    if j == 0:
                        ins = dve.reciprocal(f[:, 0, :], tot[:, k, :])
                    elif j == 1:
                        ins = dve.tensor_tensor(f[:, 1, :], tot[:, k, :], f[:, 0, :], ALU.mult)
                    elif j == 2:
                        ins = dve.tensor_scalar(f[:, 1, :], f[:, 1, :], 1e-5, None, ALU.add)
                    elif j == 3:
                        ins = dve.reciprocal(f[:, 2, :], f[:, 1, :])
                    elif j == 4:
                        ins = dve.tensor_tensor(f[:, 2, :], f[:, 2, :], f[:, 0, :], ALU.mult)
                    else:
                        ins = dve.tensor_tensor(f[:, 3, :], f[:, 2, :], f[:, 0, :], ALU.mult)
                    ins.then_inc(s["f_step"], 1)

                if first:
                    tokens(0)
                    inverse_temperatures()
                if third:
                    dve.wait_ge(s["o_done"], t + 2)
                    xa = tile_of(m.xa, t - 1)
                    dve.scalar_tensor_tensor(xa, OB[:], p["b_out"][:, 0:1], xa, ALU.add, ALU.add)\
                       .then_inc(s["out_ready"], 1)
                if second:
                    normaliser(0)
                if first:
                    tokens(1)
                if second:
                    normaliser(1)
                    dve.wait_ge(s["gt_done"], t + 3)
                    dve.wait_ge(s["bm_ready"], t + 1)
                    dve.tensor_tensor(gtm[:], GT[:].rearrange("p (n g) -> p n g", n=4),
                                      p["headmask"].unsqueeze(1).broadcast_to([P, 4, P]), ALU.mult)\
                       .then_inc(s["gtm_ready"], 1)
                    normaliser(2)
                if first:
                    scaled(0)
                if second:
                    normaliser(3)
                if first:
                    largest(0)
                if second:
                    normaliser(4)
                if first:
                    scaled(1)
                if second:
                    normaliser(5)
                if first:
                    largest(1)
                if second:
                    dve.wait_ge(s["b_done"], t + 1)
                    dve.wait_ge(s["f_step"], 6 * t + 6)
                    dve.wait_ge(s["o_done"], t + 2)
                    dve.tensor_tensor(bm[:], OB[:].rearrange("p (n g) -> p n g", n=4),
                                      f[:, 3, :].unsqueeze(2).broadcast_to([P, 4, P]), ALU.mult)\
                       .then_inc(s["bm_ready"], 1)

            run(dve, step)

        @block.gpsimd
        def _(pool):
            pool.sem_inc(s["lt_done"], 2)
            pool.sem_inc(s["gt_done"], 2)
            pool.sem_inc(s["o_done"], 2)

def lstm_stage(nc, m):
    p = m.par
    STEPS = 8
    CH = STEPS * HB
    SC = 2.0 ** 12
    with ExitStack() as c:
        def sb(name, shape, dt=F32):
            return c.enter_context(nc.sbuf_tensor(f"ls_{name}", shape, dt))

        xn = m.xn_steps
        hs = sb("hs", [P, 2 * STEPS, HB])
        hx, unscale = sb("hx", [P, 2, STEPS, HB]), sb("unscale", [P, STEPS, HB])
        wscaled = sb("wscaled", [P, 2 * E * HID])
        u = sb("u", [P, 3, P])
        bias = sb("bias", [P, P])
        vs, rest = sb("vs", [P, 3, P]), sb("rest", [P, 3, P])
        vp = [sb(f"v{k}", [P, 3, P], BF16) for k in range(3)]
        gates, ig, cell, hc, tc = (sb("gates", [P, 3, HB]), sb("ig", [P, HB]), sb("cell", [P, HB]),
                                   sb("hc", [P, HB]), sb("tc", [P, HB]))
        og = sb("og", [P, HB])
        h1, h2 = sb("h1", [P, HB], F16), sb("h2", [P, HB], F16)
        names = ("split_step w_step u_ready zeros warm z_done zo_done o_ready "
                 "gates_ready ig_ready cell_ready tc_ready og_ready h1_ready h32_ready h2_ready hc_ready "
                 "scaled out_ready").split()
        sem = c.enter_context(StageSemaphores(nc, "ls"))
        s = {n: sem(n) for n in names}
        block = c.enter_context(nc.Block())
        bank = m.bank
        xa_bt = m.xa[:].rearrange("p (b t) -> p b t", b=HB)

        @block.tensor
        def _(pe):
            def o_of(b, step):
                return (bank[b][:, 2 * step * HB:2 * (step + 1) * HB].rearrange("p (g b) -> p g b", g=2),
                        bank[2 + b][:, step * HB:(step + 1) * HB])

            def prepare(chunk, b, part):
                two = bank[b][:, 0:2 * CH].rearrange("p (s g b) -> p s g b", s=STEPS, g=2)
                sel = p["gate_sel"][0:3, :].rearrange("p (s g b) -> p s g b", s=STEPS, g=3)
                x = xn[:, bass.ds(chunk * CH, CH)]
                if part == 0:
                    pe.matmul(two, bias[0:3, :], sel[:, :, 0:2, :], start=True, stop=False, skip_group_check=True)
                elif part < 3:
                    pe.matmul(two[:, :, part - 1, :], u[:, part - 1, :], x, start=False, stop=False,
                              skip_group_check=True)
                elif part == 3:
                    pe.matmul(bank[2 + b][:, 0:CH], bias[0:3, :], sel[:, :, 2, :], start=True, stop=False,
                              skip_group_check=True)
                else:
                    pe.matmul(bank[2 + b][:, 0:CH], u[:, 2, :], x, start=False, stop=False, skip_group_check=True)

            pe.wait_ge(s["u_ready"], 1)
            pe.wait_ge(s["zeros"], 1)
            for part in range(5):
                prepare(0, 0, part)
            with pe.Fori(0, HW // (2 * STEPS)) as i:
                for b in range(2):
                    for q in range(STEPS):
                        t = 2 * STEPS * i + STEPS * b + q
                        pe.wait_ge(s["h1_ready"], t + 1)
                        ig, o = o_of(b, q)
                        for part in range(3):
                            for g in range(3):
                                pe.matmul(ig[:, g, :] if g < 2 else o, vp[part][:, g, :], h1[:],
                                          start=False, stop=False, skip_group_check=True)
                        pe.wait_ge(s["h2_ready"], t + 1)
                        for g in range(3):
                            for part in range(2):
                                mm = pe.matmul(ig[:, g, :] if g < 2 else o, vp[part][:, g, :], h2[:],
                                               start=False, stop=(part == 1), skip_group_check=True)
                            if g:
                                mm.then_inc(s["z_done"] if g == 1 else s["zo_done"], 1)
                        if q < 5:
                            prepare(2 * i + b + 1, 1 - b, q)

        @block.scalar
        def _(act):
            act.activation(tc[:, 0:1], p["ident"][:, 0:1], ACT.Tanh).then_inc(s["warm"], 1)
            with act.Fori(0, HW // (2 * STEPS)) as i:
                for b in range(2):
                    for q in range(STEPS):
                        t = 2 * STEPS * i + STEPS * b + q
                        act.wait_ge(s["z_done"], t + 1)
                        act.activation(gates[:, 0:2, :], bank[b][:, 2 * q * HB:2 * (q + 1) * HB].rearrange(
                            "p (g b) -> p g b", g=2), ACT.Tanh).then_inc(s["gates_ready"], 1)
                        act.wait_ge(s["zo_done"], t + 1)
                        act.activation(gates[:, 2, :], bank[2 + b][:, q * HB:(q + 1) * HB], ACT.Tanh)\
                           .then_inc(s["o_ready"], 1)
                        act.wait_ge(s["cell_ready"], t + 1)
                        act.activation(tc[:], cell[:], ACT.Tanh).then_inc(s["tc_ready"], 1)

        @block.gpsimd
        def _(pool):
            pool.sem_inc(s["scaled"], 2)
            scaled = wscaled[:]
            pool.tensor_scalar(scaled, m.w12[:], m.wscale[:, 0:1], None, ALU.mult).then_inc(s["split_step"], 1)
            pool.wait_ge(s["split_step"], 1)
            pool.tensor_copy(m.wp[0][:], scaled).then_inc(s["split_step"], 1)
            pool.wait_ge(s["split_step"], 2)
            pool.tensor_tensor(m.wp[1][:], scaled, m.wp[0][:], ALU.subtract).then_inc(s["split_step"], 1)
            pool.memset(unscale[:], 1.0 / SC).then_inc(s["split_step"], 1)
            pool.wait_ge(s["split_step"], 4)
            with pool.Fori(0, HW // (2 * STEPS)) as i:
                for b in range(2):
                    j = 2 * i + b
                    pool.wait_ge(s["h32_ready"], STEPS * (j + 1))
                    pool.tensor_tensor(hx[:, b], hs[:, STEPS * b:STEPS * (b + 1), :], unscale[:], ALU.mult)\
                        .then_inc(s["scaled"], 1)
                    pool.wait_ge(s["scaled"], j + 3)
                    x = xa_bt[:, :, bass.ds(STEPS * j, STEPS)]
                    pool.tensor_tensor(x, hx[:, b].rearrange("p s b -> p b s"), x, ALU.add).then_inc(s["out_ready"], 1)

        @block.vector
        def _(dve):
            count = [0]

            def link(ins):
                count[0] += 1
                ins.then_inc(s["w_step"], 1)
                dve.wait_ge(s["w_step"], count[0])

            for g, n in enumerate("igo"):
                half = 1.0 if n == "g" else 0.5
                dve.tensor_scalar(u[:, g, :], p[f"u_{n}"], half, None, ALU.mult)
                dve.tensor_scalar(vs[:, g, :], p[f"v_{n}"], half / SC, None, ALU.mult)
            link(dve.tensor_scalar(bias[0:3, :], p["lstm_b"][0:3, :], p["lstm_half"][0:3, :], None, ALU.mult))
            link(dve.tensor_copy(vp[0][:], vs[:]))
            link(dve.tensor_tensor(rest[:], vs[:], vp[0][:], ALU.subtract))
            link(dve.tensor_copy(vp[1][:], rest[:]))
            link(dve.tensor_tensor(vs[:], rest[:], vp[1][:], ALU.subtract))
            dve.tensor_copy(vp[2][:], vs[:])
            dve.memset(xn[:, COLS:COLS + CH], 0.0)
            dve.memset(hc[:], 0.0)
            dve.memset(h1[:], 0.0)
            link(dve.memset(h2[:], 0.0))
            dve.sem_inc(s["u_ready"], 1)
            dve.sem_inc(s["zeros"], 1)
            dve.sem_inc(s["h1_ready"], 1)
            dve.sem_inc(s["h2_ready"], 1)
            dve.sem_inc(s["hc_ready"], 1)
            with dve.Fori(0, HW // (2 * STEPS)) as i:
                for b in range(2):
                    dve.wait_ge(s["scaled"], 2 * i + b + 1)
                    for q in range(STEPS):
                        t = 2 * STEPS * i + STEPS * b + q
                        dve.wait_ge(s["gates_ready"], t + 1)
                        dve.scalar_tensor_tensor(ig[:], gates[:, 0, :], 1.0, gates[:, 1, :], ALU.add, ALU.mult)\
                           .then_inc(s["ig_ready"], 1)
                        dve.wait_ge(s["ig_ready"], t + 1)
                        dve.wait_ge(s["hc_ready"], t + 1)
                        dve.scalar_tensor_tensor(cell[:], ig[:], 0.5, hc[:], ALU.mult, ALU.add)\
                           .then_inc(s["cell_ready"], 1)
                        dve.wait_ge(s["o_ready"], t + 1)
                        dve.tensor_scalar(og[:], gates[:, 2, :], SC / 2, SC / 2, ALU.mult, ALU.add)\
                           .then_inc(s["og_ready"], 1)
                        dve.wait_ge(s["tc_ready"], t + 1)
                        dve.wait_ge(s["og_ready"], t + 1)
                        h32 = hs[:, STEPS * b + q, :]
                        dve.tensor_tensor(h1[:], og[:], tc[:], ALU.mult).then_inc(s["h1_ready"], 1)
                        dve.tensor_tensor(h32, og[:], tc[:], ALU.mult).then_inc(s["h32_ready"], 1)
                        dve.wait_ge(s["h32_ready"], t + 1)
                        dve.tensor_tensor(h2[:], h32, h1[:], ALU.subtract).then_inc(s["h2_ready"], 1)
                        dve.scalar_tensor_tensor(hc[:], h32, 1.0 / SC, cell[:], ALU.mult, ALU.mult)\
                           .then_inc(s["hc_ready"], 1)


def sigmoid_attention_stage(nc, m):
    p = m.par
    with ExitStack() as c:
        def sb(name, shape, dt=F32):
            return c.enter_context(nc.sbuf_tensor(f"sg_{name}", shape, dt))

        sem = c.enter_context(StageSemaphores(nc, "sg"))
        x = sb("x", [P, 2, TW])
        qz = sb("qz", [P, 2, 2, TW])
        xt = sb("xt", [P, 2, TW])
        att = sb("att", [P, 4, TW])
        names = "zeroed warm x_ready q_done q_ready xt_done xt_ready s_done att_ready v_done out_ready".split()
        s = {n: sem(n) for n in names}
        block = c.enter_context(nc.Block())
        bank = m.bank
        SB = (6, 7, 3, 2)

        def run(engine, step):
            step(-1, 1, True, False)
            with engine.Fori(0, TILES // 2 - 1) as i:
                for k in range(2):
                    step(2 * i + k, k, True, True)
            step(TILES - 2, 0, True, True)
            step(TILES - 1, 1, False, True)

        @block.gpsimd
        def _(pool):
            pool.sem_inc(s["v_done"], 8)
            with pool.Fori(0, TILES // 2) as i:
                for k in range(2):
                    t = 2 * i + k
                    pool.wait_ge(s["v_done"], 4 * t + 4)
                    pool.tensor_copy(x[:, k, :], tile_of(m.xn, t)).then_inc(s["x_ready"], 1)

        @block.tensor
        def _(pe):
            def step(t, k, prepare, attend):
                u = t + 1

                def scores(n):
                    h, b = n // 2, n % 2
                    pe.wait_ge(s["att_ready"], 4 * t + n + 1)
                    for q in range(2):
                        mm = pe.matmul(bank[SB[n]][:, q * HW:(q + 1) * HW],
                                       x[:, k, (2 * b + q) * P:(2 * b + q + 1) * P],
                                       qz[:, k, h, b * HW:(b + 1) * HW], start=True, stop=True)
                    mm.then_inc(s["s_done"], 1)

                def values(n):
                    h, b = n // 2, n % 2
                    pe.wait_ge(s["att_ready"], 4 * t + n + 5)
                    for q in range(2):
                        mm = pe.matmul(bank[k][C * h:C * (h + 1), b * HW:(b + 1) * HW],
                                       xt[:, k, (2 * b + q) * P + C * h:(2 * b + q) * P + C * (h + 1)],
                                       att[:, n, q * HW:(q + 1) * HW], start=(q == 0), stop=(q == 1))
                    mm.then_inc(s["v_done"], 1)

                if attend:
                    pe.wait_ge(s["q_ready"], 2 * t + 3)
                    scores(0)
                    scores(1)
                if prepare:
                    pe.wait_ge(s["x_ready"], u + 1)
                    pe.wait_ge(s["q_ready"], 2 * u + 1)
                    pe.matmul(bank[4][:], p["q_w"], x[:, 1 - k, :], start=True, stop=True).then_inc(s["q_done"], 1)
                if attend:
                    scores(2)
                    scores(3)
                if prepare:
                    pe.wait_ge(s["xt_ready"], u + 1)
                    for q in range(4):
                        mm = pe.transpose(bank[5][:, q * P:(q + 1) * P], x[:, 1 - k, q * P:(q + 1) * P], p["ident"])
                    mm.then_inc(s["xt_done"], 1)
                if attend:
                    pe.wait_ge(s["xt_ready"], t + 2)
                    pe.wait_ge(s["out_ready"], t + 1)
                    for n in range(4):
                        values(n)

            run(pe, step)

        @block.scalar
        def _(act):
            act.sem_inc(s["q_ready"], 1)
            act.sem_inc(s["att_ready"], 4)
            act.activation(att[:, 0, 0:1], p["ident"][:, 0:1], ACT.Sigmoid).then_inc(s["warm"], 1)
            act.wait_ge(s["warm"], 1)
            act.wait_ge(s["zeroed"], 1)

            def step(t, k, prepare, attend):
                u = t + 1

                def weights(n):
                    act.wait_ge(s["s_done"], 4 * t + n + 1)
                    act.wait_ge(s["v_done"], 4 * t + n + 1 + 4)
                    act.activation(att[:, n, :], bank[SB[n]][:], ACT.Sigmoid).then_inc(s["att_ready"], 1)

                if attend:
                    weights(0)
                    weights(1)
                if prepare:
                    act.wait_ge(s["q_done"], u + 1)
                    act.wait_ge(s["v_done"], 4 * u + 4)
                    for h in range(2):
                        r = slice(C * h, C * (h + 1))
                        act.activation(qz[r, 1 - k, h, :], bank[4][r, :], ACT.Copy).then_inc(s["q_ready"], 1)
                if attend:
                    weights(2)
                    weights(3)

            run(act, step)

        @block.vector
        def _(dve):
            dve.sem_inc(s["xt_ready"], 1)
            dve.sem_inc(s["out_ready"], 2)
            dve.memset(qz[:], 0.0).then_inc(s["zeroed"], 1)

            def step(t, k, prepare, attend):
                u = t + 1
                if prepare:
                    dve.wait_ge(s["xt_done"], u + 1)
                    dve.wait_ge(s["v_done"], 4 * u + 4)
                    dve.tensor_copy(xt[:, 1 - k, :], bank[5][:]).then_inc(s["xt_ready"], 1)
                if attend:
                    dve.wait_ge(s["v_done"], 4 * t + 4 + 8)
                    xa = tile_of(m.xa, t)
                    dve.tensor_tensor(xa, bank[k][:], xa, ALU.add).then_inc(s["out_ready"], 1)

            run(dve, step)


def route_stage(nc, m):
    p = m.par
    G = TILES * 4 * 2
    with ExitStack() as c:
        def sb(name, shape, dt=F32):
            return c.enter_context(nc.sbuf_tensor(f"ro_{name}", shape, dt))

        sem = c.enter_context(StageSemaphores(nc, "ro"))
        x1 = sb("x1", [P, 2, TW], F16)
        lg = sb("lg", [P, G, E])
        e, e2, pick = sb("e", [P, G, E]), sb("e2", [P, G, E]), sb("pick", [P, G, E])
        masks = sb("masks", [P, 2, G, E])
        top = sb("top", [P, 4, G])
        dt = sb("dt", [2 * E, TILES, TW])
        names = "warm x1_ready first_part parts_ready gate_done lg_ready exp_in e_ready step d_ready dt_done "\
                "dt_ready stored"
        s = {n: sem(n) for n in names.split()}
        block = c.enter_context(nc.Block())
        bank = m.bank

        @block.tensor
        def _(pe):
            for t in range(TILES):
                if t >= 2:
                    pe.wait_ge(s["lg_ready"], t - 1)
                for q in range(4):
                    mm = pe.matmul(bank[4 + t % 2][:, q * 2 * E:(q + 1) * 2 * E],
                                   m.xn[:, t * TW + q * P:t * TW + (q + 1) * P], p["gate_w"], start=True, stop=True)
                mm.then_inc(s["gate_done"], 1)
            pe.wait_ge(s["d_ready"], 1)
            for t in range(TILES):
                if t >= 2:
                    pe.wait_ge(s["dt_ready"], t - 1)
                for q in range(4):
                    g = 2 * (4 * t + q)
                    mm = pe.transpose(bank[6 + t % 2][0:2 * E, q * P:(q + 1) * P],
                                      e2[:, g:g + 2, :].rearrange("p g e -> p (g e)"), p["ident"])
                mm.then_inc(s["dt_done"], 1)

        @block.scalar
        def _(act):
            act.activation(top[:, 3, 0:1], p["ident"][:, 0:1], ACT.Exp).then_inc(s["warm"], 1)
            act.wait_ge(s["warm"], 1)
            for t in range(TILES):
                if t >= 2:
                    act.wait_ge(s["parts_ready"], 2 * (t - 1))
                act.activation(x1[:, t % 2, :], tile_of(m.xn, t), ACT.Copy).then_inc(s["x1_ready"], 1)
                act.wait_ge(s["x1_ready"], t + 1)
                for h in range(2):
                    act.activation(m.xs[h][0:C, t * TW:(t + 1) * TW], x1[C * h:C * (h + 1), t % 2, :], ACT.Copy)\
                       .then_inc(s["first_part"], 1)
                if t == TILES // 2:
                    act.wait_ge(s["exp_in"], 1)
                    act.activation(e[:], lg[:], ACT.Exp).then_inc(s["e_ready"], 1)
            for t in range(TILES):
                act.wait_ge(s["dt_done"], t + 1)
                act.activation(dt[:, t, :], bank[6 + t % 2][0:2 * E, :], ACT.Copy).then_inc(s["dt_ready"], 1)

        @block.sync
        def _(sp):
            for t in range(TILES):
                sp.wait_ge(s["dt_ready"], t + 1)
                sp.dma_start(m.route[:, :, t, :].rearrange("h e n -> (h e) n"), dt[:, t, :])\
                  .then_inc(s["stored"], 16)
            sp.wait_ge(s["stored"], 16 * TILES)

        @block.gpsimd
        def _(pool):
            for t in range(TILES):
                pool.wait_ge(s["x1_ready"], t + 1)
                for h in range(2):
                    r = slice(C * h, C * (h + 1))
                    pool.tensor_tensor(m.xs[h][C:P, t * TW:(t + 1) * TW], m.xn[r, t * TW:(t + 1) * TW],
                                       x1[r, t % 2, :], ALU.subtract).then_inc(s["parts_ready"], 1)

        @block.vector
        def _(dve):
            for t in range(TILES):
                dve.wait_ge(s["gate_done"], t + 1)
                for q in range(4):
                    ins = dve.scalar_tensor_tensor(lg[:, 8 * t + 2 * q:8 * t + 2 * q + 2, :].rearrange(
                        "p h e -> p (h e)"), bank[4 + t % 2][:, q * 2 * E:(q + 1) * 2 * E], 1.0 / XSCALE,
                        p["gate_b"], ALU.mult, ALU.add)
                ins.then_inc(s["lg_ready"], 1)
            count = [0]

            def link(ins):
                count[0] += 1
                ins.then_inc(s["step"], 1)
                dve.wait_ge(s["step"], count[0])

            def over(v):
                return v.unsqueeze(2).broadcast_to([P, G, E])

            idx = p["idx_w"][:, 0:E].unsqueeze(1).broadcast_to([P, G, E])
            dve.wait_ge(s["lg_ready"], TILES)
            link(dve.tensor_reduce(top[:, 0, :], lg[:], AXX, ALU.max))
            dve.tensor_tensor(lg[:], lg[:], over(top[:, 0, :]), ALU.subtract).then_inc(s["exp_in"], 1)

            def first_of(mask):
                link(dve.tensor_reduce(top[:, 2, :], pick[:], AXX, ALU.max))
                link(dve.tensor_tensor(mask, pick[:], over(top[:, 2, :]), ALU.is_equal))

            dve.wait_ge(s["exp_in"], 1)
            link(dve.tensor_scalar(pick[:], lg[:], 0.0, None, ALU.is_equal))
            link(dve.tensor_tensor(pick[:], pick[:], idx, ALU.mult))
            first_of(masks[:, 0])
            dve.wait_ge(s["e_ready"], 1)
            link(dve.scalar_tensor_tensor(e2[:], masks[:, 0], -2.0, e[:], ALU.mult, ALU.add))
            link(dve.tensor_reduce(top[:, 1, :], e2[:], AXX, ALU.max))
            link(dve.tensor_tensor(pick[:], e2[:], over(top[:, 1, :]), ALU.is_equal))
            link(dve.tensor_tensor(pick[:], pick[:], idx, ALU.mult))
            first_of(masks[:, 1])
            link(dve.tensor_tensor(pick[:], masks[:, 0], masks[:, 1], ALU.add))
            link(dve.tensor_tensor(e2[:], pick[:], e[:], ALU.mult))
            link(dve.tensor_reduce(top[:, 3, :], e2[:], AXX, ALU.add))
            link(dve.reciprocal(top[:, 0, :], top[:, 3, :]))
            dve.tensor_tensor(e2[:], e2[:], over(top[:, 0, :]), ALU.mult).then_inc(s["d_ready"], 1)


def expert_stage(nc, m):
    p = m.par
    with ExitStack() as c:
        def sb(name, shape, dt=F32):
            return c.enter_context(nc.sbuf_tensor(f"ex_{name}", shape, dt))

        sem = c.enter_context(StageSemaphores(nc, "ex"))
        d = sb("d", [P, 2, E, TW])
        gated, hid = sb("gated", [P, 2, TW]), sb("hid", [P, 2, TW])
        part, acc = sb("part", [P, 2, TW]), sb("acc", [P, 2, TW])
        s = {n: sem(n) for n in ("warm", "up1_done", "up2_done", "gated_ready", "hid_ready", "down_done",
                                 "part_ready", "acc_ready")}
        EQ = 4
        d_landed = [[sem(f"d_landed{k}_{q}") for q in range(E // EQ)] for k in range(2)]
        stored = [sem(f"stored{k}") for k in range(2)]
        block = c.enter_context(nc.Block())
        bank = m.bank
        N = 2 * E

        @block.sync
        def _(sp):
            od = m.out.rearrange("(h g b) c n -> g h c b n", h=2, b=2)
            sp.sem_inc(stored[0], 1)
            sp.sem_inc(stored[1], 1)

            def load_dispatch(t, k):
                for q in range(E // EQ):
                    for h in range(2):
                        src = m.route[h:h + 1, q * EQ:(q + 1) * EQ, bass.ds(t, 1), :].rearrange(
                            "h e t n -> (h t) e n")
                        sp.dma_start(d[C * h:C * (h + 1), k, q * EQ:(q + 1) * EQ], src.broadcast_to([C, EQ, TW]))\
                          .then_inc(d_landed[k][q], 16)

            def store(t, k):
                sp.wait_ge(s["acc_ready"], E * (t + 1) + 2)
                for h in range(2):
                    sp.dma_start(od[bass.ds(t, 1), h].rearrange("g c b n -> (g c) b n"),
                                 acc[C * h:C * (h + 1), k, :].rearrange("p (b n) -> p b n", b=2))\
                      .then_inc(stored[k], 16)

            for k in range(2):
                load_dispatch(k, k)
            with sp.Fori(0, TILES // 2 - 1) as i:
                for k in range(2):
                    store(2 * i + k, k)
                    load_dispatch(2 * i + k + 2, k)
            for k in range(2):
                store(TILES - 2 + k, k)
            for k in range(2):
                sp.wait_ge(stored[k], 32 * (TILES // 2) + 1)

        @block.gpsimd
        def _(pool):
            pool.sem_inc(s["acc_ready"], 2)
            with pool.Fori(0, TILES // 2) as i:
                for k in range(2):
                    t = 2 * i + k
                    pool.wait_ge(stored[k], 32 * i + 1)
                    for e in range(E):
                        pool.wait_ge(s["part_ready"], E * t + e + 3)
                        if e:
                            pool.wait_ge(s["acc_ready"], E * t + e + 2)
                        pool.tensor_tensor(acc[:, k, :], part[:, e % 2, :],
                                           acc[:, k, :] if e else tile_of(m.xa, t), ALU.add)\
                            .then_inc(s["acc_ready"], 1)

        @block.tensor
        def _(pe):
            pe.sem_inc(s["down_done"], 1)
            def up(t, n):
                e, h = n // 2, n % 2
                x = m.xs[h][:, bass.ds(t * TW, TW)]
                for w in range(2):
                    pe.wait_ge(s["gated_ready"] if w == 0 else s["hid_ready"], N * t + n + 1)
                    for q in range(2):
                        mm = pe.matmul(bank[2 * w + n % 2][:], m.wp[q][:, (2 * e + w) * HID:(2 * e + w + 1) * HID],
                                       x, start=(q == 0), stop=(q == 1))
                    mm.then_inc(s["up1_done"] if w == 0 else s["up2_done"], 1)

            def down(t, n):
                e, h = n // 2, n % 2
                pe.wait_ge(s["hid_ready"], N * t + n + 3)
                if h == 0:
                    pe.wait_ge(s["part_ready"], E * t + e + 1)
                mm = pe.matmul(bank[4 + e % 2][C * h:C * (h + 1), :], m.w3[:, e * C:(e + 1) * C],
                               hid[:, n % 2, :], start=True, stop=True)
                mm.then_inc(s["down_done"], 1)

            with pe.Fori(0, TILES // 2) as i:
                for r in range(2 * N + 2):
                    if r < 2 * N:
                        up(2 * i + r // N, r % N)
                    if r >= 2:
                        down(2 * i + (r - 2) // N, (r - 2) % N)

        @block.scalar
        def _(act):
            act.sem_inc(s["gated_ready"], 2)
            act.activation(gated[:, 0, 0:1], p["ident"][:, 0:1], ACT.Silu).then_inc(s["warm"], 1)
            act.wait_ge(s["warm"], 1)
            with act.Fori(0, TILES // 2) as i:
                for k in range(2):
                    for n in range(N):
                        r = N * (2 * i + k) + n
                        act.wait_ge(s["up1_done"], r + 1)
                        act.wait_ge(s["hid_ready"], r + 1)
                        act.activation(gated[:, n % 2, :], bank[n % 2][:], ACT.Silu, scale=m.unscale[:, 0:1])\
                           .then_inc(s["gated_ready"], 1)

        @block.vector
        def _(dve):
            dve.sem_inc(s["hid_ready"], 2)
            dve.sem_inc(s["part_ready"], 2)
            with dve.Fori(0, TILES // 2) as i:
                for k in range(2):
                    t = 2 * i + k

                    def hidden(n):
                        r = N * t + n
                        dve.wait_ge(s["up2_done"], r + 1)
                        dve.wait_ge(s["gated_ready"], r + 3)
                        dve.wait_ge(s["down_done"], N * t + max(n - 1, 0) + 1)
                        dve.tensor_tensor(hid[:, n % 2, :], bank[2 + n % 2][:], gated[:, n % 2, :], ALU.mult)\
                           .then_inc(s["hid_ready"], 1)

                    def gather(e):
                        dve.wait_ge(s["down_done"], N * t + 2 * e + 3)
                        dve.wait_ge(s["acc_ready"], E * t + e + 1)
                        if e % EQ == 0:
                            dve.wait_ge(d_landed[k][e // EQ], 32 * (i + 1))
                        dve.scalar_tensor_tensor(part[:, e % 2, :], bank[4 + e % 2][:], m.unscale[:, 0:1], d[:, k, e, :],
                                                 ALU.mult, ALU.mult)\
                           .then_inc(s["part_ready"], 1)

                    for e in range(E):
                        hidden(2 * e)
                        hidden(2 * e + 1)
                        if e:
                            gather(e - 1)
                    gather(E - 1)



def param_views(m):
    views = {}
    for chunk, cols in LAYOUT.items():
        at = 0
        for name, n in cols.items():
            views[name] = m.chunk[chunk][:, at:at + n]
            at += n
    return views


def build(nc, x, dram, out):
    m = Mem()
    m.x, m.dram, m.out = x, dram, out
    with ExitStack() as c:
        m.chunk = {n: c.enter_context(nc.sbuf_tensor(f"par_{n}", [P, widths(n)], F32)) for n in LAYOUT}
        m.w12 = c.enter_context(nc.sbuf_tensor("w12", [P, 2 * E * HID], F32))
        m.w3 = c.enter_context(nc.sbuf_tensor("w3", [P, E * C], F32))
        m.xpad = c.enter_context(nc.sbuf_tensor("xpad", [P, (HB + 1) * PADI + 2 * PADW + 2], F32))
        m.xa = c.enter_context(nc.sbuf_tensor("xa", [P, COLS], F32))
        m.bank = [c.enter_context(nc.psum_tensor(f"bank{k}", [P, TW], F32)) for k in range(8)]
        m.conv0_landed = c.enter_context(nc.semaphore("conv0_landed"))
        m.attn_landed = c.enter_context(nc.semaphore("attn_landed"))
        m.rest_landed = c.enter_context(nc.semaphore("rest_landed"))
        m.moe_landed = c.enter_context(nc.semaphore("moe_landed"))
        m.par = param_views(m)
        m.eps5 = m.par["eps5"]
        conv_ffn_stage(nc, m, 0, m.xa)
        m.wrange = c.enter_context(nc.sbuf_tensor("wrange", [P, 2], F32))
        attention_stage(nc, m, m.xa)
        m.stats = c.enter_context(nc.sbuf_tensor("stats", [P, HB, 6], F32))
        m.wscale = c.enter_context(nc.sbuf_tensor("wscale", [P, 1], F32))
        m.unscale = c.enter_context(nc.sbuf_tensor("unscale", [P, 1], F32))
        conv_ffn_stage(nc, m, 1, m.xa, m.stats)
        weight_scale_stage(nc, m)
        m.xn = m.xpad[:, 0:COLS]
        whiten_stage(nc, m)

        def normed(t):
            return tile_of(m.xn, t).rearrange("p (b t) -> p b t", b=2)

        layer_norm_stage(nc, m, "ln2", normed)
        slice_attention_stage(nc, m)
        m.wp = [c.enter_context(nc.sbuf_tensor(f"wp{q}", [P, 2 * E * HID], F16)) for q in range(2)]
        CH = 8 * HB
        with nc.sbuf_tensor("xn_steps", [P, COLS + CH], F32) as xn_steps:
            m.xn_steps = xn_steps

            def normed_by_step(t):
                return xn_steps[:, 0:COLS].rearrange("p (t b) -> p b t", b=HB)[:, 2 * t:2 * t + 2, :]

            layer_norm_stage(nc, m, "ln3", normed_by_step)
            lstm_stage(nc, m)
        layer_norm_stage(nc, m, "ln4", normed)
        sigmoid_attention_stage(nc, m)
        m.route = nc.dram_tensor("route", (2, E, TILES, TW), F32, kind="Internal").ap()
        m.xs = [c.enter_context(nc.sbuf_tensor(f"xs{h}", [P, COLS], F16)) for h in range(2)]
        layer_norm_stage(nc, m, "ln5", normed, XSCALE)
        route_stage(nc, m)
        expert_stage(nc, m)


def both(w, cols=None):
    o = np.zeros((2 * w.shape[0], 2 * w.shape[1]), w.dtype)
    o[:w.shape[0], :w.shape[1]] = w
    o[w.shape[0]:, w.shape[1]:] = w
    return o


def twice(v):
    return np.concatenate([v, v], 0)


def rows(v):
    return np.ascontiguousarray(np.broadcast_to(v[None, :], (P, v.size)))


def by_half(w):
    o = np.zeros((P, 2 * w.shape[1]), w.dtype)
    o[:C, :w.shape[1]] = w
    o[C:, w.shape[1]:] = w
    return o


def out_by_half(w):
    o = np.zeros((w.shape[0], 2 * P), w.dtype)
    o[:, :C] = w
    o[:, P + C:] = w
    return o


def padded_rows(a, n=P):
    o = np.zeros((n, a.shape[1]), a.dtype)
    o[:a.shape[0]] = a
    return o


def lay_out(v):
    f = np.float32
    q = {}
    for n in (0, 1):
        q[f"dw{n}_w"] = twice(v[f"L0_conv_dw{n}_w"].reshape(C, 9))
        q[f"dw{n}_s"] = twice(v[f"L0_conv_dw{n}_s"][:, None])
        q[f"dw{n}_b"] = twice(v[f"L0_conv_dw{n}_b"][:, None])
        q[f"f{n}_w1"] = by_half(v[f"L0_conv_f{n}_w1"][:, :, 0, 0].T)
        q[f"f{n}_s1"] = v[f"L0_conv_f{n}_s1"][:, None]
        q[f"f{n}_b1"] = v[f"L0_conv_f{n}_b1"][:, None]
        q[f"f{n}_w2"] = v[f"L0_conv_f{n}_w2"][:, :, 0, 0].T
        q[f"f{n}_s2"] = twice(v[f"L0_conv_f{n}_s2"][:, None])
        q[f"f{n}_b2"] = twice(v[f"L0_conv_f{n}_b2"][:, None])
    q["wq"] = both(v["L0_conv_wq"].T)
    q["wk"] = both(v["L0_conv_wkv"][:C].T)
    q["wv"] = both(v["L0_conv_wkv"][C:].T)
    q["scale"] = rows(np.tile(v["L0_conv_scale_p"].reshape(C), 2))
    pos = np.zeros((P, P), f)
    for a in range(2):
        for h in range(2):
            pos[SLOT * a:SLOT * a + WR * WR, C * h:C * h + C] = v["L0_conv_pos"][0]
    q["pos"] = pos
    toep = np.zeros((P, HD, P), f)
    w = v["L0_conv_dwc_w"][:, 0]
    for ro in range(WR):
        for co in range(WR):
            for ky in range(5):
                for kx in range(5):
                    ri, ci = ro + ky - 2, co + kx - 2
                    if 0 <= ri < WR and 0 <= ci < WR:
                        for a in range(2):
                            toep[SLOT * a + ri * WR + ci, :, SLOT * a + ro * WR + co] = w[:, ky, kx]
    q["toep"] = toep.reshape(P, HD * P)
    q["dwc_b"] = np.tile(v["L0_conv_dwc_b"], 2 * NH)[:, None]
    q["proj"] = both(v["L0_conv_proj_w"].T)
    q["proj_b"] = twice(v["L0_conv_proj_b"][:, None])
    i = np.arange(P)
    q["ident"] = np.eye(P, dtype=f)
    q["headmask"] = (i[:, None] // HD == i[None, :] // HD).astype(f)
    q["headind"] = (i[:, None] // HD == np.arange(2 * NH)[None, :]).astype(f)
    valid = (i % SLOT < WR * WR).astype(f)
    q["slots"] = np.stack([valid * (i < SLOT), valid * (i >= SLOT)], 1).astype(f)
    same = (i[:, None] // C == i[None, :] // C).astype(f)
    q["mean"] = same / f(C)
    q["center"] = np.eye(P, dtype=f) - same / f(C)
    half = (i[:, None] // C == np.arange(8)[None, :] % 2)
    tile = np.arange(8)[None, :] // 2
    q["var_rows"] = np.concatenate([(half & (tile == k)) / f(C) for k in range(4)], 1).astype(f)
    q["spread"] = np.concatenate([padded_rows((half & (tile == k)).T.astype(f)) for k in range(4)], 1)
    q["pair"] = (i[:, None] // 2 == i[None, :] // 2).astype(f) / f(2)
    q["fold"] = (i[:, None] % C == i[None, :] % C).astype(f)
    q["group16"] = q["headmask"]
    q["fc1"] = both(v["L1_conv_fc1_w"].T)
    q["ln_g"] = rows(np.tile(v["L1_conv_ln_g"], 2))
    q["ln_b"] = rows(np.tile(v["L1_conv_ln_b"], 2))
    q["fc2"] = padded_rows(both(v["L1_conv_fc2_w"].T))
    q["x_weight"] = np.repeat(v["L1_conv_x_weight"], P)[:, None]
    q["w_x"] = by_half(v["L2_attn_W_x"].T)
    q["b_x"] = v["L2_attn_b_x"][:, None]
    q["w_slice"] = heads8(v["L2_attn_W_slice"].T)
    q["b_slice"] = np.tile(v["L2_attn_b_slice"], 8)[:, None]
    rowed = (i[:, None] // HD == np.arange(2 * HEADS)[None, :] % HEADS)
    mine = [rowed & (np.arange(2 * HEADS)[None, :] // HEADS == h) for h in range(2)]
    q["temp_rows"] = np.concatenate([np.where(r, np.tile(v["L2_attn_W_temp"].T, (HEADS, 1)), f(0)) for r in mine], 1)
    q["temp_spread"] = np.concatenate([padded_rows(r.T.astype(f)) for r in mine], 1)
    q["b_temp"] = np.repeat(v["L2_attn_b_temp"], P)[:, None]
    q["w_out"] = out_by_half(v["L2_attn_W_out"].T)
    q["b_out"] = twice(v["L2_attn_b_out"][:, None])
    lstm_b = np.zeros((3, P), f)
    for n, g in enumerate(("i", "c", "o")):
        q["u_" + "igo"[n]] = both(v[f"L2_ffn_U_{g}"])
        q["v_" + "igo"[n]] = both(v[f"L2_ffn_V_{g}"])
        lstm_b[n] = np.tile(v[f"L2_ffn_b_{g}"], 2)
    q["lstm_b"] = padded_rows(lstm_b)
    q["lstm_half"] = padded_rows(np.array([[0.5], [1.0], [0.5]], f))
    q["eps5"] = np.full((P, 1), 1e-5, f)
    q["gate_sel"] = padded_rows(np.tile(np.repeat(np.eye(3, dtype=f), HB, 1), (1, 8)))
    q["q_w"] = both(v["L3_attn_q_weight"])
    q["gate_w"] = both(v["L3_ffn_gate_w"])
    q["gate_b"] = rows(np.tile(v["L3_ffn_gate_b"], 2))
    q["idx_w"] = rows(np.tile(np.arange(E, 0, -1), 2).astype(f))
    arrays = {}
    for chunk, cols in LAYOUT.items():
        for name, n in cols.items():
            assert q[name].shape == (P, n), (name, q[name].shape)
        arrays[chunk] = np.concatenate([q[name] for name in cols], 1)
    w12 = np.stack([v["L3_ffn_w1"], v["L3_ffn_w2"]], 1).transpose(2, 0, 1, 3).reshape(C, 2 * E * HID)
    arrays["w12"] = twice(w12)
    arrays["w3"] = v["L3_ffn_w3"].transpose(1, 0, 2).reshape(HID, E * C)
    return {n: np.ascontiguousarray(a) for n, a in arrays.items()}


def heads8(w):
    o = np.zeros((P, P), w.dtype)
    for h in range(8):
        o[16 * h:16 * h + 16, 16 * h:16 * h + 16] = w
    return o


def kernel(**inputs):
    import concourse.bacc as bacc
    from concourse.bass_utils import run_bass_kernel_spmd

    v = {n: np.ascontiguousarray(a) for n, a in inputs.items()}
    nc = bacc.Bacc("TRN2", target_bir_lowering=False, num_devices=1)
    arrays = {"in_x": v["x"].reshape(B, C, HW)}
    arrays.update({f"in_{n}": a for n, a in lay_out(v).items()})
    aps = {n: nc.dram_tensor(n, a.shape, mybir.dt.from_np(a.dtype), kind="ExternalInput").ap()
           for n, a in arrays.items()}
    out = nc.dram_tensor("out", (B, C, HW), F32, kind="ExternalOutput").ap()
    build(nc, aps["in_x"], {n[3:]: a for n, a in aps.items() if n != "in_x"}, out)
    r = run_bass_kernel_spmd(nc, [arrays], core_ids=[0])
    return r.results[0]["out"].reshape(B, C, SIDE, SIDE)
```
